# Optimizing a Trainium2 kernel written in Bass

```python
import numpy as np
import jax
import jax.numpy as jnp

def _softmax(x, axis=-1):
    return jax.nn.softmax(x, axis=axis)

def _gelu(x):
    return jax.nn.gelu(x, approximate=True)

def _silu(x):
    return jax.nn.silu(x)

def _sigmoid(x):
    return jax.nn.sigmoid(x)

def _layernorm(x, axis=-1, eps=1e-05):
    m = jnp.mean(x, axis=axis, keepdims=True)
    v = jnp.var(x, axis=axis, keepdims=True)
    return (x - m) / jnp.sqrt(v + eps)

def _scatter_add(tgt, idx, src, axis=0):
    return tgt.at[idx].add(src)

def _segment_sum(src, seg, n):
    return jax.ops.segment_sum(src, seg, n)
kernel_name = 'mk_adaln_d1_jaxref_r4_52f4b9'

def setup_inputs(seed: int=0):
    np.random.seed(seed)
    _w = jnp.asarray

    def _L0_attn_setup():
        import jax, jax.numpy as jnp
        import numpy as np
        EPS = 1e-15
        HEAD_DIM = 32
        PAD_VAL = 1.0
        key = jax.random.key(seed)
        k1, k2, k3, k4 = jax.random.split(key, 4)
        B, N, C = (2, 1024, 512)
        s = 1.0 / np.sqrt(C).astype(np.float32)
        x = jax.random.normal(k1, (B, N, C), jnp.float32)
        w_qkv = jax.random.normal(k2, (3 * C, C), jnp.float32) * s
        w_proj = jax.random.normal(k3, (C, C), jnp.float32) * s
        b_proj = jax.random.normal(k4, (C,), jnp.float32) * 0.01
        return {'x': x, 'w_qkv': w_qkv, 'w_proj': w_proj, 'b_proj': b_proj}
    _L0_attn_in = _L0_attn_setup()

    def _L0_ffn_setup():
        import jax, jax.numpy as jnp
        import numpy as np
        TOP_K = 2
        key = jax.random.key(seed)
        ks = jax.random.split(key, 4)
        G, S, F, E, H = (4, 512, 512, 8, 512)
        return {'x': jax.random.normal(ks[0], (G, S, F), dtype=jnp.float32), 'router_logits': jax.random.normal(ks[1], (F, E), dtype=jnp.float32) * 0.02, 'gating_einsum': jax.random.normal(ks[2], (E, 2, H, F), dtype=jnp.float32) * 0.02, 'linear': jax.random.normal(ks[3], (E, H, F), dtype=jnp.float32) * 0.02, 'per_expert_scale': jnp.ones((E,), dtype=jnp.float32), 'router_scale': jnp.ones((F,), dtype=jnp.float32)}
    _L0_ffn_in = _L0_ffn_setup()
    _L0_c = _w((lambda *s: np.random.randn(*s).astype(np.float32) * 0.05)(2, 512))
    _L0_wmod = _w((lambda *s: np.random.randn(*s).astype(np.float32) * 0.05)(512, 6 * 512) * 512 ** (-0.5))
    _d = {'L0_attn_x': _L0_attn_in['x'], 'L0_attn_w_qkv': _L0_attn_in['w_qkv'], 'L0_attn_w_proj': _L0_attn_in['w_proj'], 'L0_attn_b_proj': _L0_attn_in['b_proj'], 'L0_ffn_router_logits': _L0_ffn_in['router_logits'], 'L0_ffn_gating_einsum': _L0_ffn_in['gating_einsum'], 'L0_ffn_linear': _L0_ffn_in['linear'], 'L0_ffn_per_expert_scale': _L0_ffn_in['per_expert_scale'], 'L0_ffn_router_scale': _L0_ffn_in['router_scale'], 'L0_c': _L0_c, 'L0_wmod': _L0_wmod}
    _x0 = _d['L0_attn_x']
    _d['L0_attn_x'] = jax.random.normal(jax.random.fold_in(jax.random.key(seed), 1), (2, 4096, 512), dtype=_x0.dtype)
    del _x0
    return _d

def reference(L0_attn_x, L0_attn_w_qkv, L0_attn_w_proj, L0_attn_b_proj, L0_ffn_router_logits, L0_ffn_gating_einsum, L0_ffn_linear, L0_ffn_per_expert_scale, L0_ffn_router_scale, L0_c, L0_wmod):

    def _L0_attn_ref(x, w_qkv, w_proj, b_proj):
        import jax, jax.numpy as jnp
        import numpy as np
        EPS = 1e-15
        HEAD_DIM = 32
        PAD_VAL = 1.0
        B, N, C = x.shape
        d = HEAD_DIM
        h = C // d
        qkv = (x @ w_qkv.T).reshape(B, N, 3, C)
        q, k, v = (qkv[:, :, 0], qkv[:, :, 1], qkv[:, :, 2])

        def to_heads(t):
            return t.reshape(B, N, h, d).transpose(0, 2, 3, 1)
        q = jax.nn.relu(to_heads(q))
        k = jax.nn.relu(to_heads(k))
        v = to_heads(v)
        v_pad = jnp.pad(v, ((0, 0), (0, 0), (0, 1), (0, 0)), constant_values=PAD_VAL)
        vk = jnp.einsum('bhen,bhdn->bhed', v_pad, k)
        out = jnp.einsum('bhed,bhdn->bhen', vk, q)
        out = out[:, :, :-1] / (out[:, :, -1:] + EPS)
        out = out.reshape(B, C, N).transpose(0, 2, 1)
        return out @ w_proj.T + b_proj

    def _L0_ffn_ref(x, router_logits, gating_einsum, linear, per_expert_scale, router_scale):
        import jax, jax.numpy as jnp
        import numpy as np
        TOP_K = 2
        G, S, F = x.shape
        E = router_logits.shape[-1]
        H = linear.shape[1]
        k = TOP_K
        dtype = x.dtype
        var = jnp.mean(jnp.square(x.astype(jnp.float32)), axis=-1, keepdims=True)
        router_input = x * jax.lax.rsqrt(var + 1e-06).astype(dtype)
        root_size = jax.lax.rsqrt(jnp.array(F, dtype=dtype))
        router_input = router_input * root_size * router_scale.astype(dtype)
        logits = jnp.einsum('gsd,de->gse', router_input, router_logits.astype(dtype))
        logits32 = logits.astype(jnp.float32)
        probs = jax.nn.softmax(logits32, axis=-1)
        _, choices = jax.lax.approx_max_k(logits32, k=k)
        indicator = jax.nn.one_hot(choices, E, dtype=probs.dtype).sum(axis=-2)
        renorm = jnp.sum(indicator * probs, axis=-1, keepdims=True)
        renorm = jnp.where(renorm > 0.0, renorm, 1.0)
        weights = probs / renorm
        x_flat = x.reshape((-1, F))
        batch_size = G * S
        choices_flat = choices.ravel()
        xs_order = choices_flat.argsort()
        xs_reverse_argsort = xs_order.argsort()
        xs_indices = jnp.repeat(jnp.arange(batch_size), k)[xs_order]
        sorted_xs = x_flat[xs_indices, :]
        choices_oh = jax.nn.one_hot(choices, num_classes=E, dtype=jnp.int32)
        tokens_per_expert = jnp.sum(choices_oh, axis=(0, 1, 2))
        combine_weights = (choices_oh.astype(jnp.float32) * jnp.expand_dims(weights, axis=2)).sum(axis=-1).astype(weights.dtype)
        w_gate = jnp.transpose(gating_einsum, (0, 3, 1, 2)).reshape(E, F, 2 * H)
        gate_out = jax.lax.ragged_dot(sorted_xs, w_gate.astype(dtype), group_sizes=tokens_per_expert)
        gate_out = gate_out.reshape(gate_out.shape[0], 2, H)
        activation = jax.nn.gelu(gate_out[:, 0, :]) * gate_out[:, 1, :]
        expert_outputs = jax.lax.ragged_dot(activation, linear.astype(dtype), group_sizes=tokens_per_expert)
        expert_indices = jnp.repeat(jnp.arange(E), tokens_per_expert, total_repeat_length=expert_outputs.shape[0])
        expert_outputs = expert_outputs * per_expert_scale.astype(expert_outputs.dtype)[expert_indices, None]
        out = expert_outputs[xs_reverse_argsort].reshape((G, S, k, -1))
        out = jnp.einsum('blkd,blk->bld', out, combine_weights, preferred_element_type=out.dtype)
        return out
    x = L0_attn_x
    mod = (_silu(L0_c) @ L0_wmod).reshape(L0_c.shape[0], 6, 1, -1)
    sa, ca, ga, sb, cb, gb = (mod[:, 0], mod[:, 1], mod[:, 2], mod[:, 3], mod[:, 4], mod[:, 5])
    ga = (2 * (ga >= 0) - 1) * jnp.maximum(jnp.abs(ga), 0.25)
    gb = (2 * (gb >= 0) - 1) * jnp.maximum(jnp.abs(gb), 0.25)
    h = _layernorm(x, axis=-1) * (1 + ca) + sa
    x = x + ga * _L0_attn_ref(h, L0_attn_w_qkv, L0_attn_w_proj, L0_attn_b_proj)
    h = _layernorm(x, axis=-1) * (1 + cb) + sb
    x = x + gb * _L0_ffn_ref(h, L0_ffn_router_logits, L0_ffn_gating_einsum, L0_ffn_linear, L0_ffn_per_expert_scale, L0_ffn_router_scale)
    return x

_drawn_inputs = setup_inputs


def setup_inputs(seed=0):
    import zlib

    import numpy as np

    out = dict(_drawn_inputs(seed))
    spreads = {'L0_ffn_per_expert_scale': (1.0, 0.6), 'L0_ffn_router_scale': (1.0, 0.6)}
    factors = {'L0_attn_w_qkv': 8.0,
     'L0_attn_w_proj': 7.993,
     'L0_attn_b_proj': 8.0,
     'L0_ffn_router_logits': 6.807,
     'L0_ffn_gating_einsum': 5.853,
     'L0_ffn_linear': 5.858,
     'L0_c': 4.628,
     'L0_wmod': 4.646}
    for name, (base, spread) in spreads.items():
        noise = np.random.default_rng([zlib.crc32(name.encode()), seed]).standard_normal(out[name].shape)
        drawn = base * np.exp(spread * noise) if base else spread * noise
        out[name] = jnp.asarray(drawn.astype(out[name].dtype))
    for name, factor in factors.items():
        out[name] = (out[name] * factor).astype(out[name].dtype)
    return out
```

```python
from contextlib import ExitStack

import numpy as np

import concourse.bass as bass
from concourse import mybir

F32 = mybir.dt.float32
F32R = mybir.dt.float32r
BF16 = mybir.dt.bfloat16
I32 = mybir.dt.int32
U32 = mybir.dt.uint32
ALU = mybir.AluOpType
ACT = mybir.ActivationFunctionType
AX = mybir.AxisListType

P = 128
B, S, C = 2, 4096, 512
E, H = 8, 512
HEAD = 32
NT = B * S
FC = C // P
GT = 512
TPG = GT // P
NG = NT // GT
GPB = NG // B
HG = C // P
LN_EPS = 1e-5
DEN_EPS = 1e-15
RMS_EPS = 1e-6
VW = 132
EW = FC * 2 * H + (H // P) * C
DOWN = FC * 2 * H
QW = 1536
QPE = EW // QW
CAP = NT + P
ROW = 528
W_AT, TOK_AT = C, C + E
META = 12
ITEMS = (2 * NT + E * (P - 1)) // P
RING = 4
SCAT = 16 * 2 * TPG

PASSES = ((0, 0), (0, 1), (1, 0))


def at_least(eng, sem, value):
    if isinstance(value, int) and value <= 0:
        return
    eng.wait_ge(sem, value)


class Steps:

    def __init__(self, eng, sem, each):
        self.eng, self.sem, self.each = eng, sem, each

    def begin(self, turn):
        self.base, self.n = turn * self.each, 0

    def did(self, ins):
        self.n += 1
        ins.then_inc(self.sem, 1)

    def settle(self, wait=at_least):
        wait(self.eng, self.sem, self.base + self.n)

    def end(self):
        assert self.n == self.each, (self.n, self.each)


def build(nc, x, c_t, wmod, wqkv, wproj, b_proj, r_w, r_scale, pes, moe_w, out):
    qd = nc.dram_tensor("q_split", (NG * 2 * P, FC * GT), F32, kind="Internal").ap()
    wd = nc.dram_tensor("expert_split", (E * QPE * P, 2 * QW), F32, kind="Internal").ap()
    mod_d = nc.dram_tensor("mod_rows", (B, 6 * C), F32, kind="Internal").ap()
    xs = nc.dram_tensor("expert_rows", (E * CAP + P, ROW), F32, kind="Internal").ap()

    keep, ph1, ph2, ph3 = ExitStack(), ExitStack(), ExitStack(), ExitStack()

    def sb(stack, name, shape, dt, side=None):
        return stack.enter_context(nc.sbuf_tensor(name, shape, dt, side=side) if side else nc.sbuf_tensor(name, shape, dt))

    def sem(name):
        return keep.enter_context(nc.semaphore(name))

    bank = [keep.enter_context(nc.psum_tensor(f"bank{i}", [P, 512], F32)) for i in range(8)]

    ident = sb(keep, "ident", [P, P], F32)
    before = sb(keep, "before", [P, P], BF16)
    ones = sb(keep, "ones", [P, P], BF16)
    headmask = sb(keep, "headmask", [P, P], F32)
    iota_e = sb(keep, "iota_e", [P, E], F32)
    list_at = sb(keep, "list_at", [P, E], F32)
    lane = sb(keep, "lane", [P, 1], F32)
    item_no = sb(keep, "item_no", [P, ITEMS], F32)
    modcol = sb(keep, "modcol", [P, 2 * FC * B], F32)
    modbc = sb(keep, "modbc", [P, B, 4, C], F32)
    bproj = sb(keep, "bproj", [P, C], F32)
    wp = [sb(keep, f"wp_{k}", [P, B, FC, C], F32R) for k in ("hi", "lo")]
    kv = sb(keep, "kv", [P, B, HG, VW], F32)
    rw = sb(keep, "rw", [P, FC, E], F32)
    rscale = sb(keep, "rscale", [P, FC], F32)
    pes_bc = sb(keep, "pes_bc", [P, E], F32)
    next_row = sb(keep, "next_row", [P, E], F32)
    tok_no = sb(keep, "tok_no", [P, TPG], F32)
    tables = sb(keep, "tables", [P, 2, ITEMS], I32)

    wq = [sb(ph1, f"wq_{k}", [P, FC, 3 * C], F32R) for k in ("hi", "lo")]
    raw = sb(ph1, "raw", [P, 2, QW], F32)
    sp_hl = [sb(ph1, f"split_{k}", [P, QW], F32R) for k in ("hi", "lo")]
    xg = sb(ph1, "xg", [P, TPG, C], F32)
    hf = [sb(ph1, f"hf{i}", [P, FC, P], F32) for i in range(2)]
    h_t = [sb(ph1, f"h_t_{k}", [P, FC, GT], F32R) for k in ("hi", "lo")]
    k_sb = [sb(ph1, f"k_sb{i}", [P, C], F32) for i in range(2)]
    v_sb = [sb(ph1, f"v_sb{i}", [P, HG, VW], F32) for i in range(2)]
    qf = sb(ph1, "qf", [P, FC, GT], F32)
    q_hl = [sb(ph1, f"q_{k}", [P, FC, GT], F32R) for k in ("hi", "lo")]
    mod_odd = sb(ph1, "mod_odd", [P, FC, C], F32)
    mod_stage = [qf, mod_odd]
    modbc_flat = modbc[:, :, :, :].rearrange("p b m n -> p (b m n)")
    mod_row = modbc_flat[0:B, 0:6 * C].rearrange("b (m n) -> b m n", m=6)
    mod_tmp = modbc_flat[0:B, 6 * C:7 * C]
    wproj_f = sb(ph1, "wproj_f", [P, FC, C], F32)
    c_sb = sb(ph1, "c_sb", [P, FC * B], F32)
    c_exp = sb(ph1, "c_exp", [P, FC * B], F32)
    silu_c = sb(ph1, "silu_c", [P, FC * B], F32)
    st = sb(ph1, "st", [P, TPG, 6], F32)
    mv = sb(ph1, "mv", [P, TPG, 2], F32)
    ve = sb(ph1, "ve", [P, TPG], F32)
    lnv = sb(ph1, "lnv", [P, TPG], F32)
    y0 = sb(ph1, "y0", [P, TPG], F32)
    nt1 = sb(ph1, "nt1", [P, TPG], F32)
    nt2 = sb(ph1, "nt2", [P, TPG], F32)
    ph1.close()

    q2 = [sb(ph2, f"q2_{k}", [P, FC, GT], F32R) for k in ("hi", "lo")]
    nd = [sb(ph2, f"nd_{k}", [P, B, HG, 2, P], F32R) for k in ("hi", "lo")]
    ndf = sb(ph2, "ndf", [P, HG, 2, P], F32)
    den_sb = [sb(ph2, f"den_sb{i}", [P, GT], F32) for i in range(2)]
    onf = [sb(ph2, f"onf{i}", [P, GT], F32) for i in range(2)]
    on = [sb(ph2, f"on_{k}", [P, FC, GT], F32R) for k in ("hi", "lo")]
    xb = sb(ph2, "xb", [P, TPG, C], F32)
    x1 = sb(ph2, "x1", [P, TPG, C], F32)
    lnt = sb(ph2, "lnt", [P, C], F32)
    rows = [sb(ph2, f"rows{i}", [P, TPG, ROW], F32) for i in range(2)]
    h2t = sb(ph2, "h2t", [P, TPG, C], F32)
    sq_out = sb(ph2, "sq_out", [P, C], F32)
    ss = sb(ph2, "ss", [P, TPG], F32)
    st2 = sb(ph2, "st2", [P, TPG, 6], F32)
    mv2 = sb(ph2, "mv2", [P, TPG, 2], F32)
    ve2, ln2, y2, na2, nb2, rstd2 = (sb(ph2, f"ln2_{i}", [P, TPG], F32) for i in range(6))
    ve3, ln3, y3, na3, nb3, rs3 = (sb(ph2, f"rms_{i}", [P, TPG], F32) for i in range(6))
    lg, mx, oh0, oh1, mk, dl, ex, pr, ip, wts, pos = (sb(ph2, f"route_{i}", [P, TPG, E], F32) for i in range(11))
    chosen = sb(ph2, "chosen", [P, 2, TPG, E], F32)
    destf = sb(ph2, "destf", [P, 2, TPG], F32)
    ix = sb(ph2, "ix", [P, TPG, E], U32)
    ixf = sb(ph2, "ixf", [P, TPG, 2], F32)
    mkb = sb(ph2, "mkb", [P, TPG, E], BF16)
    se, rse, rn, rng, rrn = (sb(ph2, f"sum_{i}", [P, TPG], F32) for i in range(5))
    dest = [sb(ph2, f"dest{i}", [P, 2, TPG], U32) for i in range(2)]
    padrow = sb(ph2, "padrow", [P, ROW], F32)
    pad_to = sb(ph2, "pad_to", [P, E + 1], U32)
    cnt, ntl, cend, dlt = (sb(ph2, f"cnt_{i}", [P, E], F32) for i in range(4))
    cnti = sb(ph2, "cnti", [P, E], I32)
    ntli = sb(ph2, "ntli", [P, E], I32)
    it_e, it_r, it_t = (sb(ph2, f"it_{i}", [P, ITEMS], F32) for i in range(3))
    ph2.close()

    wbuf = sb(ph3, "wbuf", [P, 2 * 2 * EW], F32R)
    xrow = sb(ph3, "xrow", [P, ROW], F32)
    x_t = [sb(ph3, f"x_t_{k}", [P, C], F32R) for k in ("hi", "lo")]
    act_t = [sb(ph3, f"act_t_{k}", [P, H], F32R) for k in ("hi", "lo")]
    gact = sb(ph3, "gact", [P, H], F32)
    hact = sb(ph3, "hact", [P, H], F32)
    meta = sb(ph3, "meta", [P, RING * META], F32)
    cur_w = sb(ph3, "cur_w", [P, 1], F32)
    cur_tok = sb(ph3, "cur_tok", [P, 1], U32)
    in_b1 = sb(ph3, "in_b1", [P, 1], F32)
    in_b0 = sb(ph3, "in_b0", [P, 1], F32)
    gb0 = sb(ph3, "gb0", [P, C], F32)
    gbr = sb(ph3, "gbr", [P, C], F32)
    orow = sb(ph3, "orow", [P, C], F32)

    def f32(ap):
        return ap.bitcast(F32)

    T_B, Q_B, K_B, V_B, KV_B = bank[0:2], bank[2:4], bank[4], bank[5], bank[6:8]
    Y_B, D_B, N_B, R_B = bank[0:2], bank[2:4], bank[4:6], bank[6]
    XT_B, HT_B, G_B, U_B, O_B = bank[0], bank[1], bank[2], bank[3], bank[4]

    s_c, s_x, s_const = sem("c_loaded"), sem("x_loaded"), sem("const_loaded")
    s_raw, s_mod = [sem("raw_even"), sem("raw_odd")], [sem("wmod_even"), sem("wmod_odd")]
    s_modst, s_modbc = sem("mod_stored"), sem("modbc_loaded")
    s_qst, s_wst, s_zst = sem("q_stored"), sem("split_stored"), sem("zero_stored")
    s_passed = sem("waits_passed")
    s_id, s_vset, s_cexp, s_silu, s_modpe, s_modrow, s_colpe, s_col = (
        sem("ident_ready"), sem("vector_setup"), sem("c_exp_ready"), sem("silu_ready"), sem("mod_product"),
        sem("mod_row_ready"), sem("mod_col_turned"), sem("mod_col_ready"))
    s_wga = sem("proj_split")
    s_hi, s_lo = sem("split_hi"), sem("split_lo")
    s_var, s_seed, s_z, s_ln = sem("var_ready"), sem("rstd_seed"), sem("z_ready"), sem("ln1_step")
    s_T, s_hf, s_hhi, s_hlo = sem("z_turned"), sem("h_ready"), sem("h_hi_ready"), sem("h_lo_ready")
    s_q, s_qe, s_qhi, s_qlo = sem("q_done"), sem("q_taken"), sem("q_hi_ready"), sem("q_lo_ready")
    s_k, s_v, s_ke, s_ve, s_vk, s_kv = sem("k_done"), sem("v_done"), sem("k_taken"), sem("v_taken"), sem("kv_done"), sem("kv_added")
    s_aln = sem("scalar_ln_step")
    s_nd, s_ndstep, s_q2, s_x2, s_x1st = sem("nd_ready"), sem("nd_step"), sem("q_back"), sem("x_back"), sem("x1_stored")
    s_den, s_num, s_dene, s_on, s_rec = sem("den_done"), sem("num_done"), sem("den_taken"), sem("on_ready"), sem("recip_step")
    s_onhi, s_onlo, s_y, s_xb, s_x1 = sem("on_hi_ready"), sem("on_lo_ready"), sem("proj_done"), sem("xb_ready"), sem("x1_ready")
    s_ln2, s_var2, s_seed2, s_aln2 = sem("ln2_step"), sem("var2_ready"), sem("rstd2_seed"), sem("scalar_ln2_step")
    s_h2, s_sq, s_h2t, s_h2te, s_lg = sem("h2_ready"), sem("sq_ready"), sem("h2_turned"), sem("h2t_ready"), sem("logits_done")
    s_var3, s_seed3, s_aln3, s_ex, s_dl = sem("rms_ready"), sem("rms_seed"), sem("scalar_rms_step"), sem("exp_ready"), sem("logits_less_max")
    s_r1, s_r2, s_mk, s_rank, s_ranku = sem("route_step"), sem("place_step"), sem("mask_ready"), sem("rank_done"), sem("rank_taken")
    s_rowm, s_free, s_dest, s_scat = sem("row_numbers"), sem("rows_free"), sem("dest_ready"), sem("rows_scattered")
    s_it, s_pad, s_padi = sem("item_step"), sem("pads_scattered"), sem("pad_rows_ready")
    s_w, s_xr, s_xt, s_xthi, s_xtlo, s_meta = sem("weights_loaded"), sem("rows_loaded"), sem("x_turned"), sem("x_hi_ready"), sem("x_lo_ready"), sem("meta_kept")
    s_g, s_u, s_ga, s_h, s_ht, s_hthi, s_htlo = sem("gate_done"), sem("up_done"), sem("gelu_ready"), sem("act_ready"), sem("act_turned"), sem("act_hi_ready"), sem("act_lo_ready")
    s_o, s_cur, s_gb0, s_gbr, s_or, s_add = sem("down_done"), sem("cur_ready"), sem("gb0_ready"), sem("gb_rows_step"), sem("out_rows_ready"), sem("rows_added")

    def wait_apart(eng, sem, value):
        at_least(eng, sem, value)
        if not isinstance(value, int):
            eng.sem_inc(s_passed, 1)

    def group_rows(t, g):
        return t[bass.ds(g * GT, GT), :].rearrange("(t p) c -> p t c", p=P)

    def batch_of(g):
        return g // GPB if isinstance(g, int) else (g >> 3) & 1

    assert GPB == 8

    def phase1_over(eng):
        eng.wait_ge(s_kv, 2 * NG)
        eng.wait_ge(s_qst, 32 * NG)
        eng.wait_ge(s_wst, 32 * E * QPE)
        eng.wait_ge(s_wga, 8)

    def phase2_over(eng):
        eng.wait_ge(s_pad, 16 * (E + 1))
        eng.wait_ge(s_x1st, 16 * NG)
        eng.wait_ge(s_zst, 16)
        eng.wait_ge(s_it, ITEM_STEPS)

    ITEM_STEPS = 42

    block = keep.enter_context(nc.Block())

    @block.sync
    def _(sp):
        sp.dma_start(c_sb[:, :], c_t).then_inc(s_c, 16)
        sp.dma_start(xg[:, :, :], group_rows(x, 0)).then_inc(s_x, 16)

        def load_wmod(m):
            at_least(sp, s_modpe, m - 1)
            sp.dma_start(mod_stage[m % 2][:, :, :], wmod[:, m * C:(m + 1) * C].rearrange("(f p) n -> p f n", p=P)).then_inc(s_mod[m % 2], 16)

        def load_raw(turn, half, src):
            at_least(sp, s_lo, 2 * turn + half - 1)
            sp.dma_start(raw[:, half, :], src).then_inc(s_raw[half], 16)

        load_wmod(0)
        load_wmod(1)
        for f in range(2):
            load_raw(f // 2, f % 2, wqkv[:, f * QW:(f + 1) * QW])
        for f in range(2, FC):
            load_raw(f // 2, f % 2, wqkv[:, f * QW:(f + 1) * QW])
        for m in range(2, 6):
            load_wmod(m)
        sp.dma_start(wproj_f[:, :, :], wproj.rearrange("p (f n) -> p f n", f=FC)).then_inc(s_const, 16)
        sp.dma_start(bproj[:, :], b_proj.partition_broadcast(P)).then_inc(s_const, 16)
        sp.dma_start(rw[:, :, :], r_w.rearrange("p (f e) -> p f e", f=FC)).then_inc(s_const, 16)
        sp.dma_start(rscale[:, :], r_scale).then_inc(s_const, 16)
        sp.dma_start(pes_bc[:, :], pes.partition_broadcast(P)).then_inc(s_const, 16)

        def load_expert_raw(g, s):
            load_raw(FC // 2 + g, s, moe_w[bass.ds((2 * g + s) * P, P), :])

        def store_expert(g, s):
            sp.wait_ge(s_lo, FC + 2 * g + s + 1)
            for k in range(2):
                sp.dma_start(wd[bass.ds((2 * g + s) * P, P), k * QW:(k + 1) * QW], f32(sp_hl[k][:, :])).then_inc(s_wst, 16)

        for s in range(2):
            load_expert_raw(0, s)

        def group1(g, last=False):
            if not last:
                sp.wait_ge(s_T, TPG * (g + 1))
                sp.dma_start(xg[:, :, :], group_rows(x, g + 1)).then_inc(s_x, 16)
            store_expert(g, 0)
            if not last:
                load_expert_raw(g + 1, 0)
            sp.wait_ge(s_qlo, g + 1)
            for k in range(2):
                sp.dma_start(qd[bass.ds((2 * g + k) * P, P), :], f32(q_hl[k][:, :, :]).rearrange("p f t -> p (f t)")).then_inc(s_qst, 16)
            store_expert(g, 1)
            if not last:
                load_expert_raw(g + 1, 1)

        group1(0)
        with sp.Fori(1, NG - 1) as g:
            group1(g)
        group1(NG - 1, last=True)

        phase1_over(sp)

        def load_q(g):
            for k in range(2):
                sp.dma_start(f32(q2[k][:, :, :]).rearrange("p f t -> p (f t)"), qd[bass.ds((2 * g + k) * P, P), :]).then_inc(s_q2, 16)

        def load_x(g):
            sp.dma_start(xb[:, :, :], group_rows(x, g)).then_inc(s_x2, 16)

        load_q(0)
        load_x(0)
        sp.wait_ge(s_padi, 1)
        sp.dma_start(out[NT:NT + P, :], padrow[:, 0:C]).then_inc(s_zst, 16)

        def group2(g, last=False):
            if not last:
                sp.wait_ge(s_num, HG * (g + 1))
                load_q(g + 1)
            sp.wait_ge(s_x1, TPG * (g + 1))
            sp.dma_start(group_rows(out, g), x1[:, :, :]).then_inc(s_x1st, 16)
            if not last:
                load_x(g + 1)

        group2(0)
        with sp.Fori(1, NG - 1) as g:
            group2(g)
        group2(NG - 1, last=True)

        phase2_over(sp)

        def load_weights(e, half):
            for q in range(QPE):
                sp.dma_start(f32(wbuf[:, bass.ds(half * 2 * EW + q * 2 * QW, 2 * QW)]),
                             wd[bass.ds((e * QPE + q) * P, P), :]).then_inc(s_w, 16)

        def load_rows(i):
            r = sp.value_load(tables[0:1, 0, bass.ds(i, 1)], min_val=0, max_val=E * CAP)
            sp.dma_start(xrow[:, :], xs[bass.ds(r, P), :]).then_inc(s_xr, 16)

        def next_weights(i):
            e = sp.value_load(tables[0:1, 1, bass.ds(i, 1)], min_val=0, max_val=E - 1)
            e_before = sp.value_load(tables[0:1, 1, bass.ds(i - 1, 1)], min_val=0, max_val=E - 1)
            with sp.If(e > e_before):
                with sp.If(e < E - 1):
                    wait_apart(sp, s_w, 16 * QPE * (e + 1))
                    wait_apart(sp, s_o, i)
                    nxt = sp.value_load(tables[0:1, 1, bass.ds(i, 1)], min_val=0, max_val=E - 2) + 1
                    load_weights(nxt, nxt & 1)

        def item(i):
            sp.wait_ge(s_xt, i)
            wait_apart(sp, s_meta, i)
            load_rows(i)

        load_rows(0)
        for e in range(2):
            at_least(sp, s_w, 16 * QPE * e)
            load_weights(e, e)
        item(1)
        item(2)
        with sp.Fori(3, ITEMS) as i:
            next_weights(i - 2)
            item(i)
        next_weights(ITEMS - 2)
        sp.wait_ge(s_add, 16 * ITEMS)

    @block.gpsimd
    def _(pool):
        pool.memset(ident[:, :], 0.0).then_inc(s_id, 1)
        pool.memset(before[:, :], 1.0).then_inc(s_id, 1)
        pool.memset(ones[:, :], 1.0).then_inc(s_id, 1)
        pool.memset(headmask[:, :], 1.0).then_inc(s_id, 1)
        pool.wait_ge(s_id, 4)
        pool.affine_select(out=ident[:, :], in_=ident[:, :], compare_op=ALU.not_equal, fill=1.0, base=0,
                           pattern=[[-1, P]], channel_multiplier=1).then_inc(s_id, 1)
        pool.affine_select(out=before[:, :], in_=before[:, :], compare_op=ALU.is_gt, fill=0.0, base=0,
                           pattern=[[1, P]], channel_multiplier=-1).then_inc(s_id, 1)
        blocks = headmask[:, :].rearrange("p (a n) -> p a n", n=HEAD)
        pool.affine_select(out=blocks, in_=blocks, compare_op=ALU.is_ge, fill=0.0, base=0,
                           pattern=[[-HEAD, P // HEAD], [0, HEAD]], channel_multiplier=1).then_inc(s_id, 1)
        pool.wait_ge(s_id, 7)
        pool.affine_select(out=blocks, in_=blocks, compare_op=ALU.is_ge, fill=0.0, base=HEAD - 1,
                           pattern=[[HEAD, P // HEAD], [0, HEAD]], channel_multiplier=-1).then_inc(s_id, 1)
        pool.iota(iota_e[:, :], [[1, E]], base=0, channel_multiplier=0, allow_small_or_imprecise_dtypes=True).then_inc(s_id, 1)
        pool.iota(lane[:, :], [[1, 1]], base=0, channel_multiplier=1, allow_small_or_imprecise_dtypes=True).then_inc(s_id, 1)
        pool.iota(list_at[:, :], [[CAP, E]], base=0, channel_multiplier=0, allow_small_or_imprecise_dtypes=True).then_inc(s_id, 1)
        pool.iota(next_row[:, :], [[CAP, E]], base=0, channel_multiplier=0, allow_small_or_imprecise_dtypes=True).then_inc(s_id, 1)
        pool.iota(item_no[:, :], [[1, ITEMS]], base=0, channel_multiplier=0, allow_small_or_imprecise_dtypes=True).then_inc(s_id, 1)
        pool.iota(tok_no[:, :], [[P, TPG]], base=0, channel_multiplier=1, allow_small_or_imprecise_dtypes=True).then_inc(s_id, 1)

        def group1(g):
            pool.wait_ge(s_qhi, g + 1)
            at_least(pool, s_qst, 32 * g)
            pool.tensor_tensor(q_hl[1][:, :, :], qf[:, :, :], f32(q_hl[0][:, :, :]), ALU.subtract).then_inc(s_qlo, 1)

        group1(0)
        pool.wait_ge(s_modbc, 16 * B)
        pool.wait_ge(s_const, 16 * 5)
        for b in range(B):
            at_least(pool, s_wga, 4 * b)
            for f in range(FC):
                last = pool.tensor_tensor(mod_odd[:, f, :], wproj_f[:, f, :], modbc[:, b, 0, :], ALU.mult)
            last.then_inc(s_wga, 1)
            pool.wait_ge(s_wga, 4 * b + 1)
            pool.tensor_copy(wp[0][:, b, :, :], mod_odd[:, :, :]).then_inc(s_wga, 1)
            pool.wait_ge(s_wga, 4 * b + 2)
            pool.tensor_tensor(wp[1][:, b, :, :], mod_odd[:, :, :], f32(wp[0][:, b, :, :]), ALU.subtract).then_inc(s_wga, 1)
            pool.tensor_tensor(modbc[:, b, 0, :], modbc[:, b, 0, :], bproj[:, :], ALU.mult).then_inc(s_wga, 1)
        with pool.Fori(1, NG) as g:
            group1(g)

        phase1_over(pool)
        pool.memset(rows[0][:, :, C:], 0.0).then_inc(s_free, 1)
        pool.memset(rows[1][:, :, C:], 0.0)
        pool.memset(padrow[:, :], 0.0).then_inc(s_padi, 1)
        pool.wait_ge(s_padi, 1)
        pool.tensor_scalar(padrow[:, TOK_AT:TOK_AT + 1].bitcast(I32), lane[:, :], float(NT), None, ALU.add).then_inc(s_padi, 1)

        def add_bias(g):
            pool.wait_ge(s_x2, 16 * (g + 1))
            for t in range(TPG):
                pool.tensor_tensor(xb[:, t, :], xb[:, t, :], modbc[:, batch_of(g), 0, :] if isinstance(g, int) else
                                   modbc[:, bass.ds(batch_of(g), 1), 0, :].rearrange("p a n -> p (a n)"), ALU.add).then_inc(s_xb, 1)

        def low_on(g):
            for j in range(HG):
                pool.wait_ge(s_onhi, HG * g + j + 1)
                pool.tensor_tensor(on[1][:, j, :], onf[j % 2][:, :], f32(on[0][:, j, :]), ALU.subtract).then_inc(s_onlo, 1)

        def number_rows(g, par):
            if not isinstance(g, int) or g:
                wait_apart(pool, s_rowm, 2 * g)
            pool.tensor_copy(rows[par][:, :, TOK_AT].bitcast(I32), tok_no[:, :]).then_inc(s_rowm, 1)
            wait_apart(pool, s_rowm, 2 * g + 1)
            pool.tensor_scalar(tok_no[:, :], tok_no[:, :], float(GT), None, ALU.add).then_inc(s_rowm, 1)

        def scatter(g, par):
            pool.wait_ge(s_scat, SCAT * g)
            pool.sem_inc(s_free, 1)
            pool.wait_ge(s_dest, g + 1)
            wait_apart(pool, s_rowm, 2 * g + 1)
            for t in range(TPG):
                for k in range(2):
                    pool.indirect_dma_start(out=xs, out_offset=bass.IndirectOffsetOnAxis(dest[par][:, k, t:t + 1], 0),
                                            in_=rows[par][:, t, :], in_offset=None).then_inc(s_scat, 16)

        def group2(g, par, last=False, first=False):
            if not first:
                scatter(g - 1, 1 - par)
            number_rows(g, par)
            if not last:
                low_on(g + 1)
                add_bias(g + 1)

        low_on(0)
        add_bias(0)
        group2(0, 0, first=True)
        group2(1, 1)
        group2(2, 0)
        with pool.Fori(1, (NG - 2) // 2) as j:
            group2(2 * j + 1, 1)
            group2(2 * j + 2, 0)
        group2(NG - 1, 1, last=True)
        scatter(NG - 1, 1)
        pool.wait_ge(s_padi, 3)
        pool.wait_ge(s_scat, SCAT * NG)
        for e in range(E + 1):
            pool.indirect_dma_start(out=xs, out_offset=bass.IndirectOffsetOnAxis(pad_to[:, e:e + 1], 0),
                                    in_=padrow[:, :], in_offset=None).then_inc(s_pad, 16)

        phase2_over(pool)

        def item(i):
            pool.wait_ge(s_or, i + 1)
            wait_apart(pool, s_add, 16 * i)
            pool.indirect_dma_start(out=out, out_offset=bass.IndirectOffsetOnAxis(cur_tok[:, 0:1], 0), in_=orow[:, :],
                                    in_offset=None, compute_op=ALU.add).then_inc(s_add, 16)

        item(0)
        with pool.Fori(1, ITEMS) as i:
            item(i)
        pool.wait_ge(s_add, 16 * ITEMS)

    @block.scalar
    def _(act):
        act.preload_act_table_set("natural_log_exp_and_others")
        act.wait_ge(s_c, 16)
        act.activation(c_exp[:, :], c_sb[:, :], ACT.Exp, scale=-1.0).then_inc(s_cexp, 1)

        def split_hi(turn, half, dst, settled=None):
            act.wait_ge(s_raw[half], 16 * (turn + 1))
            if settled is not None:
                at_least(act, s_wst, settled)
            act.activation(dst, raw[:, half, :], ACT.Copy).then_inc(s_hi, 1)

        aln = Steps(act, s_aln, 1)

        def seed1(g):
            aln.begin(g)
            act.wait_ge(s_var, g + 1)
            aln.did(act.activation(lnv[:, :], ve[:, :], ACT.Ln))
            aln.settle()
            act.activation(y0[:, :], lnv[:, :], ACT.Exp, scale=-0.5).then_inc(s_seed, 1)
            aln.end()

        def hi1(g, t):
            act.wait_ge(s_hf, TPG * g + t + 1)
            act.activation(h_t[0][:, :, t * P:(t + 1) * P], hf[t % 2][:, :, :], ACT.Copy).then_inc(s_hhi, 1)

        seed1(0)
        for f in range(FC):
            split_hi(f // 2, f % 2, wq[0][:, f, :])
            hi1(0, f)
        act.wait_ge(s_modrow, 6)
        act.dma_start(mod_d.rearrange("b (m n) -> b m n", m=6), mod_row[:, :, :]).then_inc(s_modst, 16)
        act.wait_ge(s_modst, 16)
        act.wait_ge(s_col, 1)
        for b in range(B):
            act.dma_start(modbc[:, b, :, :].rearrange("p m n -> p (m n)"), mod_d[b, 2 * C:6 * C].partition_broadcast(P)).then_inc(s_modbc, 16)

        def group1(g, last=False):
            if not last:
                seed1(g + 1)
            for j in range(FC):
                act.wait_ge(s_q, FC * g + j + 1)
                if j == 0:
                    at_least(act, s_qlo, g)
                act.activation(qf[:, j, :], Q_B[j % 2][:, :], ACT.Relu).then_inc(s_qe, 1)
            at_least(act, s_qst, 32 * g)
            act.wait_ge(s_qe, FC * (g + 1))
            act.activation(q_hl[0][:, :, :], qf[:, :, :], ACT.Copy).then_inc(s_qhi, 1)
            split_hi(FC // 2 + g, 0, sp_hl[0][:, :], 32 * 2 * g)
            for t in range(TPG):
                act.wait_ge(s_k, TPG * g + t + 1)
                at_least(act, s_vk, TPG * g + t - 1)
                act.activation(k_sb[t % 2][:, :], K_B[:, :], ACT.Relu).then_inc(s_ke, 1)
                if not last:
                    hi1(g + 1, t)
                if t == 1:
                    split_hi(FC // 2 + g, 1, sp_hl[0][:, :], 32 * (2 * g + 1))

        group1(0)
        with act.Fori(1, NG - 1) as g:
            group1(g)
        group1(NG - 1, last=True)

        phase1_over(act)
        aln2, aln3 = Steps(act, s_aln2, 1), Steps(act, s_aln3, 1)

        def den(g, j):
            act.wait_ge(s_den, HG * g + j + 1)
            at_least(act, s_on, HG * g + j - 1)
            act.activation(den_sb[j % 2][:, :], D_B[j % 2][:, :], ACT.Copy, bias=DEN_EPS).then_inc(s_dene, 1)

        def on_hi(g, j):
            act.wait_ge(s_on, HG * g + j + 1)
            at_least(act, s_y, TPG * g)
            act.activation(on[0][:, j, :], onf[j % 2][:, :], ACT.Copy).then_inc(s_onhi, 1)

        def seed2(g, half):
            h = slice(2 * half, 2 * half + 2)
            aln2.begin(2 * g + half)
            act.wait_ge(s_var2, 2 * g + half + 1)
            aln2.did(act.activation(ln2[:, h], ve2[:, h], ACT.Ln))
            aln2.settle()
            act.activation(y2[:, h], ln2[:, h], ACT.Exp, scale=-0.5).then_inc(s_seed2, 1)
            aln2.end()

        def square(g, t, par):
            act.wait_ge(s_h2, TPG * g + t + 1)
            at_least(act, s_sq, TPG * g + t)
            if t == 0:
                at_least(act, s_var3, g)
            act.activation(sq_out[:, :], rows[par][:, t, 0:C], ACT.Square, accum_out=ss[:, t:t + 1]).then_inc(s_sq, 1)

        def group2(g, par, last=False):
            seed2(g, 0)
            square(g, 0, par)
            square(g, 1, par)
            seed2(g, 1)
            if last:
                square(g, 2, par)
                square(g, 3, par)
            else:
                den(g + 1, 0)
                den(g + 1, 1)
                on_hi(g + 1, 0)
                square(g, 2, par)
                on_hi(g + 1, 1)
                den(g + 1, 2)
                square(g, 3, par)
                den(g + 1, 3)
                on_hi(g + 1, 2)
                on_hi(g + 1, 3)
            for t in range(TPG):
                act.wait_ge(s_h2t, TPG * g + t + 1)
                at_least(act, s_lg, TPG * g)
                act.activation(h2t[:, t, :], Y_B[t % 2][:, :], ACT.Copy).then_inc(s_h2te, 1)
            aln3.begin(g)
            act.wait_ge(s_var3, g + 1)
            aln3.did(act.activation(ln3[:, :], ve3[:, :], ACT.Ln))
            aln3.settle()
            act.activation(y3[:, :], ln3[:, :], ACT.Exp, scale=-0.5).then_inc(s_seed3, 1)
            aln3.end()
            act.wait_ge(s_dl, g + 1)
            act.activation(ex[:, :, :], dl[:, :, :], ACT.Exp).then_inc(s_ex, 1)

        den(0, 0)
        den(0, 1)
        on_hi(0, 0)
        on_hi(0, 1)
        den(0, 2)
        den(0, 3)
        on_hi(0, 2)
        on_hi(0, 3)
        group2(0, 0)
        with act.Fori(0, (NG - 2) // 2) as j:
            group2(2 * j + 1, 1)
            group2(2 * j + 2, 0)
        group2(NG - 1, 1, last=True)

        phase2_over(act)
        act.preload_act_table(ACT.Gelu_apprx_tanh)

        def x_hi(i):
            act.wait_ge(s_xt, i + 1)
            at_least(act, s_u, i)
            act.activation(x_t[0][:, :], XT_B[:, :], ACT.Copy).then_inc(s_xthi, 1)

        def gelu(i):
            act.wait_ge(s_g, i + 1)
            at_least(act, s_h, i)
            act.activation(gact[:, :], G_B[:, :], ACT.Gelu_apprx_tanh).then_inc(s_ga, 1)

        def act_hi(i):
            act.wait_ge(s_ht, i + 1)
            at_least(act, s_o, i)
            act.activation(act_t[0][:, :], HT_B[:, :], ACT.Copy).then_inc(s_hthi, 1)

        def gb_rows(i):
            act.wait_ge(s_cur, 2 * (i + 1))
            act.activation(gb0[:, :], modbc[:, 0, 3, :], ACT.Copy, scale=in_b0[:, 0:1]).then_inc(s_gb0, 1)

        x_hi(0)
        gelu(0)
        x_hi(1)

        def item(i, last=False):
            gelu(i)
            act_hi(i - 1)
            if not last:
                x_hi(i + 1)
            gb_rows(i - 1)

        item(1)
        with act.Fori(2, ITEMS - 1) as i:
            item(i)
        item(ITEMS - 1, last=True)
        act_hi(ITEMS - 1)
        gb_rows(ITEMS - 1)

    @block.vector
    def _(dve):
        tt, ts, stt = dve.tensor_tensor, dve.tensor_scalar, dve.scalar_tensor_tensor

        dve.memset(kv[:, :, :, :], 0.0).then_inc(s_kv, NG)
        for i in range(2):
            dve.memset(v_sb[i][:, :, P:], 1.0).then_inc(s_vset, 1)
        setup = Steps(dve, s_vset, 0)
        setup.begin(0)
        setup.n = 2
        dve.wait_ge(s_c, 16)
        dve.wait_ge(s_cexp, 1)
        setup.did(ts(c_exp[:, :], c_exp[:, :], 1.0, None, ALU.add))
        setup.settle()
        setup.did(dve.reciprocal(c_exp[:, :], c_exp[:, :]))
        setup.settle()
        tt(silu_c[:, :], c_sb[:, :], c_exp[:, :], ALU.mult).then_inc(s_silu, 1)

        lns = Steps(dve, s_ln, 2 * TPG + 4)

        def stats1(g):
            lns.begin(g)
            dve.wait_ge(s_x, 16 * (g + 1))
            for t in range(TPG):
                lns.did(dve.bn_stats(st[:, t, :], xg[:, t, :]))
            lns.settle(wait_apart)
            for t in range(TPG):
                lns.did(dve.bn_aggr(mv[:, t, :], st[:, t, :]))
            lns.settle()
            ts(ve[:, :], mv[:, :, 1], LN_EPS, None, ALU.add).then_inc(s_var, 1)
            dve.wait_ge(s_seed, g + 1)
            newton(lns, y0[:, :], ve[:, :], nt1[:, :], nt2[:, :], None)
            for t in range(TPG):
                ts(xg[:, t, :], xg[:, t, :], mv[:, t, 0:1], nt2[:, t:t + 1], ALU.subtract, ALU.mult).then_inc(s_z, 1)
            lns.end()

        def newton(steps, y, v, a, res, factor):
            steps.did(tt(a, y, y, ALU.mult))
            steps.settle()
            steps.did(tt(a, a, v, ALU.mult))
            steps.settle()
            steps.did(ts(a, a, -0.5, 1.5, ALU.mult, ALU.add))
            steps.settle()
            if factor is None:
                steps.did(tt(res, y, a, ALU.mult))
            else:
                steps.did(stt(res, y, factor, a, ALU.mult, ALU.mult))
            steps.settle()

        def turn1(g, t):
            dve.wait_ge(s_T, TPG * g + t + 1)
            at_least(dve, s_hlo, TPG * g + t - 1)
            for f in range(FC):
                at = f * B + batch_of(g)
                last = ts(hf[t % 2][:, f, :], T_B[t % 2][:, f * P:(f + 1) * P], modcol[:, bass.ds(FC * B + at, 1)],
                          modcol[:, bass.ds(at, 1)], ALU.mult, ALU.add)
            last.then_inc(s_hf, 1)
            dve.wait_ge(s_hhi, TPG * g + t + 1)
            dve.wait_ge(s_hf, TPG * g + t + 1)
            tt(h_t[1][:, :, t * P:(t + 1) * P], hf[t % 2][:, :, :], f32(h_t[0][:, :, t * P:(t + 1) * P]), ALU.subtract).then_inc(s_hlo, 1)

        def split_lo(turn, half, hi, lo):
            dve.wait_ge(s_hi, 2 * turn + half + 1)
            dve.wait_ge(s_raw[half], 16 * (turn + 1))
            tt(lo, raw[:, half, :], f32(hi), ALU.subtract).then_inc(s_lo, 1)

        def mod_part(m):
            dve.wait_ge(s_modpe, m + 1)
            src = Q_B[m % 2][0:B, :]
            if m in (0, 3):
                dve.tensor_copy(mod_row[:, m, :], src).then_inc(s_modrow, 1)
            elif m in (1, 4):
                ts(mod_row[:, m, :], src, 1.0, None, ALU.add).then_inc(s_modrow, 1)
            else:
                setup.did(ts(mod_tmp[:, :], src, 0.0, 2.0, ALU.is_ge, ALU.mult))
                setup.settle()
                setup.did(ts(mod_tmp[:, :], mod_tmp[:, :], -1.0, None, ALU.add))
                setup.settle()
                setup.did(tt(mod_row[:, m, :], src, mod_tmp[:, :], ALU.mult))
                setup.settle()
                stt(mod_row[:, m, :], mod_row[:, m, :], 0.25, mod_tmp[:, :], ALU.max, ALU.mult).then_inc(s_modrow, 1)

        stats1(0)
        mod_part(0)
        mod_part(1)
        dve.wait_ge(s_colpe, 1)
        dve.tensor_copy(modcol[:, :], K_B[:, 0:2 * FC * B]).then_inc(s_col, 1)
        dve.wait_ge(s_col, 1)
        for f in range(FC):
            split_lo(f // 2, f % 2, wq[0][:, f, :], wq[1][:, f, :])
            turn1(0, f)
        for m in range(2, 6):
            mod_part(m)

        def group1(g, last=False):
            if not last:
                stats1(g + 1)
            split_lo(FC // 2 + g, 0, sp_hl[0][:, :], sp_hl[1][:, :])
            for t in range(TPG):
                dve.wait_ge(s_v, TPG * g + t + 1)
                at_least(dve, s_vk, TPG * g + t - 1)
                dve.tensor_copy(v_sb[t % 2][:, :, 0:P], V_B[:, :].rearrange("p (a n) -> p a n", a=HG)).then_inc(s_ve, 1)
                if not last:
                    turn1(g + 1, t)
                if t == 1:
                    split_lo(FC // 2 + g, 1, sp_hl[0][:, :], sp_hl[1][:, :])
            dve.wait_ge(s_vk, TPG * (g + 1))
            dve.wait_ge(s_kv, NG + g)
            for a in range(2):
                b = batch_of(g)
                acc = (kv[:, b, 2 * a:2 * a + 2, 0:P + 1] if isinstance(b, int) else
                       kv[:, bass.ds(b, 1), 2 * a:2 * a + 2, 0:P + 1].rearrange("p b a n -> p (b a) n"))
                last_add = tt(acc, acc, KV_B[a][:, 0:2 * VW].rearrange("p (a n) -> p a n", a=2)[:, :, 0:P + 1], ALU.add)
            last_add.then_inc(s_kv, 1)

        group1(0)
        with dve.Fori(1, NG - 1) as g:
            group1(g)
        group1(NG - 1, last=True)

        phase1_over(dve)
        nds = Steps(dve, s_ndstep, 0)
        nds.begin(0)
        dve.wait_ge(s_const, 16 * 5)
        dve.wait_ge(s_id, 14)
        nds.did(tt(rw[:, :, :], rw[:, :, :], rscale[:, :].unsqueeze(2).to_broadcast([P, FC, E]), ALU.mult))
        mask = headmask[:, :].unsqueeze(1).to_broadcast([P, HG, P])
        for b in range(B):
            nds.did(tt(ndf[:, :, 0, :], kv[:, b, :, P:P + 1].to_broadcast([P, HG, P]), mask, ALU.mult))
            nds.did(tt(ndf[:, :, 1, :], kv[:, b, :, 0:P], mask, ALU.mult))
            nds.settle()
            nds.did(dve.tensor_copy(nd[0][:, b, :, :, :].rearrange("p a k n -> p (a k n)"), ndf[:, :, :, :].rearrange("p a k n -> p (a k n)")))
            nds.settle()
            tt(nd[1][:, b, :, :, :].rearrange("p a k n -> p (a k n)"), ndf[:, :, :, :].rearrange("p a k n -> p (a k n)"),
               f32(nd[0][:, b, :, :, :].rearrange("p a k n -> p (a k n)")), ALU.subtract).then_inc(s_nd, 1)
            dve.wait_ge(s_nd, b + 1)

        rec = Steps(dve, s_rec, 1)

        def divide(g, j):
            rec.begin(HG * g + j)
            dve.wait_ge(s_dene, HG * g + j + 1)
            rec.did(dve.reciprocal(den_sb[j % 2][:, :], den_sb[j % 2][:, :]))
            dve.wait_ge(s_num, HG * g + j + 1)
            at_least(dve, s_onlo, HG * g + j - 1)
            rec.settle()
            tt(onf[j % 2][:, :], N_B[j % 2][:, :], den_sb[j % 2][:, :], ALU.mult).then_inc(s_on, 1)
            rec.end()

        l2 = Steps(dve, s_ln2, 2 * TPG + 2 * 4 + TPG)

        def residual(g, t):
            dve.wait_ge(s_y, TPG * g + t + 1)
            dve.wait_ge(s_xb, TPG * g + t + 1)
            if t == 0:
                at_least(dve, s_x1st, 16 * g)
            tt(x1[:, t, :], Y_B[t % 2][:, :], xb[:, t, :], ALU.add).then_inc(s_x1, 1)
            dve.wait_ge(s_x1, TPG * g + t + 1)
            l2.did(dve.bn_stats(st2[:, t, :], x1[:, t, :]))
            l2.settle(wait_apart)
            l2.did(dve.bn_aggr(mv2[:, t, :], st2[:, t, :]))

        def rstd2_of(g, half):
            h = slice(2 * half, 2 * half + 2)
            l2.settle()
            ts(ve2[:, h], mv2[:, h, 1], LN_EPS, None, ALU.add).then_inc(s_var2, 1)
            dve.wait_ge(s_seed2, 2 * g + half + 1)
            newton(l2, y2[:, h], ve2[:, h], na2[:, h], rstd2[:, h], None)

        def norm2(g, t, par):
            dve.wait_ge(s_free, g + 1)
            b = batch_of(g)

            def bc(k):
                return modbc[:, b, k, :] if isinstance(b, int) else modbc[:, bass.ds(b, 1), k, :].rearrange("p a n -> p (a n)")

            if t:
                dve.wait_ge(s_h2, TPG * g + t)
            l2.did(stt(lnt[:, :], x1[:, t, :], mv2[:, t, 0:1], bc(2), ALU.subtract, ALU.mult))
            l2.settle()
            stt(rows[par][:, t, 0:C], lnt[:, :], rstd2[:, t:t + 1], bc(1), ALU.mult, ALU.add).then_inc(s_h2, 1)

        r1 = Steps(dve, s_r1, 4 + 1 + 2 * TPG + 4 + 10)
        r2 = Steps(dve, s_r2, 4)

        def per_row(ap):
            return ap.unsqueeze(2).to_broadcast([P, TPG, E])

        def per_expert(ap):
            return ap.unsqueeze(1).to_broadcast([P, TPG, E])

        def route(g, par):
            r1.begin(g)
            dve.wait_ge(s_sq, TPG * (g + 1))
            ts(ve3[:, :], ss[:, :], 1.0 / C, RMS_EPS, ALU.mult, ALU.add).then_inc(s_var3, 1)
            dve.wait_ge(s_seed3, g + 1)
            newton(r1, y3[:, :], ve3[:, :], na3[:, :], rs3[:, :], float(np.float32(C) ** np.float32(-0.5)))
            dve.wait_ge(s_lg, TPG * (g + 1))
            r1.did(tt(lg[:, :, :], R_B[:, 0:TPG * E].rearrange("p (t e) -> p t e", e=E), per_row(rs3[:, :]), ALU.mult))
            r1.settle(wait_apart)
            for t in range(TPG):
                r1.did(dve.max(mx[:, t, :], lg[:, t, :]))
            r1.settle()
            tt(dl[:, :, :], lg[:, :, :], mx[:, :, 0:1].to_broadcast([P, TPG, E]), ALU.subtract).then_inc(s_dl, 1)
            for t in range(TPG):
                r1.did(dve.max_index(ix[:, t, :], mx[:, t, :], lg[:, t, :]))
            r1.settle()
            r1.did(dve.tensor_copy(ixf[:, :, :], ix[:, :, 0:2]))
            r1.settle()
            r1.did(tt(oh0[:, :, :], per_expert(iota_e[:, :]), ixf[:, :, 0:1].to_broadcast([P, TPG, E]), ALU.is_equal))
            r1.did(tt(oh1[:, :, :], per_expert(iota_e[:, :]), ixf[:, :, 1:2].to_broadcast([P, TPG, E]), ALU.is_equal))
            r1.settle()
            tt(mkb[:, :, :], oh0[:, :, :], oh1[:, :, :], ALU.add).then_inc(s_mk, 1)
            r1.did(tt(mk[:, :, :], oh0[:, :, :], oh1[:, :, :], ALU.add))
            dve.wait_ge(s_ex, g + 1)
            r1.did(dve.tensor_reduce(se[:, :], ex[:, :, :], AX.X, ALU.add))
            r1.settle()
            r1.did(dve.reciprocal(rse[:, :], se[:, :]))
            r1.settle()
            r1.did(tt(pr[:, :, :], ex[:, :, :], per_row(rse[:, :]), ALU.mult))
            r1.settle()
            r1.did(tt(ip[:, :, :], pr[:, :, :], mk[:, :, :], ALU.mult))
            r1.settle()
            r1.did(dve.tensor_reduce(rn[:, :], ip[:, :, :], AX.X, ALU.add))
            r1.settle()
            r1.did(ts(rng[:, :], rn[:, :], 0.0, None, ALU.is_le))
            r1.settle()
            r1.did(tt(rng[:, :], rng[:, :], rn[:, :], ALU.add))
            r1.settle()
            r1.did(dve.reciprocal(rrn[:, :], rng[:, :]))
            r1.settle()
            r1.did(tt(wts[:, :, :], ip[:, :, :], per_row(rrn[:, :]), ALU.mult))
            r1.settle()
            dve.wait_ge(s_free, g + 1)
            r1.did(tt(rows[par][:, :, W_AT:W_AT + E], wts[:, :, :], per_expert(pes_bc[:, :]), ALU.mult))
            r1.end()

        def place(g, par):
            r2.begin(g)
            dve.wait_ge(s_rank, g + 1)
            r2.did(tt(pos[:, :, :], R_B[:, TPG * E:2 * TPG * E].rearrange("p (t e) -> p t e", e=E), per_expert(next_row[:, :]), ALU.add))
            r2.settle()
            tt(next_row[:, :], next_row[:, :], R_B[:, 2 * TPG * E:2 * TPG * E + E], ALU.add).then_inc(s_ranku, 1)
            r2.did(tt(chosen[:, 0, :, :], pos[:, :, :], oh0[:, :, :], ALU.mult))
            r2.did(tt(chosen[:, 1, :, :], pos[:, :, :], oh1[:, :, :], ALU.mult))
            r2.settle()
            r2.did(dve.tensor_reduce(destf[:, :, :], chosen[:, :, :, :], AX.X, ALU.add))
            dve.wait_ge(s_free, g + 1)
            dve.wait_ge(s_r1, r1.each * (g + 1))
            r2.settle()
            dve.tensor_copy(dest[par][:, :, :], destf[:, :, :]).then_inc(s_dest, 1)
            r2.end()

        def group2(g, par, last=False, first=False):
            l2.begin(g)
            residual(g, 0)
            if not first:
                place(g - 1, 1 - par)
            residual(g, 1)
            rstd2_of(g, 0)
            norm2(g, 0, par)
            norm2(g, 1, par)
            residual(g, 2)
            residual(g, 3)
            rstd2_of(g, 1)
            if not last:
                divide(g + 1, 0)
            norm2(g, 2, par)
            if not last:
                divide(g + 1, 1)
            norm2(g, 3, par)
            if not last:
                divide(g + 1, 2)
                divide(g + 1, 3)
            l2.end()
            route(g, par)

        for j in range(HG):
            divide(0, j)
        group2(0, 0, first=True)
        with dve.Fori(0, (NG - 2) // 2) as j:
            group2(2 * j + 1, 1)
            group2(2 * j + 2, 0)
        group2(NG - 1, 1, last=True)
        place(NG - 1, 1)

        its = Steps(dve, s_it, ITEM_STEPS)
        its.begin(0)

        def step(ins):
            its.did(ins)
            its.settle()

        dve.wait_ge(s_ranku, NG)
        dve.wait_ge(s_padi, 2)
        ts(pad_to[:, E:E + 1], lane[:, :], float(E * CAP), None, ALU.add)
        ts(pad_to[:, 0:E], next_row[:, :], lane[:, 0:1], None, ALU.add).then_inc(s_padi, 1)
        step(tt(cnt[:, :], next_row[:, :], list_at[:, :], ALU.subtract))
        step(ts(cnti[:, :], cnt[:, :], 1.0, float(P - 1), ALU.max, ALU.add))
        step(ts(ntli[:, :], cnti[:, :], P.bit_length() - 1, None, ALU.arith_shift_right))
        step(dve.tensor_copy(ntl[:, :], ntli[:, :]))
        step(dve.tensor_copy(cend[:, :], ntl[:, :]))
        for e in range(1, E):
            step(tt(cend[:, e:e + 1], cend[:, e - 1:e], ntl[:, e:e + 1], ALU.add))
        step(ts(dlt[:, :], ntl[:, :], -float(P), float(CAP), ALU.mult, ALU.add))
        step(ts(it_r[:, :], item_no[:, :], float(P), None, ALU.mult))
        step(ts(it_e[:, :], item_no[:, :], 0.0, None, ALU.mult))
        for e in range(E - 1):
            step(stt(it_e[:, :], item_no[:, :], cend[:, e:e + 1], it_e[:, :], ALU.is_ge, ALU.add))
            step(ts(it_t[:, :], item_no[:, :], cend[:, e:e + 1], dlt[:, e:e + 1], ALU.is_ge, ALU.mult))
            step(tt(it_r[:, :], it_r[:, :], it_t[:, :], ALU.add))
        step(ts(it_t[:, :], item_no[:, :], cend[:, E - 1:E], None, ALU.is_lt))
        step(ts(it_r[:, :], it_r[:, :], -float(E * CAP), None, ALU.add))
        step(tt(it_r[:, :], it_r[:, :], it_t[:, :], ALU.mult))
        step(ts(it_r[:, :], it_r[:, :], float(E * CAP), None, ALU.add))
        step(dve.tensor_copy(tables[:, 0, :], it_r[:, :]))
        step(dve.tensor_copy(tables[:, 1, :], it_e[:, :]))
        its.end()

        phase2_over(dve)

        def x_lo(i):
            dve.wait_ge(s_xthi, i + 1)
            at_least(dve, s_u, i)
            tt(x_t[1][:, :], XT_B[:, :], f32(x_t[0][:, :]), ALU.subtract).then_inc(s_xtlo, 1)

        def keep_meta(i):
            dve.wait_ge(s_xr, 16 * (i + 1))
            dve.tensor_copy(meta[:, bass.ds((i % RING if isinstance(i, int) else i & (RING - 1)) * META, META)],
                            xrow[:, W_AT:W_AT + META]).then_inc(s_meta, 1)

        def glu(i):
            dve.wait_ge(s_u, i + 1)
            dve.wait_ge(s_ga, i + 1)
            at_least(dve, s_ht, i)
            tt(hact[:, :], U_B[:, :], gact[:, :], ALU.mult).then_inc(s_h, 1)

        def act_lo(i):
            dve.wait_ge(s_hthi, i + 1)
            tt(act_t[1][:, :], HT_B[:, :], f32(act_t[0][:, :]), ALU.subtract).then_inc(s_htlo, 1)

        gbs = Steps(dve, s_gbr, 3)

        def out_rows(i):
            gbs.begin(i)
            at = (i % RING if isinstance(i, int) else i & (RING - 1)) * META
            e = dve.value_load(tables[0:1, 1, bass.ds(i, 1)], min_val=0, max_val=E - 1)
            at_least(dve, s_add, 16 * i)
            dve.wait_ge(s_meta, i + 1)
            gbs.did(dve.tensor_copy(cur_w[:, :], meta[:, bass.ds(at + e, 1)]))
            gbs.did(dve.tensor_copy(cur_tok[:, :], meta[:, bass.ds(at + E, 1)].bitcast(U32)))
            gbs.settle()
            ts(in_b0[:, :], cur_tok[:, :], float(S), None, ALU.is_lt).then_inc(s_cur, 1)
            ts(in_b1[:, :], cur_tok[:, :], float(S), None, ALU.is_ge).then_inc(s_cur, 1)
            dve.wait_ge(s_cur, 2 * (i + 1))
            dve.wait_ge(s_gb0, i + 1)
            gbs.did(stt(gbr[:, :], modbc[:, 1, 3, :], in_b1[:, 0:1], gb0[:, :], ALU.mult, ALU.add))
            dve.wait_ge(s_o, i + 1)
            gbs.settle()
            stt(orow[:, :], O_B[:, :], cur_w[:, 0:1], gbr[:, :], ALU.mult, ALU.mult).then_inc(s_or, 1)
            gbs.end()

        keep_meta(0)
        x_lo(0)
        glu(0)
        keep_meta(1)
        x_lo(1)

        def item(i, last=False):
            act_lo(i - 1)
            glu(i)
            if not last:
                keep_meta(i + 1)
                x_lo(i + 1)
            out_rows(i - 1)

        item(1)
        with dve.Fori(2, ITEMS - 1) as i:
            item(i)
        item(ITEMS - 1, last=True)
        act_lo(ITEMS - 1)
        out_rows(ITEMS - 1)

    @block.tensor
    def _(pe):
        mm = pe.matmul

        pe.wait_ge(s_silu, 1)
        for m in range(6):
            pe.wait_ge(s_mod[m % 2], 16 * (m // 2 + 1))
            at_least(pe, s_modrow, m - 1)
            for f in range(FC):
                last = mm(Q_B[m % 2][0:B, :], silu_c[:, f * B:(f + 1) * B], mod_stage[m % 2][:, f, :], start=(f == 0), stop=(f == FC - 1))
            last.then_inc(s_modpe, 1)
            if m == 1:
                pe.wait_ge(s_id, 6)
                pe.wait_ge(s_modrow, 2)
                for r in range(2 * FC):
                    last = pe.transpose(K_B[:, r * B:(r + 1) * B], mod_row[:, r // FC, r % FC * P:(r % FC + 1) * P], ident[0:B, 0:B])
                last.then_inc(s_colpe, 1)

                def turn(g, t):
                    pe.wait_ge(s_z, TPG * g + t + 1)
                    at_least(pe, s_hf, TPG * g + t - 1)
                    for f in range(FC):
                        last = pe.transpose(T_B[t % 2][:, f * P:(f + 1) * P], xg[:, t, f * P:(f + 1) * P], ident[:, :])
                    last.then_inc(s_T, 1)

                for t in range(TPG):
                    turn(0, t)

        def product(dst, parts, n, stationary, moving):
            k = 0
            for f in range(n):
                for a, b in PASSES[:parts]:
                    last = mm(dst, stationary(a, f), moving(b, f), start=(k == 0), stop=(k == parts * n - 1))
                    k += 1
            return last

        def kv_sums(g, t):
            pe.wait_ge(s_ke, TPG * g + t + 1)
            pe.wait_ge(s_ve, TPG * g + t + 1)
            if t == 0:
                pe.wait_ge(s_kv, NG + g)
            for a in range(HG):
                last = mm(KV_B[a // 2][:, a % 2 * VW:a % 2 * VW + P + 1], k_sb[t % 2][:, a * P:(a + 1) * P], v_sb[t % 2][:, a, 0:P + 1],
                          start=(t == 0 and a % 2 == 0), stop=(t == TPG - 1), skip_group_check=True)
            last.then_inc(s_vk, 1)

        def group1(g, last=False):
            pe.wait_ge(s_hlo, TPG * (g + 1))
            for j in range(FC):
                at_least(pe, s_qe, FC * g + j - 1)
                product(Q_B[j % 2][:, :], 3, FC, lambda a, f: wq[a][:, f, j * P:(j + 1) * P],
                        lambda b, f: h_t[b][:, f, :]).then_inc(s_q, 1)
            for t in range(TPG):
                at_least(pe, s_ke, TPG * g + t)
                product(K_B[:, :], 3, FC, lambda a, f: h_t[a][:, f, t * P:(t + 1) * P],
                        lambda b, f: wq[b][:, f, C:2 * C]).then_inc(s_k, 1)
                at_least(pe, s_ve, TPG * g + t)
                product(V_B[:, :], 3, FC, lambda a, f: h_t[a][:, f, t * P:(t + 1) * P],
                        lambda b, f: wq[b][:, f, 2 * C:3 * C]).then_inc(s_v, 1)
                if not last:
                    turn(g + 1, t)
                if t:
                    kv_sums(g, t - 1)
            kv_sums(g, TPG - 1)

        pe.wait_ge(s_lo, FC)
        pe.wait_ge(s_modrow, 6)
        group1(0)
        with pe.Fori(1, NG - 1) as g:
            group1(g)
        group1(NG - 1, last=True)

        phase1_over(pe)
        pe.wait_ge(s_nd, B)

        def attend(g, b):
            pe.wait_ge(s_q2, 32 * (g + 1))
            for j in range(HG):
                at_least(pe, s_dene, HG * g + j - 1)
                product(D_B[j % 2][:, :], 3, 1, lambda a, f: nd[a][:, b, j, 0, :], lambda k, f: q2[k][:, j, :]).then_inc(s_den, 1)
                at_least(pe, s_on, HG * g + j - 1)
                product(N_B[j % 2][:, :], 3, 1, lambda a, f: nd[a][:, b, j, 1, :], lambda k, f: q2[k][:, j, :]).then_inc(s_num, 1)

        def rank(g):
            pe.wait_ge(s_mk, g + 1)
            for t in range(TPG):
                dst = R_B[:, (TPG + t) * E:(TPG + t + 1) * E]
                for s in range(t):
                    mm(dst, ones[:, :], mkb[:, s, :], start=(s == 0), stop=False)
                mm(dst, before[:, :], mkb[:, t, :], start=(t == 0), stop=True)
            for t in range(TPG):
                last = mm(R_B[:, 2 * TPG * E:2 * TPG * E + E], ones[:, :], mkb[:, t, :], start=(t == 0), stop=(t == TPG - 1))
            last.then_inc(s_rank, 1)

        def group2(g, par, b_next, first=False):
            b = batch_of(g)
            pe.wait_ge(s_onlo, HG * (g + 1))
            for t in range(TPG):
                at_least(pe, s_x1, TPG * g + t - 1)
                if t == 0:
                    at_least(pe, s_h2te, TPG * g)
                product(Y_B[t % 2][:, :], 3, FC, lambda a, f: on[a][:, f, t * P:(t + 1) * P],
                        lambda k, f: wp[k][:, b, f, :] if isinstance(b, int) else
                        wp[k][:, bass.ds(b, 1), f, :].rearrange("p a n -> p (a n)")).then_inc(s_y, 1)
                if t == 0 and not first:
                    rank(g - 1)
            if b_next is not None:
                attend(g + 1, b_next)
            pe.wait_ge(s_x1, TPG * (g + 1))
            at_least(pe, s_ranku, g)

            def logits(t):
                pe.wait_ge(s_h2te, TPG * g + t + 1)
                for f in range(FC):
                    last = mm(R_B[:, t * E:(t + 1) * E], h2t[:, t, f * P:(f + 1) * P], rw[:, f, :], start=(f == 0), stop=(f == FC - 1))
                last.then_inc(s_lg, 1)

            for t in range(TPG):
                pe.wait_ge(s_h2, TPG * g + t + 1)
                at_least(pe, s_h2te, TPG * g + t - 1)
                for f in range(FC):
                    last = pe.transpose(Y_B[t % 2][:, f * P:(f + 1) * P], rows[par][:, t, f * P:(f + 1) * P], ident[:, :])
                last.then_inc(s_h2t, 1)
                if t:
                    logits(t - 1)
            logits(TPG - 1)

        attend(0, 0)
        group2(0, 0, 0, first=True)
        with pe.Fori(0, (GPB - 2) // 2) as j:
            group2(2 * j + 1, 1, 0)
            group2(2 * j + 2, 0, 0)
        with pe.Fori((GPB - 2) // 2, (NG - 2) // 2) as j:
            group2(2 * j + 1, 1, 1)
            group2(2 * j + 2, 0, 1)
        group2(NG - 1, 1, None)
        rank(NG - 1)

        phase2_over(pe)

        def expert_of(i):
            return pe.value_load(tables[0:1, 1, bass.ds(i, 1)], min_val=0, max_val=E - 1)

        def weights(e, at):
            base = pe.snap((e & 1) * (2 * EW), min_val=0, max_val=2 * EW)
            return lambda k, f: wbuf[:, bass.ds(base + (at(f) // QW * 2 * QW + k * QW + at(f) % QW), 512)]

        def turn_rows(i):
            pe.wait_ge(s_xr, 16 * (i + 1))
            at_least(pe, s_xtlo, i)
            for f in range(FC):
                last = pe.transpose(XT_B[:, f * P:(f + 1) * P], xrow[:, f * P:(f + 1) * P], ident[:, :])
            last.then_inc(s_xt, 1)

        def gate(i, e):
            pe.wait_ge(s_xtlo, i + 1)
            pe.wait_ge(s_w, 16 * QPE * (e + 1))
            at_least(pe, s_ga, i)
            product(G_B[:, :], 3, FC, lambda a, f: x_t[a][:, f * P:(f + 1) * P], weights(e, lambda f: f * 2 * H)).then_inc(s_g, 1)

        def up(i, e):
            at_least(pe, s_h, i)
            product(U_B[:, :], 3, FC, lambda a, f: x_t[a][:, f * P:(f + 1) * P], weights(e, lambda f: f * 2 * H + H)).then_inc(s_u, 1)

        def turn_act(i):
            pe.wait_ge(s_h, i + 1)
            at_least(pe, s_htlo, i)
            for f in range(H // P):
                last = pe.transpose(HT_B[:, f * P:(f + 1) * P], hact[:, f * P:(f + 1) * P], ident[:, :])
            last.then_inc(s_ht, 1)

        def down(i, e):
            pe.wait_ge(s_htlo, i + 1)
            at_least(pe, s_or, i)
            product(O_B[:, :], 3, H // P, lambda a, f: act_t[a][:, f * P:(f + 1) * P], weights(e, lambda f: DOWN + f * C)).then_inc(s_o, 1)

        turn_rows(0)
        e = expert_of(0)
        gate(0, e)
        up(0, e)
        turn_rows(1)

        def item(i, last=False):
            e, e_before = expert_of(i), expert_of(i - 1)
            gate(i, e)
            turn_act(i - 1)
            up(i, e)
            if not last:
                turn_rows(i + 1)
            down(i - 1, e_before)

        item(1)
        with pe.Fori(2, ITEMS - 1) as i:
            item(i)
        item(ITEMS - 1, last=True)
        turn_act(ITEMS - 1)
        down(ITEMS - 1, expert_of(ITEMS - 1))

    ph3.close()
    keep.close()




def laid_out(i):
    def chunks(a):
        return np.ascontiguousarray(a.reshape(-1, P, a.shape[1]).transpose(1, 0, 2).reshape(P, -1))

    gate = i["L0_ffn_gating_einsum"].transpose(0, 3, 1, 2).reshape(E, C, 2 * H)
    experts = np.stack([np.concatenate([chunks(gate[e]), chunks(i["L0_ffn_linear"][e])], axis=1) for e in range(E)])
    experts = np.ascontiguousarray(experts.reshape(E, P, QPE, QW).transpose(0, 2, 1, 3).reshape(E * QPE * P, QW))
    return {
        "x": np.ascontiguousarray(i["L0_attn_x"].reshape(NT, C)),
        "c_t": chunks(i["L0_c"].T),
        "wmod": np.ascontiguousarray(i["L0_wmod"]),
        "wqkv": chunks(i["L0_attn_w_qkv"].T),
        "wproj": chunks(i["L0_attn_w_proj"].T),
        "b_proj": np.ascontiguousarray(i["L0_attn_b_proj"]),
        "r_w": chunks(i["L0_ffn_router_logits"]),
        "r_scale": chunks(i["L0_ffn_router_scale"].reshape(C, 1)),
        "pes": np.ascontiguousarray(i["L0_ffn_per_expert_scale"]),
        "moe_w": experts,
    }


def kernel(**inputs):
    from concourse import bacc
    from concourse.bass_utils import run_bass_kernel_spmd

    nc = bacc.Bacc("TRN2", target_bir_lowering=False, num_devices=1)
    arrays = laid_out({k: np.asarray(v) for k, v in inputs.items()})
    aps = {n: nc.dram_tensor(f"in_{n}", a.shape, F32, kind="ExternalInput").ap() for n, a in arrays.items()}
    out = nc.dram_tensor("out_rows", (NT + P, C), F32, kind="ExternalOutput").ap()
    build(nc, out=out, **aps)
    got = run_bass_kernel_spmd(nc, [{f"in_{n}": a for n, a in arrays.items()}], core_ids=[0])
    return got.results[0]["out_rows"][:NT].reshape(B, S, C)
```

```python
from contextlib import ExitStack

import numpy as np

import concourse.bass as bass
from concourse import mybir

F32 = mybir.dt.float32
F32R = mybir.dt.float32r
BF16 = mybir.dt.bfloat16
I32 = mybir.dt.int32
U32 = mybir.dt.uint32
ALU = mybir.AluOpType
ACT = mybir.ActivationFunctionType
AX = mybir.AxisListType

P = 128
B, S, C = 2, 4096, 512
E, H = 8, 512
HEAD = 32
NT = B * S
FC = C // P
GT = 512
TPG = GT // P
NG = NT // GT
GPB = NG // B
HG = C // P
HEADS = C // HEAD
LN_EPS = 1e-5
DEN_EPS = 1e-15
RMS_EPS = 1e-6
VW = 132
EW = FC * 2 * H + (H // P) * C
DOWN = FC * 2 * H
QW = 1536
QPE = EW // QW
CAP = NT + P
ROW = 528
W_AT, TOK_AT = C, C + E
META = 12
ITEMS = (2 * NT + E * (P - 1)) // P
RING = 4
EARLY = 3
SCAT = 16 * 2

PASSES = ((0, 0), (0, 1), (1, 0))


def at_least(eng, sem, value):
    if isinstance(value, int) and value <= 0:
        return
    eng.wait_ge(sem, value)


class Steps:

    def __init__(self, eng, sem, each):
        self.eng, self.sem, self.each = eng, sem, each

    def begin(self, turn, missing=0):
        self.base, self.n, self.at = turn * self.each - missing, 0, {}

    def did(self, ins, name=None):
        self.n += 1
        self.at[name] = self.n
        ins.then_inc(self.sem, 1)

    def after(self, name, wait=at_least):
        wait(self.eng, self.sem, self.base + self.at[name])

    def settle(self, wait=at_least):
        wait(self.eng, self.sem, self.base + self.n)

    def end(self, missing=0):
        assert self.n == self.each - missing, (self.n, self.each)


def build(nc, x, c_t, wmod, wqkv, wproj, b_proj, r_w, r_scale, pes, moe_w, out):
    qd = nc.dram_tensor("q_rows", (NG * P, FC * GT), F32, kind="Internal").ap()
    wd = nc.dram_tensor("expert_split", (E * QPE * P, 2 * QW), F32, kind="Internal").ap()
    mod_d = nc.dram_tensor("mod_rows", (B, 4 * C), F32, kind="Internal").ap()
    xs = nc.dram_tensor("expert_rows", (E * CAP + P, ROW), F32, kind="Internal").ap()

    keep, ph1, ph2, ph3 = ExitStack(), ExitStack(), ExitStack(), ExitStack()

    def sb(stack, name, shape, dt, side=None):
        return stack.enter_context(nc.sbuf_tensor(name, shape, dt, side=side) if side else nc.sbuf_tensor(name, shape, dt))

    def sem(name):
        return keep.enter_context(nc.semaphore(name))

    bank = [keep.enter_context(nc.psum_tensor(f"bank{i}", [P, 512], F32)) for i in range(8)]

    ident = sb(keep, "ident", [P, P], F32)
    before = sb(keep, "before", [P, P], BF16)
    ones = sb(keep, "ones", [P, P], BF16)
    headmask = sb(keep, "headmask", [P, P], F32)
    inhead = sb(keep, "inhead", [P, FC, HEADS], F32)
    iota_e = sb(keep, "iota_e", [P, E], F32)
    list_at = sb(keep, "list_at", [P, E], F32)
    lane = sb(keep, "lane", [P, 1], F32)
    item_no = sb(keep, "item_no", [P, ITEMS], F32)
    modcol = sb(keep, "modcol", [P, 2 * FC * B], F32)
    modbc = sb(keep, "modbc", [P, B, 4, C], F32)
    bproj = sb(keep, "bproj", [P, C], F32)
    gab = sb(keep, "gab", [P, B, C], F32)
    wproj_f = sb(keep, "wproj_f", [P, FC, C], F32)
    kv = sb(keep, "kv", [P, B, HG, VW], F32)
    rw = sb(keep, "rw", [P, FC, E], F32)
    rscale = sb(keep, "rscale", [P, FC], F32)
    pes_bc = sb(keep, "pes_bc", [P, E], F32)
    next_row = sb(keep, "next_row", [P, E], F32)
    tok_no = sb(keep, "tok_no", [P, TPG], F32)
    tables = sb(keep, "tables", [P, 3, ITEMS], I32)

    padrow = sb(keep, "padrow", [P, ROW], F32)
    pad_to = sb(keep, "pad_to", [P, E], U32)

    wq = [sb(ph1, f"wq_{k}", [P, 3 * FC * C], F32R) for k in ("hi", "lo")]
    raw = sb(ph1, "raw", [P, 2, QW], F32)
    sp_hl = [sb(ph1, f"split_{k}", [P, QW], F32R) for k in ("hi", "lo")]
    xg = sb(ph1, "xg", [P, TPG, C], F32)
    hf = [sb(ph1, f"hf{i}", [P, FC, P], F32) for i in range(2)]
    h_t = [[sb(ph1, f"h_t{i}_{k}", [P, FC, GT], F32R) for k in ("hi", "lo")] for i in range(2)]
    k_sb = [sb(ph1, f"k_sb{i}", [P, C], F32) for i in range(2)]
    v_sb = [sb(ph1, f"v_sb{i}", [P, HG, VW], F32) for i in range(2)]
    qf = [sb(ph1, f"qf{i}", [P, FC, GT], F32) for i in range(2)]
    mod_stage = [sb(ph1, f"mod_stage{i}", [P, FC, C], F32) for i in range(3)]
    mod_stage = [*mod_stage[:2], *mod_stage, qf[1]]
    modbc_flat = modbc[:, :, :, :].rearrange("p b m n -> p (b m n)")
    mod_row = modbc_flat[0:B, 0:6 * C].rearrange("b (m n) -> b m n", m=6)
    mod_tmp = modbc_flat[0:B, 6 * C:7 * C]
    c_sb = sb(ph1, "c_sb", [P, FC * B], F32)
    c_exp = sb(ph1, "c_exp", [P, FC * B], F32)
    silu_c = sb(ph1, "silu_c", [P, FC * B], F32)
    st = sb(ph1, "st", [P, TPG, 6], F32)
    mv = sb(ph1, "mv", [P, TPG, 2], F32)
    ve = sb(ph1, "ve", [P, TPG], F32)
    lnv = sb(ph1, "lnv", [P, TPG], F32)
    y0 = sb(ph1, "y0", [P, TPG], F32)
    nt1 = sb(ph1, "nt1", [P, TPG], F32)
    nt2 = sb(ph1, "nt2", [P, TPG], F32)
    ph1.close()

    def tile2(name, dt=F32R):
        return sb(ph2, name, [P, FC, GT], dt)

    on = [[tile2("on0_hi"), tile2("on0_lo")]]
    qb = [tile2(f"qb{i}", F32) for i in range(2)]
    xb = [sb(ph2, "xb0", [P, TPG, C], F32)]
    kvp = [sb(ph2, f"kvp_{k}", [P, B, FC, C], F32R) for k in ("hi", "lo")]
    on.append([tile2("on1_hi"), tile2("on1_lo")])
    xb.append(sb(ph2, "xb1", [P, TPG, C], F32))
    ksums = sb(ph2, "ksums", [P, B, FC, HEADS], F32)
    ksum_now = sb(ph2, "ksum_now", [P, FC, HEADS], F32)
    sel_f = sb(ph2, "sel_f", [HEADS, C], F32)
    sel = sb(ph2, "sel", [HEADS, C], F32R)
    den = sb(ph2, "den", [HEADS, GT], F32)
    rec0 = sb(ph2, "rec0", [HEADS, GT], F32)
    rec = sb(ph2, "rec", [HEADS, GT], F32)
    rec_hl = [sb(ph2, f"rec_{k}", [HEADS, GT], F32R) for k in ("hi", "lo")]
    onf = [sb(ph2, f"onf{i}", [P, GT], F32) for i in range(2)]
    x1 = sb(ph2, "x1", [P, TPG, C], F32)
    lnt = [sb(ph2, f"lnt{i}", [P, C], F32) for i in range(2)]
    rows = [sb(ph2, f"rows{i}", [P, TPG, ROW], F32) for i in range(2)]
    kvp_f = [[rows[b][:, t, 0:C] for t in range(TPG)] for b in range(B)]
    h2t = sb(ph2, "h2t", [P, TPG, C], F32)
    sq_out = sb(ph2, "sq_out", [P, C], F32)
    lg_t = sb(ph2, "lg_t", [E, GT], F32)
    ss = sb(ph2, "ss", [P, TPG], F32)
    st2 = sb(ph2, "st2", [P, TPG, 6], F32)
    mv2 = sb(ph2, "mv2", [P, TPG, 2], F32)
    ve2, ln2, y2, na2, nb2, rstd2 = (sb(ph2, f"ln2_{i}", [P, TPG], F32) for i in range(6))
    ve3, ln3, y3, na3, nb3, rs3 = (sb(ph2, f"rms_{i}", [P, TPG], F32) for i in range(6))
    lg, mx, dl, ex, em, ip, wts, pos = (sb(ph2, f"route_{i}", [P, TPG, E], F32) for i in range(8))
    oh = sb(ph2, "oh", [P, 2, TPG, E], F32)
    chosen = sb(ph2, "chosen", [P, 2, TPG, E], F32)
    destf = sb(ph2, "destf", [P, 2, TPG], F32)
    ix = sb(ph2, "ix", [P, TPG, E], U32)
    ixf = sb(ph2, "ixf", [P, 2, TPG], F32)
    mkb = sb(ph2, "mkb", [P, TPG, E], BF16)
    se, rse, rn, rng, rrn = (sb(ph2, f"sum_{i}", [P, TPG], F32) for i in range(5))
    dest = [sb(ph2, f"dest{i}", [P, 2, TPG], U32) for i in range(2)]
    cnt, ntl, cend = (sb(ph2, f"cnt_{i}", [P, E], F32) for i in range(3))
    cnti = sb(ph2, "cnti", [P, E], I32)
    ntli = sb(ph2, "ntli", [P, E], I32)
    it_e, it_r, it_t, it_k = (sb(ph2, f"it_{i}", [P, ITEMS], F32) for i in range(4))
    ph2.close()

    wbuf = sb(ph3, "wbuf", [P, 2 * 2 * EW], F32R)
    xrow = [sb(ph3, f"xrow{i}", [P, ROW], F32) for i in range(RING)]
    x_t = [sb(ph3, f"x_t_{k}", [P, C], F32R) for k in ("hi", "lo")]
    act_t = [sb(ph3, f"act_t_{k}", [P, H], F32R) for k in ("hi", "lo")]
    gact = sb(ph3, "gact", [P, H], F32)
    hact = sb(ph3, "hact", [P, H], F32)
    meta = [sb(ph3, f"meta{i}", [P, META], F32) for i in range(RING)]
    cur_w = sb(ph3, "cur_w", [P, 1], F32)
    cur_tok = [sb(ph3, f"cur_tok{i}", [P, 1], U32) for i in range(2)]
    in_b1 = sb(ph3, "in_b1", [P, 1], F32)
    in_b0 = sb(ph3, "in_b0", [P, 1], F32)
    gb0 = sb(ph3, "gb0", [P, C], F32)
    gbr = sb(ph3, "gbr", [P, C], F32)
    orow = [sb(ph3, f"orow{i}", [P, C], F32) for i in range(2)]

    def f32(ap):
        return ap.bitcast(F32)

    T_B, Q_B, K_B, V_B, KV_B = bank[0:2], bank[2:4], bank[4], bank[5], bank[6:8]
    Y_B, H2_B, RB_B, D_B, R_B = bank[0:2], bank[2:4], bank[4:6], bank[6], bank[7]
    M_B = [bank[2:6], [*bank[2:4], *bank[2:4]]]
    XT_B, HT_B, G_B, U_B, O_B = bank[0], bank[1], bank[2], bank[3], bank[4]

    s_c, s_x, s_const = sem("c_loaded"), sem("x_loaded"), sem("const_loaded")
    s_raw, s_mod = [sem("raw_even"), sem("raw_odd")], [sem(f"wmod{m}_loaded") for m in range(6)]
    s_modst, s_modbc = sem("mod_stored"), sem("modbc_loaded")
    s_qst, s_wst, s_zst = sem("q_stored"), sem("split_stored"), sem("zero_stored")
    s_passed = sem("waits_passed")
    s_id, s_vset, s_cexp, s_silu, s_modpe, s_modrow, s_colpe, s_col = (
        sem("ident_ready"), sem("vector_setup"), sem("c_exp_ready"), sem("silu_ready"), sem("mod_product"),
        sem("mod_row_ready"), sem("mod_col_turned"), sem("mod_col_ready"))
    s_gab = sem("gab_ready")
    s_hi, s_lo, s_elo = sem("split_hi"), sem("qkv_split_lo"), sem("expert_split_lo")
    s_var, s_seed, s_z, s_ln = sem("var_ready"), sem("rstd_seed"), sem("z_ready"), sem("ln1_step")
    s_T, s_hf, s_hhi, s_hlo = sem("z_turned"), sem("h_ready"), sem("h_hi_ready"), sem("h_lo_ready")
    s_q, s_qe = sem("q_done"), sem("q_taken")
    s_k, s_v, s_ke, s_ve, s_vk, s_kv = sem("k_done"), sem("v_done"), sem("k_taken"), sem("v_taken"), sem("kv_done"), sem("kv_added")
    s_aln = sem("scalar_ln_step")
    s_prep, s_kvm, s_kvt, s_kvte, s_mp, s_mf, s_mhi, s_mlo, s_sel = (
        sem("prep_step"), sem("sums_ready"), sem("sums_turned"), sem("turned_sums_taken"), sem("kvp_done"),
        sem("kvp_ready"), sem("kvp_hi_ready"), sem("kvp_lo_ready"), sem("sel_ready"))
    s_q2, s_x2, s_x1st, s_ksum = sem("q_back"), sem("x_back"), sem("x1_stored"), sem("ksum_ready")
    s_den, s_dene, s_aden, s_rec0, s_recstep, s_rec, s_rechi, s_reclo, s_rb, s_on = (
        sem("den_done"), sem("den_taken"), sem("scalar_den_step"), sem("recip_seed"), sem("recip_step"), sem("recip_ready"),
        sem("recip_hi_ready"), sem("recip_lo_ready"), sem("recip_spread"), sem("on_ready"))
    s_onhi, s_onlo, s_y, s_xb, s_x1 = sem("on_hi_ready"), sem("on_lo_ready"), sem("proj_done"), sem("xb_ready"), sem("x1_ready")
    s_step2, s_var2, s_seed2, s_aln2 = sem("vector_step2"), sem("var2_ready"), sem("rstd2_seed"), sem("scalar_ln2_step")
    s_h2, s_sq, s_h2t, s_h2te = sem("h2_ready"), sem("sq_ready"), sem("h2_turned"), sem("h2t_ready")
    s_lgp, s_lgt, s_lg = sem("logits_done"), sem("logits_taken"), sem("logits_turned")
    s_var3, s_seed3, s_aln3, s_ex, s_dl = sem("rms_ready"), sem("rms_seed"), sem("scalar_rms_step"), sem("exp_ready"), sem("logits_less_max")
    s_mk, s_rank, s_ranku = sem("mask_ready"), sem("rank_done"), sem("rank_taken")
    s_rowm, s_free, s_dest = sem("row_numbers"), sem("rows_cleared"), sem("dest_ready")
    s_scat = [sem(f"tile{t}_scattered") for t in range(TPG)]
    s_it, s_pad0, s_pad, s_padi = sem("item_step"), sem("first_pads_scattered"), sem("pads_scattered"), sem("pad_rows_ready")
    s_w, s_xt, s_xthi, s_xtlo, s_meta = sem("weights_loaded"), sem("x_turned"), sem("x_hi_ready"), sem("x_lo_ready"), sem("meta_kept")
    s_xr = [sem(f"rows{i}_loaded") for i in range(RING)]
    s_g, s_u, s_ga, s_h, s_ht, s_hthi, s_htlo = sem("gate_done"), sem("up_done"), sem("gelu_ready"), sem("act_ready"), sem("act_turned"), sem("act_hi_ready"), sem("act_lo_ready")
    s_o, s_cur, s_gb0, s_gbr, s_or, s_add = sem("down_done"), sem("cur_ready"), sem("gb0_ready"), sem("gb_rows_step"), sem("out_rows_ready"), sem("rows_added")

    def wait_apart(eng, sem, value):
        at_least(eng, sem, value)
        if not isinstance(value, int):
            eng.sem_inc(s_passed, 1)

    def group_rows(t, g):
        return t[bass.ds(g * GT, GT), :].rearrange("(t p) c -> p t c", p=P)

    def has(g, ahead):
        return not isinstance(g, int) or g + ahead < NG

    def run_groups2(eng, group2, before_last=None):
        for g in range(3):
            group2(g, g % 2)
        with eng.Fori(1, (NG - 4) // 2) as j:
            group2(2 * j + 1, 1)
            group2(2 * j + 2, 0)
        for g in range(NG - 3, NG):
            if before_last and g == NG - 1:
                before_last()
            group2(g, g % 2)

    def run_items(eng, item):
        for i in range(1, RING + 2):
            item(i, i % RING)
        with eng.Fori(1, (ITEMS - 3) // RING) as j:
            for u in range(RING):
                item(RING * j + 2 + u, (2 + u) % RING)
        item(ITEMS - 1, (ITEMS - 1) % RING)

    assert (ITEMS - 3) % RING == 0

    def batch_of(g):
        return g // GPB if isinstance(g, int) else (g >> 3) & 1

    assert GPB == 8

    def phase1_over(eng):
        eng.wait_ge(s_kv, 2 * NG)
        eng.wait_ge(s_qst, 16 * NG)
        eng.wait_ge(s_wst, 32 * E * QPE)
        eng.wait_ge(s_gab, B)

    def phase2_over(eng):
        for t in range(TPG):
            eng.wait_ge(s_scat[t], SCAT * NG)
        eng.wait_ge(s_pad0, 16)
        eng.wait_ge(s_x1st, 16 * NG)
        eng.wait_ge(s_zst, 32)
        eng.wait_ge(s_it, ITEM_STEPS)

    ITEM_STEPS = 5 + E - 1 + 11

    block = keep.enter_context(nc.Block())

    @block.sync
    def _(sp):
        sp.dma_start(c_sb[:, :], c_t).then_inc(s_c, 16)
        sp.dma_start(xg[:, :, :], group_rows(x, 0)).then_inc(s_x, 16)

        def load_wmod(m):
            if m in (2, 3):
                sp.wait_ge(s_modpe, m - 1)
            sp.dma_start(mod_stage[m][:, :, :], wmod[:, m * C:(m + 1) * C].rearrange("(f p) n -> p f n", p=P)).then_inc(s_mod[m], 16)

        load_wmod(0)
        load_wmod(1)
        for f in range(FC):
            at_least(sp, s_lo, f - 1)
            sp.dma_start(raw[:, f % 2, :], wqkv[:, f * QW:(f + 1) * QW]).then_inc(s_raw[f % 2], 16)

        def load_x1(g):
            sp.wait_ge(s_T, TPG * g)
            sp.dma_start(xg[:, :, :], group_rows(x, g)).then_inc(s_x, 16)

        load_x1(1)
        for m in range(2, 6):
            load_wmod(m)

        def load_expert_raw(g, s):
            if isinstance(g, int) and g == 0:
                sp.wait_ge(s_lo, FC)
            else:
                sp.wait_ge(s_elo, 2 * (g - 1) + s + 1)
            sp.dma_start(raw[:, s, :], moe_w[bass.ds((2 * g + s) * P, P), :]).then_inc(s_raw[s], 16)

        def store_expert(g, s):
            sp.wait_ge(s_elo, 2 * g + s + 1)
            for k in range(2):
                sp.dma_start(wd[bass.ds((2 * g + s) * P, P), k * QW:(k + 1) * QW], f32(sp_hl[k][:, :])).then_inc(s_wst, 16)

        for s in range(2):
            load_expert_raw(0, s)
        sp.dma_start(wproj_f[:, :, :], wproj.rearrange("p (f n) -> p f n", f=FC)).then_inc(s_const, 16)
        sp.dma_start(bproj[:, :], b_proj.partition_broadcast(P)).then_inc(s_const, 16)
        sp.dma_start(rw[:, :, :], r_w.rearrange("p (f e) -> p f e", f=FC)).then_inc(s_const, 16)
        sp.dma_start(rscale[:, :], r_scale).then_inc(s_const, 16)
        sp.dma_start(pes_bc[:, :], pes.partition_broadcast(P)).then_inc(s_const, 16)

        def group1(g, par, last=False):
            if not last and not (isinstance(g, int) and g == 0):
                load_x1(g + 1)
            store_expert(g, 0)
            if not last:
                load_expert_raw(g + 1, 0)
            wait_apart(sp, s_qst, 16 * g)
            sp.wait_ge(s_qe, FC * (g + 1))
            sp.dma_start(qd[bass.ds(g * P, P), :], qf[par][:, :, :].rearrange("p f t -> p (f t)")).then_inc(s_qst, 16)
            store_expert(g, 1)
            if not last:
                load_expert_raw(g + 1, 1)

        for g in range(3):
            group1(g, g % 2)
        with sp.Fori(1, (NG - 2) // 2) as j:
            group1(2 * j + 1, 1)
            group1(2 * j + 2, 0)
        group1(NG - 1, 1, last=True)

        phase1_over(sp)

        def load_q(g, par):
            wait_apart(sp, s_q2, 16 * g)
            wait_apart(sp, s_on, HG * (g - 1))
            sp.dma_start(qb[par][:, :, :].rearrange("p f t -> p (f t)"), qd[bass.ds(g * P, P), :]).then_inc(s_q2, 16)

        def load_x(g, par):
            wait_apart(sp, s_x2, 16 * g)
            sp.dma_start(xb[par][:, :, :], group_rows(x, g)).then_inc(s_x2, 16)

        load_q(0, 0)
        load_x(0, 0)
        load_q(1, 1)
        load_x(1, 1)
        sp.wait_ge(s_padi, 1)
        sp.dma_start(out[NT:NT + P, :], padrow[:, 0:C]).then_inc(s_zst, 16)
        sp.wait_ge(s_padi, 2)
        sp.dma_start(xs[E * CAP:E * CAP + P, :], padrow[:, :]).then_inc(s_zst, 16)

        def group2(g, par):
            more = has(g, 2)
            if more:
                load_q(g + 2, par)
            sp.wait_ge(s_x1, TPG * (g + 1))
            sp.dma_start(group_rows(out, g), x1[:, :, :]).then_inc(s_x1st, 16)
            if more:
                load_x(g + 2, par)

        def load_piece(e, half, q):
            sp.dma_start(f32(wbuf[:, bass.ds(half * 2 * EW + q * 2 * QW, 2 * QW)]),
                         wd[bass.ds((e * QPE + q) * P, P), :]).then_inc(s_w, 16)

        def early_weights():
            sp.wait_ge(s_on, HG * NG)
            for q in range(EARLY):
                sp.wait_ge(s_x1, TPG * (NG - 1) + q)
                load_piece(0, 0, q)

        run_groups2(sp, group2, before_last=early_weights)

        for q in range(EARLY, QPE):
            load_piece(0, 0, q)
        phase2_over(sp)

        def load_rows(i, at):
            if not isinstance(i, int) or i >= RING:
                sp.wait_ge(s_xt, i - RING + 1)
                wait_apart(sp, s_meta, i - RING + 1)
            r = sp.value_load(tables[0:1, 0, bass.ds(i, 1)], min_val=0, max_val=E * CAP)
            sp.dma_start(xrow[at][:, :], xs[bass.ds(r, P), :]).then_inc(s_xr[at], 16)

        def next_weights(i):
            e = sp.value_load(tables[0:1, 1, bass.ds(i, 1)], min_val=0, max_val=E - 1)
            e_after = sp.value_load(tables[0:1, 1, bass.ds(i + 1, 1)], min_val=0, max_val=E - 1)
            of_e = sp.value_load(tables[0:1, 2, bass.ds(i, 1)], min_val=0, max_val=ITEMS)

            def piece(q):
                wait_apart(sp, s_w, 16 * QPE * (e + 1))
                wait_apart(sp, s_o, i)
                nxt = sp.value_load(tables[0:1, 1, bass.ds(i, 1)], min_val=0, max_val=E - 2) + 1
                load_piece(nxt, nxt & 1, q)

            with sp.If(e > 0):
                with sp.If(e < E - 1):
                    with sp.If(of_e < 1):
                        for q in range(QPE // 2):
                            piece(q)
                        with sp.If(e_after > e):
                            for q in range(QPE // 2, QPE):
                                piece(q)
                    with sp.If(of_e > 0):
                        with sp.If(of_e < 2):
                            for q in range(QPE // 2, QPE):
                                piece(q)

        load_rows(0, 0)
        sp.wait_ge(s_pad, 16 * (E - 1))
        for i in range(1, RING):
            load_rows(i, i)
        sp.wait_ge(s_w, 16 * QPE)
        for q in range(QPE):
            load_piece(1, 1, q)
        load_rows(RING, 0)

        def step(i, at):
            load_rows(i, at)
            next_weights(i - RING)

        first = RING + 1
        with sp.Fori(0, (ITEMS - first) // RING) as j:
            for u in range(RING):
                step(first + RING * j + u, (first + u) % RING)
        for i in range(ITEMS - (ITEMS - first) % RING, ITEMS):
            step(i, i % RING)
        for i in range(ITEMS - RING, ITEMS - 1):
            next_weights(i)
        sp.wait_ge(s_add, 16 * ITEMS)

    @block.gpsimd
    def _(pool):
        pool.memset(ident[:, :], 0.0).then_inc(s_id, 1)
        pool.memset(before[:, :], 1.0).then_inc(s_id, 1)
        pool.memset(ones[:, :], 1.0).then_inc(s_id, 1)
        pool.memset(headmask[:, :], 1.0).then_inc(s_id, 1)
        pool.memset(inhead[:, :, :], 1.0).then_inc(s_id, 1)
        pool.wait_ge(s_id, 5)
        pool.affine_select(out=ident[:, :], in_=ident[:, :], compare_op=ALU.not_equal, fill=1.0, base=0,
                           pattern=[[-1, P]], channel_multiplier=1).then_inc(s_id, 1)
        pool.affine_select(out=before[:, :], in_=before[:, :], compare_op=ALU.is_gt, fill=0.0, base=0,
                           pattern=[[1, P]], channel_multiplier=-1).then_inc(s_id, 1)
        blocks = headmask[:, :].rearrange("p (a n) -> p a n", n=HEAD)
        pool.affine_select(out=blocks, in_=blocks, compare_op=ALU.is_ge, fill=0.0, base=0,
                           pattern=[[-HEAD, P // HEAD], [0, HEAD]], channel_multiplier=1).then_inc(s_id, 1)
        pool.wait_ge(s_id, 8)
        pool.affine_select(out=blocks, in_=blocks, compare_op=ALU.is_ge, fill=0.0, base=HEAD - 1,
                           pattern=[[HEAD, P // HEAD], [0, HEAD]], channel_multiplier=-1).then_inc(s_id, 1)
        pool.affine_select(out=inhead[:, :, :], in_=inhead[:, :, :], compare_op=ALU.is_ge, fill=0.0, base=0,
                           pattern=[[P, FC], [-HEAD, HEADS]], channel_multiplier=1).then_inc(s_id, 1)
        pool.wait_ge(s_id, 10)
        pool.affine_select(out=inhead[:, :, :], in_=inhead[:, :, :], compare_op=ALU.is_ge, fill=0.0, base=HEAD - 1,
                           pattern=[[-P, FC], [HEAD, HEADS]], channel_multiplier=-1).then_inc(s_id, 1)
        pool.iota(iota_e[:, :], [[1, E]], base=0, channel_multiplier=0, allow_small_or_imprecise_dtypes=True).then_inc(s_id, 1)
        pool.iota(lane[:, :], [[1, 1]], base=0, channel_multiplier=1, allow_small_or_imprecise_dtypes=True).then_inc(s_id, 1)
        pool.iota(list_at[:, :], [[CAP, E]], base=0, channel_multiplier=0, allow_small_or_imprecise_dtypes=True).then_inc(s_id, 1)
        pool.iota(next_row[:, :], [[CAP, E]], base=0, channel_multiplier=0, allow_small_or_imprecise_dtypes=True).then_inc(s_id, 1)
        pool.iota(item_no[:, :], [[1, ITEMS]], base=0, channel_multiplier=0, allow_small_or_imprecise_dtypes=True).then_inc(s_id, 1)
        pool.iota(tok_no[:, :], [[P, TPG]], base=0, channel_multiplier=1, allow_small_or_imprecise_dtypes=True).then_inc(s_id, 1)

        def low_expert(g, s):
            pool.wait_ge(s_hi, FC + 2 * g + s + 1)
            pool.tensor_tensor(sp_hl[1][:, :], raw[:, s, :], f32(sp_hl[0][:, :]), ALU.subtract).then_inc(s_elo, 1)

        def group1(g):
            for s in range(2):
                low_expert(g, s)

        group1(0)
        pool.wait_ge(s_modrow, 6)
        pool.dma_start(mod_d.rearrange("b (m n) -> b m n", m=4), mod_row[:, 2:6, :]).then_inc(s_modst, 16)
        pool.wait_ge(s_modst, 16)
        pool.wait_ge(s_col, 1)
        for b in range(B):
            pool.dma_start(modbc[:, b, :, :].rearrange("p m n -> p (m n)"), mod_d[b, :].partition_broadcast(P)).then_inc(s_modbc, 16)
        pool.wait_ge(s_modbc, 16 * B)
        pool.wait_ge(s_const, 16 * 5)
        for b in range(B):
            pool.tensor_tensor(gab[:, b, :], modbc[:, b, 0, :], bproj[:, :], ALU.mult).then_inc(s_gab, 1)
        with pool.Fori(1, NG) as g:
            group1(g)

        phase1_over(pool)
        for i in range(2):
            pool.memset(rows[i][:, :, C:], 0.0).then_inc(s_free, 1)
        pool.memset(padrow[:, :], 0.0).then_inc(s_padi, 1)
        pool.wait_ge(s_padi, 1)
        pool.tensor_scalar(padrow[:, TOK_AT:TOK_AT + 1].bitcast(I32), lane[:, :], float(NT), None, ALU.add).then_inc(s_padi, 1)

        def add_bias(g, par):
            pool.wait_ge(s_x2, 16 * (g + 1))
            for t in range(TPG):
                b = batch_of(g)
                row = gab[:, b, :] if isinstance(b, int) else gab[:, bass.ds(b, 1), :].rearrange("p a n -> p (a n)")
                pool.tensor_tensor(xb[par][:, t, :], xb[par][:, t, :], row, ALU.add).then_inc(s_xb, 1)

        def low_on(g, par, j):
            pool.wait_ge(s_onhi, HG * g + j + 1)
            pool.tensor_tensor(on[par][1][:, j, :], onf[j % 2][:, :], f32(on[par][0][:, j, :]), ALU.subtract).then_inc(s_onlo, 1)

        pool.memset(sel_f[:, :], 1.0).then_inc(s_sel, 1)
        pool.wait_ge(s_sel, 1)
        pool.affine_select(out=sel_f[:, :], in_=sel_f[:, :], compare_op=ALU.is_ge, fill=0.0, base=0,
                           pattern=[[1, C]], channel_multiplier=-HEAD).then_inc(s_sel, 1)
        pool.wait_ge(s_sel, 2)
        pool.affine_select(out=sel_f[:, :], in_=sel_f[:, :], compare_op=ALU.is_ge, fill=0.0, base=HEAD - 1,
                           pattern=[[-1, C]], channel_multiplier=HEAD).then_inc(s_sel, 1)
        pool.wait_ge(s_sel, 3)
        pool.tensor_copy(sel[:, :], sel_f[:, :]).then_inc(s_sel, 1)

        def number_rows(g, par):
            if not isinstance(g, int) or g:
                wait_apart(pool, s_rowm, 2 * g)
            pool.tensor_copy(rows[par][:, :, TOK_AT].bitcast(I32), tok_no[:, :]).then_inc(s_rowm, 1)
            wait_apart(pool, s_rowm, 2 * g + 1)
            pool.tensor_scalar(tok_no[:, :], tok_no[:, :], float(GT), None, ALU.add).then_inc(s_rowm, 1)

        def scatter(g, par):
            pool.wait_ge(s_dest, g + 1)
            wait_apart(pool, s_rowm, 2 * g + 1)
            for t in range(TPG):
                wait_apart(pool, s_scat[t], SCAT * g)
                for k in range(2):
                    pool.indirect_dma_start(out=xs, out_offset=bass.IndirectOffsetOnAxis(dest[par][:, k, t:t + 1], 0),
                                            in_=rows[par][:, t, :], in_offset=None).then_inc(s_scat[t], 16)

        def group2(g, par):
            if has(g, 1):
                low_on(g + 1, 1 - par, 0)
                low_on(g + 1, 1 - par, 1)
                if not isinstance(g, int) or g:
                    add_bias(g + 1, 1 - par)
                low_on(g + 1, 1 - par, 2)
                low_on(g + 1, 1 - par, 3)
                if isinstance(g, int) and g == 0:
                    add_bias(g + 1, 1 - par)
            if not isinstance(g, int) or g:
                scatter(g - 1, 1 - par)
            number_rows(g, par)

        add_bias(0, 0)
        for j in range(HG):
            low_on(0, 0, j)
        run_groups2(pool, group2)
        pool.wait_ge(s_padi, 3)

        def pad(e):
            return pool.indirect_dma_start(out=xs, out_offset=bass.IndirectOffsetOnAxis(pad_to[:, e:e + 1], 0),
                                           in_=padrow[:, :], in_offset=None)

        pad(0).then_inc(s_pad0, 16)
        scatter(NG - 1, 1)
        for e in range(1, E):
            pad(e).then_inc(s_pad, 16)

        phase2_over(pool)

        def item(i, at):
            pool.wait_ge(s_or, i + 1)
            wait_apart(pool, s_add, 16 * i)
            pool.indirect_dma_start(out=out, out_offset=bass.IndirectOffsetOnAxis(cur_tok[at % 2][:, 0:1], 0), in_=orow[at % 2][:, :],
                                    in_offset=None, compute_op=ALU.add).then_inc(s_add, 16)

        item(0, 0)
        run_items(pool, item)
        pool.wait_ge(s_add, 16 * ITEMS)

    @block.scalar
    def _(act):
        act.preload_act_table_set("natural_log_exp_and_others")
        act.wait_ge(s_c, 16)
        act.activation(c_exp[:, :], c_sb[:, :], ACT.Exp, scale=-1.0).then_inc(s_cexp, 1)

        def split_hi(turn, half, dst):
            act.wait_ge(s_raw[half], 16 * (turn + 1))
            act.activation(dst, raw[:, half, :], ACT.Copy).then_inc(s_hi, 1)

        def expert_hi(g, s):
            at_least(act, s_wst, 32 * (2 * g + s))
            split_hi(FC // 2 + g, s, sp_hl[0][:, :])

        aln = Steps(act, s_aln, 1)

        def seed1(g):
            aln.begin(g)
            act.wait_ge(s_var, g + 1)
            aln.did(act.activation(lnv[:, :], ve[:, :], ACT.Ln))
            aln.settle()
            act.activation(y0[:, :], lnv[:, :], ACT.Exp, scale=-0.5).then_inc(s_seed, 1)
            aln.end()

        def hi1(g, t, par):
            act.wait_ge(s_hf, TPG * g + t + 1)
            act.activation(h_t[par][0][:, :, t * P:(t + 1) * P], hf[t % 2][:, :, :], ACT.Copy).then_inc(s_hhi, 1)

        seed1(0)
        for f in range(2):
            split_hi(f // 2, f % 2, wq[0][:, f * QW:(f + 1) * QW])
        for t in range(TPG):
            hi1(0, t, 0)
        for f in range(2, FC):
            split_hi(f // 2, f % 2, wq[0][:, f * QW:(f + 1) * QW])

        def group1(g, par, last=False):
            for j in range(FC):
                act.wait_ge(s_q, FC * g + j + 1)
                if j == 0:
                    at_least(act, s_qst, 16 * (g - 1))
                act.activation(qf[par][:, j, :], Q_B[j % 2][:, :], ACT.Relu).then_inc(s_qe, 1)
                if j == 1 and not last:
                    seed1(g + 1)
            expert_hi(g, 0)
            for t in range(TPG):
                if not last:
                    hi1(g + 1, t, 1 - par)
                act.wait_ge(s_k, TPG * g + t + 1)
                at_least(act, s_vk, TPG * g + t - 1)
                act.activation(k_sb[t % 2][:, :], K_B[:, :], ACT.Relu).then_inc(s_ke, 1)
                if t == 1:
                    expert_hi(g, 1)

        for g in range(3):
            group1(g, g % 2)
        with act.Fori(1, (NG - 2) // 2) as j:
            group1(2 * j + 1, 1)
            group1(2 * j + 2, 0)
        group1(NG - 1, 1, last=True)

        phase1_over(act)
        aln2, aln3, aden = Steps(act, s_aln2, 1), Steps(act, s_aln3, 1), Steps(act, s_aden, 1)

        def turned_sums(b):
            act.wait_ge(s_kvt, b + 1)
            act.activation(h2t[:, b, :], Y_B[b][:, :], ACT.Copy).then_inc(s_kvte, 1)

        def kvp_hi(b, parts):
            for a in parts:
                act.wait_ge(s_mf, HG * b + a + 1)
                act.activation(kvp[0][:, b, a, :], kvp_f[b][a], ACT.Copy).then_inc(s_mhi, 1)

        def den_out(g):
            aden.begin(g)
            act.wait_ge(s_den, g + 1)
            at_least(act, s_rec, g)
            act.activation(den[:, :], D_B[0:HEADS, :], ACT.Copy, bias=DEN_EPS).then_inc(s_dene, 1)
            act.wait_ge(s_dene, g + 1)
            aden.did(act.activation(rec0[:, :], den[:, :], ACT.Ln))
            aden.settle()
            act.activation(rec0[:, :], rec0[:, :], ACT.Exp, scale=-1.0).then_inc(s_rec0, 1)
            aden.end()

        def rec_hi(g):
            act.wait_ge(s_rec, g + 1)
            at_least(act, s_rb, HG * g)
            act.activation(rec_hl[0][:, :], rec[:, :], ACT.Copy).then_inc(s_rechi, 1)

        def on_hi(g, par, j):
            act.wait_ge(s_on, HG * g + j + 1)
            at_least(act, s_y, TPG * (g - 1))
            act.activation(on[par][0][:, j, :], onf[j % 2][:, :], ACT.Copy).then_inc(s_onhi, 1)

        def seed2(g, half):
            h = slice(2 * half, 2 * half + 2)
            aln2.begin(2 * g + half)
            act.wait_ge(s_var2, 2 * g + half + 1)
            aln2.did(act.activation(ln2[:, h], ve2[:, h], ACT.Ln))
            aln2.settle()
            act.activation(y2[:, h], ln2[:, h], ACT.Exp, scale=-0.5).then_inc(s_seed2, 1)
            aln2.end()

        def square(g, t, par):
            act.wait_ge(s_h2, TPG * g + t + 1)
            at_least(act, s_sq, TPG * g + t)
            if t == 0:
                at_least(act, s_var3, g)
            act.activation(sq_out[:, :], rows[par][:, t, 0:C], ACT.Square, accum_out=ss[:, t:t + 1]).then_inc(s_sq, 1)

        def h2t_copy(g, t):
            act.wait_ge(s_h2t, TPG * g + t + 1)
            act.activation(h2t[:, t, :], H2_B[t % 2][:, :], ACT.Copy).then_inc(s_h2te, 1)

        def logits_out(g):
            act.wait_ge(s_lgp, g + 1)
            at_least(act, s_lg, g)
            act.activation(lg_t[:, :], D_B[0:E, :], ACT.Copy).then_inc(s_lgt, 1)

        def rms_seed(g):
            aln3.begin(g)
            act.wait_ge(s_var3, g + 1)
            aln3.did(act.activation(ln3[:, :], ve3[:, :], ACT.Ln))
            aln3.settle()
            act.activation(y3[:, :], ln3[:, :], ACT.Exp, scale=-0.5).then_inc(s_seed3, 1)
            aln3.end()

        def exps(g):
            act.wait_ge(s_dl, g + 1)
            act.activation(ex[:, :, :], dl[:, :, :], ACT.Exp).then_inc(s_ex, 1)

        def group2(g, par):
            before_it = not isinstance(g, int) or g > 0
            if before_it:
                rms_seed(g - 1)
            if has(g, 1):
                rec_hi(g + 1)
            if not before_it:
                kvp_hi(1, range(2, HG))
            if before_it:
                for t in range(TPG):
                    h2t_copy(g - 1, t)
            if has(g, 1):
                on_hi(g + 1, 1 - par, 0)
            seed2(g, 0)
            if has(g, 1):
                on_hi(g + 1, 1 - par, 1)
            if before_it:
                logits_out(g - 1)
            square(g, 0, par)
            square(g, 1, par)
            if has(g, 1):
                on_hi(g + 1, 1 - par, 2)
                on_hi(g + 1, 1 - par, 3)
            if before_it:
                exps(g - 1)
            seed2(g, 1)
            if has(g, 2):
                den_out(g + 2)
            square(g, 2, par)
            square(g, 3, par)

        turned_sums(0)
        kvp_hi(0, range(HG))
        turned_sums(1)
        den_out(0)
        rec_hi(0)
        den_out(1)
        for j in range(HG):
            on_hi(0, 0, j)
        kvp_hi(1, range(2))
        run_groups2(act, group2)
        for t in range(TPG):
            h2t_copy(NG - 1, t)
        rms_seed(NG - 1)
        logits_out(NG - 1)
        exps(NG - 1)

        phase2_over(act)
        act.preload_act_table(ACT.Gelu_apprx_tanh)

        def x_hi(i):
            act.wait_ge(s_xt, i + 1)
            at_least(act, s_u, i)
            act.activation(x_t[0][:, :], XT_B[:, :], ACT.Copy).then_inc(s_xthi, 1)

        def gelu(i):
            act.wait_ge(s_g, i + 1)
            at_least(act, s_h, i)
            act.activation(gact[:, :], G_B[:, :], ACT.Gelu_apprx_tanh).then_inc(s_ga, 1)

        def act_hi(i):
            act.wait_ge(s_ht, i + 1)
            at_least(act, s_o, i)
            act.activation(act_t[0][:, :], HT_B[:, :], ACT.Copy).then_inc(s_hthi, 1)

        def gb_rows(i):
            act.wait_ge(s_cur, 2 * (i + 1))
            act.activation(gb0[:, :], modbc[:, 0, 3, :], ACT.Copy, scale=in_b0[:, 0:1]).then_inc(s_gb0, 1)

        x_hi(0)
        gelu(0)
        x_hi(1)

        def item(i, at):
            gelu(i)
            act_hi(i - 1)
            if not isinstance(i, int) or i < ITEMS - 1:
                x_hi(i + 1)
            gb_rows(i - 1)

        run_items(act, item)
        act_hi(ITEMS - 1)
        gb_rows(ITEMS - 1)

    @block.vector
    def _(dve):
        tt, ts, stt = dve.tensor_tensor, dve.tensor_scalar, dve.scalar_tensor_tensor

        dve.memset(kv[:, :, :, :], 0.0).then_inc(s_kv, NG)
        for i in range(2):
            dve.memset(v_sb[i][:, :, P:], 1.0).then_inc(s_vset, 1)
        setup = Steps(dve, s_vset, 0)
        setup.begin(0)
        setup.n = 2
        dve.wait_ge(s_c, 16)
        dve.wait_ge(s_cexp, 1)
        setup.did(ts(c_exp[:, :], c_exp[:, :], 1.0, None, ALU.add))
        setup.settle()
        setup.did(dve.reciprocal(c_exp[:, :], c_exp[:, :]))
        setup.settle()
        tt(silu_c[:, :], c_sb[:, :], c_exp[:, :], ALU.mult).then_inc(s_silu, 1)

        lns = Steps(dve, s_ln, 2 * TPG + 3)

        def stats1(g):
            lns.begin(g)
            dve.wait_ge(s_x, 16 * (g + 1))
            for t in range(TPG):
                lns.did(dve.bn_stats(st[:, t, :], xg[:, t, :]))
            lns.settle(wait_apart)
            for t in range(TPG):
                lns.did(dve.bn_aggr(mv[:, t, :], st[:, t, :]))
            lns.settle()
            ts(ve[:, :], mv[:, :, 1], LN_EPS, None, ALU.add).then_inc(s_var, 1)
            dve.wait_ge(s_seed, g + 1)
            newton(lns, y0[:, :], ve[:, :], nt1[:, :], nt2[:, :])
            for t in range(TPG):
                ts(xg[:, t, :], xg[:, t, :], mv[:, t, 0:1], nt2[:, t:t + 1], ALU.subtract, ALU.mult).then_inc(s_z, 1)
            lns.end()

        def newton(steps, y, v, a, res):
            steps.did(tt(a, y, y, ALU.mult))
            steps.settle()
            steps.did(stt(a, a, -0.5, v, ALU.mult, ALU.mult))
            steps.settle()
            steps.did(stt(res, a, 1.5, y, ALU.add, ALU.mult))
            steps.settle()

        def h_of(g, t):
            dve.wait_ge(s_T, TPG * g + t + 1)
            at_least(dve, s_hlo, TPG * g + t - 1)
            for f in range(FC):
                at = f * B + batch_of(g)
                last = ts(hf[t % 2][:, f, :], T_B[t % 2][:, f * P:(f + 1) * P], modcol[:, bass.ds(FC * B + at, 1)],
                          modcol[:, bass.ds(at, 1)], ALU.mult, ALU.add)
            last.then_inc(s_hf, 1)

        def low_h(g, t, par):
            dve.wait_ge(s_hhi, TPG * g + t + 1)
            dve.wait_ge(s_hf, TPG * g + t + 1)
            tt(h_t[par][1][:, :, t * P:(t + 1) * P], hf[t % 2][:, :, :], f32(h_t[par][0][:, :, t * P:(t + 1) * P]), ALU.subtract).then_inc(s_hlo, 1)

        def split_lo(turn, half, hi, lo):
            dve.wait_ge(s_hi, 2 * turn + half + 1)
            dve.wait_ge(s_raw[half], 16 * (turn + 1))
            tt(lo, raw[:, half, :], f32(hi), ALU.subtract).then_inc(s_lo, 1)

        def mod_part(m):
            dve.wait_ge(s_modpe, m + 1)
            src = Q_B[m % 2][0:B, :]
            if m in (0, 3):
                dve.tensor_copy(mod_row[:, m, :], src).then_inc(s_modrow, 1)
            elif m in (1, 4):
                ts(mod_row[:, m, :], src, 1.0, None, ALU.add).then_inc(s_modrow, 1)
            else:
                setup.did(ts(mod_tmp[:, :], src, 0.0, 2.0, ALU.is_ge, ALU.mult))
                setup.settle()
                setup.did(ts(mod_tmp[:, :], mod_tmp[:, :], -1.0, None, ALU.add))
                setup.settle()
                setup.did(tt(mod_row[:, m, :], src, mod_tmp[:, :], ALU.mult))
                setup.settle()
                stt(mod_row[:, m, :], mod_row[:, m, :], 0.25, mod_tmp[:, :], ALU.max, ALU.mult).then_inc(s_modrow, 1)

        def low_qkv(f):
            split_lo(f // 2, f % 2, wq[0][:, f * QW:(f + 1) * QW], wq[1][:, f * QW:(f + 1) * QW])

        stats1(0)
        mod_part(0)
        low_qkv(0)
        mod_part(1)
        dve.wait_ge(s_colpe, 1)
        dve.tensor_copy(modcol[:, :], K_B[:, 0:2 * FC * B]).then_inc(s_col, 1)
        dve.wait_ge(s_col, 1)
        h_of(0, 0)
        h_of(0, 1)
        low_h(0, 0, 0)
        low_qkv(1)
        h_of(0, 2)
        low_h(0, 1, 0)
        h_of(0, 3)
        low_h(0, 2, 0)
        low_h(0, 3, 0)
        low_qkv(2)
        low_qkv(3)

        def group1(g, par, last=False):
            if not last:
                stats1(g + 1)
            for t in range(TPG):
                if not last:
                    h_of(g + 1, t)
                    low_h(g + 1, t, 1 - par)
                dve.wait_ge(s_v, TPG * g + t + 1)
                at_least(dve, s_vk, TPG * g + t - 1)
                dve.tensor_copy(v_sb[t % 2][:, :, 0:P], V_B[:, :].rearrange("p (a n) -> p a n", a=HG)).then_inc(s_ve, 1)
            dve.wait_ge(s_vk, TPG * (g + 1))
            dve.wait_ge(s_kv, NG + g)
            for a in range(2):
                b = batch_of(g)
                acc = (kv[:, b, 2 * a:2 * a + 2, 0:P + 1] if isinstance(b, int) else
                       kv[:, bass.ds(b, 1), 2 * a:2 * a + 2, 0:P + 1].rearrange("p b a n -> p (b a) n"))
                last_add = tt(acc, acc, KV_B[a][:, 0:2 * VW].rearrange("p (a n) -> p a n", a=2)[:, :, 0:P + 1], ALU.add)
            last_add.then_inc(s_kv, 1)

        group1(0, 0)
        for m in range(2, 6):
            mod_part(m)
        for g in range(1, 3):
            group1(g, g % 2)
        with dve.Fori(1, (NG - 2) // 2) as j:
            group1(2 * j + 1, 1)
            group1(2 * j + 2, 0)
        group1(NG - 1, 1, last=True)

        phase1_over(dve)
        dve.wait_ge(s_const, 16 * 5)
        dve.wait_ge(s_id, 17)
        in_heads = headmask[:, :].unsqueeze(1).to_broadcast([P, HG, P])
        def keep_sums(b):
            tt(x1[:, b, :].rearrange("p (a n) -> p a n", a=HG), kv[:, b, :, 0:P], in_heads, ALU.mult).then_inc(s_kvm, 1)
            tt(ksums[:, b, :, :], inhead[:, :, :], kv[:, b, :, P:P + 1].to_broadcast([P, HG, HEADS]), ALU.mult).then_inc(s_prep, 1)

        def ksum_of(g):
            at_least(dve, s_den, g)
            if isinstance(g, int) and g == 0:
                dve.wait_ge(s_prep, 1)
            if isinstance(g, int) and g == 1:
                dve.wait_ge(s_prep, 3)
            b = batch_of(g)
            dve.tensor_copy(ksum_now[:, :, :], ksums[:, b, :, :] if isinstance(b, int) else
                            ksums[:, bass.ds(b, 1), :, :].rearrange("p a f h -> p (a f) h")).then_inc(s_ksum, 1)

        rst = Steps(dve, s_recstep, 1)

        def recip(g):
            rst.begin(g)
            dve.wait_ge(s_rec0, g + 1)
            at_least(dve, s_reclo, g)
            rst.did(stt(den[:, :], den[:, :], -1.0, rec0[:, :], ALU.mult, ALU.mult))
            rst.settle()
            stt(rec[:, :], den[:, :], 2.0, rec0[:, :], ALU.add, ALU.mult).then_inc(s_rec, 1)
            rst.end()

        def rec_lo(g):
            dve.wait_ge(s_rechi, g + 1)
            tt(rec_hl[1][:, :], rec[:, :], f32(rec_hl[0][:, :]), ALU.subtract).then_inc(s_reclo, 1)

        def divide(g, par, j):
            dve.wait_ge(s_rb, HG * g + j + 1)
            at_least(dve, s_onlo, HG * g + j - 1)
            tt(onf[j % 2][:, :], RB_B[j % 2][:, :], qb[par][:, j, :], ALU.mult).then_inc(s_on, 1)

        def kvp_of(b, a):
            dve.wait_ge(s_mp, HG * b + a + 1)
            tt(kvp_f[b][a], M_B[b][a][:, :], modbc[:, b, 0, :], ALU.mult).then_inc(s_mf, 1)

        def kvp_lo(b):
            for a in range(HG):
                dve.wait_ge(s_mhi, HG * b + a + 1)
                tt(kvp[1][:, b, a, :], kvp_f[b][a], f32(kvp[0][:, b, a, :]), ALU.subtract).then_inc(s_mlo, 1)

        NORM_STEPS, ROUTE_STEPS = 3 * TPG + 2 * 3, 20
        turn = Steps(dve, s_step2, NORM_STEPS + ROUTE_STEPS)

        def per_row(ap):
            return ap.unsqueeze(2).to_broadcast([P, TPG, E])

        def per_expert(ap):
            return ap.unsqueeze(1).to_broadcast([P, TPG, E])

        def residual(g, t, par):
            dve.wait_ge(s_y, TPG * g + t + 1)
            dve.wait_ge(s_xb, TPG * g + t + 1)
            if t == 0:
                at_least(dve, s_x1st, 16 * g)
            tt(x1[:, t, :], Y_B[t % 2][:, :], xb[par][:, t, :], ALU.add).then_inc(s_x1, 1)

        def sums(g, t):
            dve.wait_ge(s_x1, TPG * g + t + 1)
            turn.did(dve.bn_stats(st2[:, t, :], x1[:, t, :]), f"sums{t}")

        def moments(t):
            turn.after(f"sums{t}", wait_apart)
            turn.did(dve.bn_aggr(mv2[:, t, :], st2[:, t, :]), f"moments{t}")

        def halves(half):
            return slice(2 * half, 2 * half + 2)

        def var2(half):
            h = halves(half)
            turn.after(f"moments{2 * half + 1}")
            ts(ve2[:, h], mv2[:, h, 1], LN_EPS, None, ALU.add).then_inc(s_var2, 1)

        def seed_squared(g, half):
            h = halves(half)
            dve.wait_ge(s_seed2, 2 * g + half + 1)
            turn.did(tt(na2[:, h], y2[:, h], y2[:, h], ALU.mult), f"yy{half}")

        def seed_error(half):
            h = halves(half)
            turn.after(f"yy{half}")
            turn.did(stt(na2[:, h], na2[:, h], -0.5, ve2[:, h], ALU.mult, ALU.mult), f"vyy{half}")

        def rstd2_of(half):
            h = halves(half)
            turn.after(f"vyy{half}")
            turn.did(stt(rstd2[:, h], na2[:, h], 1.5, y2[:, h], ALU.add, ALU.mult), f"rstd{half}")

        def mod_row_of(g, k):
            b = batch_of(g)
            return modbc[:, b, k, :] if isinstance(b, int) else modbc[:, bass.ds(b, 1), k, :].rearrange("p a n -> p (a n)")

        def centred(g, t):
            at_least(dve, s_h2, TPG * g + t - 1)
            if t % 2 == 0:
                turn.after(f"moments{t + 1}")
            turn.did(stt(lnt[t % 2][:, :], x1[:, t, :], mv2[:, t, 0:1], mod_row_of(g, 2), ALU.subtract, ALU.mult), f"centred{t}")

        def normed(g, t, par):
            at_least(dve, s_scat[t], SCAT * (g - 1))
            turn.after(f"centred{t}")
            if t % 2 == 0:
                turn.after(f"rstd{t // 2}")
            stt(rows[par][:, t, 0:C], lnt[t % 2][:, :], rstd2[:, t:t + 1], mod_row_of(g, 1), ALU.mult, ALU.add).then_inc(s_h2, 1)

        def rms_var(g):
            dve.wait_ge(s_sq, TPG * (g + 1))
            ts(ve3[:, :], ss[:, :], 1.0 / C, RMS_EPS, ALU.mult, ALU.add).then_inc(s_var3, 1)

        def rms_seed_squared(g):
            dve.wait_ge(s_seed3, g + 1)
            turn.did(tt(na3[:, :], y3[:, :], y3[:, :], ALU.mult), "yy_rms")

        def rms_seed_error():
            turn.after("yy_rms")
            turn.did(stt(na3[:, :], na3[:, :], -0.5, ve3[:, :], ALU.mult, ALU.mult), "vyy_rms")

        def rms():
            turn.after("vyy_rms")
            turn.did(stt(rs3[:, :], na3[:, :], 1.5, y3[:, :], ALU.add, ALU.mult), "rms")

        def logits(g):
            dve.wait_ge(s_lg, g + 1)
            turn.after("rms")
            turn.did(stt(lg[:, :, :], R_B[:, 0:TPG * E].rearrange("p (t e) -> p t e", e=E), float(np.float32(C) ** np.float32(-0.5)),
                       per_row(rs3[:, :]), ALU.mult, ALU.mult), "logits")

        def largest():
            turn.after("logits", wait_apart)
            for t in range(TPG):
                last = dve.max(mx[:, t, :], lg[:, t, :])
            turn.did(last, "largest")

        def less_max():
            turn.after("largest")
            tt(dl[:, :, :], lg[:, :, :], mx[:, :, 0:1].to_broadcast([P, TPG, E]), ALU.subtract).then_inc(s_dl, 1)

        def where_largest():
            for t in range(TPG):
                last = dve.max_index(ix[:, t, :], mx[:, t, :], lg[:, t, :])
            turn.did(last, "where")

        def chosen_two():
            turn.after("where")
            turn.did(dve.tensor_copy(ixf[:, :, :], ix[:, :, 0:2].rearrange("p t k -> p k t")), "two")

        def one_hot():
            turn.after("two")
            turn.did(tt(oh[:, :, :, :], iota_e[:, :].unsqueeze(1).unsqueeze(1).to_broadcast([P, 2, TPG, E]),
                      ixf[:, :, :].unsqueeze(3).to_broadcast([P, 2, TPG, E]), ALU.is_equal), "one_hot")

        def mask():
            turn.after("one_hot")
            tt(mkb[:, :, :], oh[:, 0, :, :], oh[:, 1, :, :], ALU.add).then_inc(s_mk, 1)

        def exp_sum(g):
            dve.wait_ge(s_ex, g + 1)
            turn.did(dve.tensor_reduce(se[:, :], ex[:, :, :], AX.X, ALU.add), "exp_sum")

        def exp_chosen(g):
            dve.wait_ge(s_mk, g + 1)
            turn.did(tt(em[:, :, :], ex[:, :, :], mkb[:, :, :], ALU.mult), "exp_chosen")

        def exp_sum_recip():
            turn.after("exp_sum")
            turn.did(dve.reciprocal(rse[:, :], se[:, :]), "exp_sum_recip")

        def probs():
            turn.after("exp_sum_recip")
            turn.did(tt(ip[:, :, :], em[:, :, :], per_row(rse[:, :]), ALU.mult), "probs")

        def renorm():
            turn.after("probs")
            turn.did(dve.tensor_reduce(rn[:, :], ip[:, :, :], AX.X, ALU.add), "renorm")

        def scaled():
            turn.did(tt(wts[:, :, :], ip[:, :, :], per_expert(pes_bc[:, :]), ALU.mult), "scaled")

        def renorm_guard():
            turn.after("renorm")
            turn.did(stt(rng[:, :], rn[:, :], 0.0, rn[:, :], ALU.is_le, ALU.add), "guarded")

        def renorm_recip():
            turn.after("guarded")
            turn.did(dve.reciprocal(rrn[:, :], rng[:, :]), "renorm_recip")

        def weights(par):
            turn.after("renorm_recip")
            turn.did(tt(rows[par][:, :, W_AT:W_AT + E], wts[:, :, :], per_row(rrn[:, :]), ALU.mult), "weights")

        def places(g):
            dve.wait_ge(s_rank, g + 1)
            turn.did(tt(pos[:, :, :], R_B[:, TPG * E:2 * TPG * E].rearrange("p (t e) -> p t e", e=E), per_expert(next_row[:, :]), ALU.add), "places")

        def next_places():
            turn.after("places")
            tt(next_row[:, :], next_row[:, :], R_B[:, 2 * TPG * E:2 * TPG * E + E], ALU.add).then_inc(s_ranku, 1)

        def places_chosen():
            turn.after("places")
            turn.did(tt(chosen[:, :, :, :], pos[:, :, :].unsqueeze(1).to_broadcast([P, 2, TPG, E]), oh[:, :, :, :], ALU.mult), "chosen")

        def two_places():
            turn.after("chosen")
            turn.did(dve.tensor_reduce(destf[:, :, :], chosen[:, :, :, :], AX.X, ALU.add), "two_places")

        def destinations(par):
            turn.after("two_places")
            dve.tensor_copy(dest[par][:, :, :], destf[:, :, :]).then_inc(s_dest, 1)

        def group2(g, par):
            router = not isinstance(g, int) or g > 0
            last = not has(g, 1)
            turn.begin(g, ROUTE_STEPS if router else 0)
            if router:
                rms_var(g - 1)
            if not last:
                rec_lo(g + 1)
            if has(g, 2):
                ksum_of(g + 2)
            residual(g, 0, par)
            if router:
                rms_seed_squared(g - 1)
            sums(g, 0)
            if router:
                rms_seed_error()
            else:
                kvp_of(1, 2)
                kvp_of(1, 3)
            residual(g, 1, par)
            moments(0)
            sums(g, 1)
            if router:
                rms()
            if not last:
                divide(g + 1, 1 - par, 0)
            moments(1)
            if not last:
                divide(g + 1, 1 - par, 1)
            var2(0)
            centred(g, 0)
            seed_squared(g, 0)
            centred(g, 1)
            seed_error(0)
            residual(g, 2, par)
            rstd2_of(0)
            sums(g, 2)
            normed(g, 0, par)
            moments(2)
            normed(g, 1, par)
            if router:
                logits(g - 1)
            if not last:
                divide(g + 1, 1 - par, 2)
            if router:
                largest()
            if not last:
                divide(g + 1, 1 - par, 3)
            if router:
                less_max()
                where_largest()
                chosen_two()
                one_hot()
                mask()
            residual(g, 3, par)
            if router and not last:
                exp_sum(g - 1)
            sums(g, 3)
            if router and not last:
                exp_chosen(g - 1)
                exp_sum_recip()
            moments(3)
            if router and not last:
                probs()
            var2(1)
            centred(g, 2)
            if router:
                places(g - 1)
            seed_squared(g, 1)
            if router and not last:
                renorm()
            centred(g, 3)
            seed_error(1)
            if router:
                places_chosen()
            if router and not last:
                renorm_guard()
                scaled()
            rstd2_of(1)
            if router:
                two_places()
            if router and not last:
                renorm_recip()
            if router:
                next_places()
            if router and not last:
                weights(1 - par)
                destinations(1 - par)
            normed(g, 2, par)
            normed(g, 3, par)
            if not router:
                kvp_lo(1)
            if router and last:
                exp_sum(g - 1)
                exp_chosen(g - 1)
                finish_weights()
                weights(1 - par)
                destinations(1 - par)
            if has(g, 2):
                recip(g + 2)
            turn.end(0 if router else ROUTE_STEPS)

        def finish_weights():
            exp_sum_recip()
            probs()
            renorm()
            scaled()
            renorm_guard()
            renorm_recip()

        dve.wait_ge(s_free, 2)
        keep_sums(0)
        ksum_of(0)
        keep_sums(1)
        tt(rw[:, :, :], rw[:, :, :], rscale[:, :].unsqueeze(2).to_broadcast([P, FC, E]), ALU.mult).then_inc(s_prep, 1)
        for a in range(HG):
            kvp_of(0, a)
        kvp_lo(0)
        ksum_of(1)
        recip(0)
        rec_lo(0)
        for j in range(HG):
            divide(0, 0, j)
        recip(1)
        kvp_of(1, 0)
        kvp_of(1, 1)
        run_groups2(dve, group2)
        turn.begin(NG, ROUTE_STEPS)
        rms_var(NG - 1)
        rms_seed_squared(NG - 1)
        rms_seed_error()
        rms()
        logits(NG - 1)
        largest()
        less_max()
        where_largest()
        chosen_two()
        one_hot()
        mask()
        exp_sum(NG - 1)
        exp_chosen(NG - 1)
        finish_weights()
        weights(1)
        places(NG - 1)
        next_places()
        places_chosen()
        two_places()
        destinations(1)
        turn.end(NORM_STEPS)

        its = Steps(dve, s_it, ITEM_STEPS)
        its.begin(0)

        def step(ins):
            its.did(ins)
            its.settle()

        dve.wait_ge(s_ranku, NG)
        dve.wait_ge(s_padi, 2)
        ts(pad_to[:, :], next_row[:, :], lane[:, 0:1], None, ALU.add).then_inc(s_padi, 1)
        step(tt(cnt[:, :], next_row[:, :], list_at[:, :], ALU.subtract))
        step(ts(cnti[:, :], cnt[:, :], 1.0, float(P - 1), ALU.max, ALU.add))
        step(ts(ntli[:, :], cnti[:, :], P.bit_length() - 1, None, ALU.arith_shift_right))
        step(dve.tensor_copy(ntl[:, :], ntli[:, :]))
        step(dve.tensor_copy(cend[:, :], ntl[:, :]))
        for e in range(1, E):
            step(tt(cend[:, e:e + 1], cend[:, e - 1:e], ntl[:, e:e + 1], ALU.add))
        lies = [h2t[:, 0:2, :].rearrange("p a n -> p (a n)")[:, 0:ITEMS * (E - 1)].rearrange("p (i e) -> p i e", e=E - 1),
                h2t[:, 2:4, :].rearrange("p a n -> p (a n)")[:, 0:ITEMS * (E - 1)].rearrange("p (i e) -> p i e", e=E - 1)]

        def all_experts(ap):
            return ap[:, 0:E - 1].unsqueeze(1).to_broadcast([P, ITEMS, E - 1])

        step(tt(lies[0], item_no[:, :].unsqueeze(2).to_broadcast([P, ITEMS, E - 1]), all_experts(cend[:, :]), ALU.is_ge))
        its.did(dve.tensor_reduce(it_e[:, :], lies[0], AX.X, ALU.add))
        step(tt(lies[1], lies[0], all_experts(ntl[:, :]), ALU.mult))
        step(dve.tensor_reduce(it_t[:, :], lies[1], AX.X, ALU.add))
        step(tt(it_k[:, :], item_no[:, :], it_t[:, :], ALU.subtract))
        step(ts(it_r[:, :], it_e[:, :], float(CAP), -float(E * CAP), ALU.mult, ALU.add))
        step(stt(it_r[:, :], it_k[:, :], float(P), it_r[:, :], ALU.mult, ALU.add))
        step(stt(it_r[:, :], item_no[:, :], cend[:, E - 1:E], it_r[:, :], ALU.is_lt, ALU.mult))
        step(ts(tables[:, 0, :], it_r[:, :], float(E * CAP), None, ALU.add))
        its.did(dve.tensor_copy(tables[:, 1, :], it_e[:, :]))
        its.did(dve.tensor_copy(tables[:, 2, :], it_k[:, :]))
        its.end()

        phase2_over(dve)

        def x_lo(i):
            dve.wait_ge(s_xthi, i + 1)
            at_least(dve, s_u, i)
            tt(x_t[1][:, :], XT_B[:, :], f32(x_t[0][:, :]), ALU.subtract).then_inc(s_xtlo, 1)

        def keep_meta(i, at):
            dve.wait_ge(s_xr[at], 16 * ((i // RING if isinstance(i, int) else i >> 2) + 1))
            dve.tensor_copy(meta[at][:, :], xrow[at][:, W_AT:W_AT + META]).then_inc(s_meta, 1)

        def glu(i):
            dve.wait_ge(s_u, i + 1)
            dve.wait_ge(s_ga, i + 1)
            at_least(dve, s_ht, i)
            tt(hact[:, :], U_B[:, :], gact[:, :], ALU.mult).then_inc(s_h, 1)

        def act_lo(i):
            dve.wait_ge(s_hthi, i + 1)
            tt(act_t[1][:, :], HT_B[:, :], f32(act_t[0][:, :]), ALU.subtract).then_inc(s_htlo, 1)

        gbs = Steps(dve, s_gbr, 3)

        def out_rows(i, at):
            gbs.begin(i)
            e = dve.value_load(tables[0:1, 1, bass.ds(i, 1)], min_val=0, max_val=E - 1)
            at_least(dve, s_or, i)
            at_least(dve, s_add, 16 * (i - 1))
            dve.wait_ge(s_meta, i + 1)
            gbs.did(dve.tensor_copy(cur_w[:, :], meta[at][:, bass.ds(e, 1)]))
            gbs.did(dve.tensor_copy(cur_tok[at % 2][:, :], meta[at][:, E:E + 1].bitcast(U32)))
            gbs.settle()
            ts(in_b0[:, :], cur_tok[at % 2][:, :], float(S), None, ALU.is_lt).then_inc(s_cur, 1)
            ts(in_b1[:, :], cur_tok[at % 2][:, :], float(S), None, ALU.is_ge).then_inc(s_cur, 1)
            dve.wait_ge(s_cur, 2 * (i + 1))
            dve.wait_ge(s_gb0, i + 1)
            gbs.did(stt(gbr[:, :], modbc[:, 1, 3, :], in_b1[:, 0:1], gb0[:, :], ALU.mult, ALU.add))
            dve.wait_ge(s_o, i + 1)
            gbs.settle()
            stt(orow[at % 2][:, :], O_B[:, :], cur_w[:, 0:1], gbr[:, :], ALU.mult, ALU.mult).then_inc(s_or, 1)
            gbs.end()

        keep_meta(0, 0)
        x_lo(0)
        glu(0)
        keep_meta(1, 1)
        x_lo(1)

        def item(i, at):
            act_lo(i - 1)
            glu(i)
            if not isinstance(i, int) or i < ITEMS - 1:
                keep_meta(i + 1, (at + 1) % RING)
                x_lo(i + 1)
            out_rows(i - 1, (at - 1) % RING)

        run_items(dve, item)
        act_lo(ITEMS - 1)
        out_rows(ITEMS - 1, (ITEMS - 1) % RING)

    @block.tensor
    def _(pe):
        mm = pe.matmul

        pe.wait_ge(s_silu, 1)
        def mod_part(m):
            pe.wait_ge(s_mod[m], 16)
            at_least(pe, s_modrow, m - 1)
            for f in range(FC):
                last = mm(Q_B[m % 2][0:B, :], silu_c[:, f * B:(f + 1) * B], mod_stage[m][:, f, :], start=(f == 0), stop=(f == FC - 1))
            last.then_inc(s_modpe, 1)

        def turn(g, t):
            pe.wait_ge(s_z, TPG * g + t + 1)
            at_least(pe, s_hf, TPG * g + t - 1)
            for f in range(FC):
                last = pe.transpose(T_B[t % 2][:, f * P:(f + 1) * P], xg[:, t, f * P:(f + 1) * P], ident[:, :])
            last.then_inc(s_T, 1)

        mod_part(0)
        pe.wait_ge(s_id, 6)
        turn(0, 0)
        turn(0, 1)
        mod_part(1)
        pe.wait_ge(s_modrow, 2)
        for r in range(2 * FC):
            last = pe.transpose(K_B[:, r * B:(r + 1) * B], mod_row[:, r // FC, r % FC * P:(r % FC + 1) * P], ident[0:B, 0:B])
        last.then_inc(s_colpe, 1)
        turn(0, 2)
        turn(0, 3)

        def product(dst, parts, n, stationary, moving):
            k = 0
            for f in range(n):
                for a, b in PASSES[:parts]:
                    last = mm(dst, stationary(a, f), moving(b, f), start=(k == 0), stop=(k == parts * n - 1))
                    k += 1
            return last

        def kv_sums(g, t):
            pe.wait_ge(s_ke, TPG * g + t + 1)
            pe.wait_ge(s_ve, TPG * g + t + 1)
            if t == 0:
                pe.wait_ge(s_kv, NG + g)
            for a in range(HG):
                last = mm(KV_B[a // 2][:, a % 2 * VW:a % 2 * VW + P + 1], k_sb[t % 2][:, a * P:(a + 1) * P], v_sb[t % 2][:, a, 0:P + 1],
                          start=(t == 0 and a % 2 == 0), stop=(t == TPG - 1), skip_group_check=True)
            last.then_inc(s_vk, 1)

        def group1(g, par, last=False):
            pe.wait_ge(s_hlo, TPG * (g + 1))
            for j in range(FC):
                at_least(pe, s_qe, FC * g + j - 1)
                product(Q_B[j % 2][:, :], 3, FC, lambda a, f: wq[a][:, f * C + j * P:f * C + (j + 1) * P],
                        lambda b, f: h_t[par][b][:, f, :]).then_inc(s_q, 1)
            if isinstance(g, int) and g == 0:
                pe.wait_ge(s_lo, FC)
            for t in range(TPG):
                if not last:
                    turn(g + 1, t)
                at_least(pe, s_ke, TPG * g + t)
                product(K_B[:, :], 3, FC, lambda a, f: h_t[par][a][:, f, t * P:(t + 1) * P],
                        lambda b, f: wq[b][:, (FC + f) * C:(FC + f + 1) * C]).then_inc(s_k, 1)
                at_least(pe, s_ve, TPG * g + t)
                product(V_B[:, :], 3, FC, lambda a, f: h_t[par][a][:, f, t * P:(t + 1) * P],
                        lambda b, f: wq[b][:, (2 * FC + f) * C:(2 * FC + f + 1) * C]).then_inc(s_v, 1)
                if t:
                    kv_sums(g, t - 1)
            kv_sums(g, TPG - 1)

        pe.wait_ge(s_lo, 2)
        pe.wait_ge(s_modrow, 2)
        group1(0, 0)
        pe.wait_ge(s_qe, FC)
        for m in range(2, 6):
            mod_part(m)
        pe.wait_ge(s_modrow, 6)
        for g in range(1, 3):
            group1(g, g % 2)
        with pe.Fori(1, (NG - 2) // 2) as j:
            group1(2 * j + 1, 1)
            group1(2 * j + 2, 0)
        group1(NG - 1, 1, last=True)

        phase1_over(pe)

        def denominators(g, par):
            pe.wait_ge(s_q2, 16 * (g + 1))
            pe.wait_ge(s_ksum, g + 1)
            at_least(pe, s_dene, g)
            at_least(pe, s_lgt, g - 2)
            for f in range(FC):
                last = mm(D_B[0:HEADS, :], ksum_now[:, f, :], qb[par][:, f, :], start=(f == 0), stop=(f == FC - 1))
            last.then_inc(s_den, 1)

        def spread(g, j):
            pe.wait_ge(s_reclo, g + 1)
            if isinstance(g, int) and g == 0:
                pe.wait_ge(s_sel, 4)
                pe.wait_ge(s_mf, HG)
            at_least(pe, s_on, HG * g + j - 1)
            for k in range(2):
                last = mm(RB_B[j % 2][:, :], sel[:, j * P:(j + 1) * P], rec_hl[k][:, :], start=(k == 0), stop=(k == 1))
            last.then_inc(s_rb, 1)

        def turn_sums(b):
            pe.wait_ge(s_kvm, b + 1)
            for a in range(HG):
                last = pe.transpose(Y_B[b][:, a * P:(a + 1) * P], x1[:, b, a * P:(a + 1) * P], ident[:, :])
            last.then_inc(s_kvt, 1)

        def project_sums(b, a):
            pe.wait_ge(s_kvte, b + 1)
            if b:
                pe.wait_ge(s_mf, HG * b + max(a - 1, 0))
            mm(M_B[b][a][:, :], h2t[:, b, a * P:(a + 1) * P], wproj_f[:, a, :], start=True, stop=True).then_inc(s_mp, 1)

        turn_sums(0)
        for a in range(HG):
            project_sums(0, a)
        denominators(0, 0)
        turn_sums(1)
        denominators(1, 1)
        for j in range(HG):
            spread(0, j)
        project_sums(1, 0)
        project_sums(1, 1)

        def rank(g):
            pe.wait_ge(s_mk, g + 1)
            for t in range(TPG):
                dst = R_B[:, (TPG + t) * E:(TPG + t + 1) * E]
                for s in range(t):
                    mm(dst, ones[:, :], mkb[:, s, :], start=(s == 0), stop=False)
                mm(dst, before[:, :], mkb[:, t, :], start=(t == 0), stop=True)
            for t in range(TPG):
                last = mm(R_B[:, 2 * TPG * E:2 * TPG * E + E], ones[:, :], mkb[:, t, :], start=(t == 0), stop=(t == TPG - 1))
            last.then_inc(s_rank, 1)

        def project(g, par, t):
            b = batch_of(g)
            if t == 0:
                pe.wait_ge(s_onlo, HG * (g + 1))
            at_least(pe, s_x1, TPG * g + t - 1)
            product(Y_B[t % 2][:, :], 3, FC, lambda a, f: on[par][a][:, f, t * P:(t + 1) * P],
                    lambda k, f: kvp[k][:, b, f, :] if isinstance(b, int) else
                    kvp[k][:, bass.ds(b, 1), f, :].rearrange("p a n -> p (a n)")).then_inc(s_y, 1)

        def turn_h2(g, par, t):
            pe.wait_ge(s_h2, TPG * g + t + 1)
            at_least(pe, s_h2te, TPG * g + t - 1)
            for f in range(FC):
                last = pe.transpose(H2_B[t % 2][:, f * P:(f + 1) * P], rows[par][:, t, f * P:(f + 1) * P], ident[:, :])
            last.then_inc(s_h2t, 1)

        def logits(g):
            pe.wait_ge(s_h2te, TPG * (g + 1))
            pe.wait_ge(s_dene, min(g + 3, NG) if isinstance(g, int) else g + 3)
            for f in range(FC):
                last = mm(D_B[0:E, :], rw[:, f, :], h2t[:, :, f * P:(f + 1) * P], start=(f == 0), stop=(f == FC - 1))
            last.then_inc(s_lgp, 1)

        def turn_logits(g):
            pe.wait_ge(s_lgt, g + 1)
            wait_apart(pe, s_ranku, g)
            for t in range(TPG):
                last = pe.transpose(R_B[:, t * E:(t + 1) * E], lg_t[:, t * P:(t + 1) * P], ident[0:E, 0:E])
            last.then_inc(s_lg, 1)

        def group2(g, par):
            before_it = not isinstance(g, int) or g > 0
            project(g, par, 0)
            if not before_it:
                project_sums(1, 2)
                project_sums(1, 3)
            if before_it:
                turn_h2(g - 1, 1 - par, 0)
                turn_h2(g - 1, 1 - par, 1)
            project(g, par, 1)
            if has(g, 1):
                spread(g + 1, 0)
                spread(g + 1, 1)
            if before_it:
                turn_h2(g - 1, 1 - par, 2)
                turn_h2(g - 1, 1 - par, 3)
            project(g, par, 2)
            if before_it:
                logits(g - 1)
            if has(g, 1):
                spread(g + 1, 2)
                spread(g + 1, 3)
            if before_it:
                turn_logits(g - 1)
            project(g, par, 3)
            if before_it:
                rank(g - 1)
            if has(g, 2):
                denominators(g + 2, par)

        run_groups2(pe, group2)
        for t in range(TPG):
            turn_h2(NG - 1, 1, t)
        logits(NG - 1)
        turn_logits(NG - 1)
        rank(NG - 1)

        phase2_over(pe)

        def expert_of(i):
            return pe.value_load(tables[0:1, 1, bass.ds(i, 1)], min_val=0, max_val=E - 1)

        def weights(e, at):
            base = pe.snap((e & 1) * (2 * EW), min_val=0, max_val=2 * EW)
            return lambda k, f: wbuf[:, bass.ds(base + (at(f) // QW * 2 * QW + k * QW + at(f) % QW), 512)]

        def turn_rows(i, at):
            pe.wait_ge(s_xr[at], 16 * ((i // RING if isinstance(i, int) else i >> 2) + 1))
            at_least(pe, s_xtlo, i)
            for f in range(FC):
                last = pe.transpose(XT_B[:, f * P:(f + 1) * P], xrow[at][:, f * P:(f + 1) * P], ident[:, :])
            last.then_inc(s_xt, 1)

        def gate(i, e):
            pe.wait_ge(s_xtlo, i + 1)
            pe.wait_ge(s_w, 16 * QPE * (e + 1))
            at_least(pe, s_ga, i)
            product(G_B[:, :], 3, FC, lambda a, f: x_t[a][:, f * P:(f + 1) * P], weights(e, lambda f: f * 2 * H)).then_inc(s_g, 1)

        def up(i, e):
            at_least(pe, s_h, i)
            product(U_B[:, :], 3, FC, lambda a, f: x_t[a][:, f * P:(f + 1) * P], weights(e, lambda f: f * 2 * H + H)).then_inc(s_u, 1)

        def turn_act(i):
            pe.wait_ge(s_h, i + 1)
            at_least(pe, s_htlo, i)
            for f in range(H // P):
                last = pe.transpose(HT_B[:, f * P:(f + 1) * P], hact[:, f * P:(f + 1) * P], ident[:, :])
            last.then_inc(s_ht, 1)

        def down(i, e):
            pe.wait_ge(s_htlo, i + 1)
            at_least(pe, s_or, i)
            product(O_B[:, :], 3, H // P, lambda a, f: act_t[a][:, f * P:(f + 1) * P], weights(e, lambda f: DOWN + f * C)).then_inc(s_o, 1)

        turn_rows(0, 0)
        e = expert_of(0)
        gate(0, e)
        up(0, e)
        turn_rows(1, 1)

        def item(i, at):
            e, e_before = expert_of(i), expert_of(i - 1)
            gate(i, e)
            turn_act(i - 1)
            up(i, e)
            if not isinstance(i, int) or i < ITEMS - 1:
                turn_rows(i + 1, (at + 1) % RING)
            down(i - 1, e_before)

        run_items(pe, item)
        turn_act(ITEMS - 1)
        down(ITEMS - 1, expert_of(ITEMS - 1))

    ph3.close()
    keep.close()




def laid_out(i):
    def chunks(a):
        return np.ascontiguousarray(a.reshape(-1, P, a.shape[1]).transpose(1, 0, 2).reshape(P, -1))

    gate = i["L0_ffn_gating_einsum"].transpose(0, 3, 1, 2).reshape(E, C, 2 * H)
    experts = np.stack([np.concatenate([chunks(gate[e]), chunks(i["L0_ffn_linear"][e])], axis=1) for e in range(E)])
    experts = np.ascontiguousarray(experts.reshape(E, P, QPE, QW).transpose(0, 2, 1, 3).reshape(E * QPE * P, QW))
    return {
        "x": np.ascontiguousarray(i["L0_attn_x"].reshape(NT, C)),
        "c_t": chunks(i["L0_c"].T),
        "wmod": np.ascontiguousarray(i["L0_wmod"]),
        "wqkv": np.concatenate([chunks(w.T) for w in np.split(i["L0_attn_w_qkv"], 3)], axis=1),
        "wproj": chunks(i["L0_attn_w_proj"].T),
        "b_proj": np.ascontiguousarray(i["L0_attn_b_proj"]),
        "r_w": chunks(i["L0_ffn_router_logits"]),
        "r_scale": chunks(i["L0_ffn_router_scale"].reshape(C, 1)),
        "pes": np.ascontiguousarray(i["L0_ffn_per_expert_scale"]),
        "moe_w": experts,
    }


def kernel(**inputs):
    from concourse import bacc
    from concourse.bass_utils import run_bass_kernel_spmd

    nc = bacc.Bacc("TRN2", target_bir_lowering=False, num_devices=1)
    arrays = laid_out({k: np.asarray(v) for k, v in inputs.items()})
    aps = {n: nc.dram_tensor(f"in_{n}", a.shape, F32, kind="ExternalInput").ap() for n, a in arrays.items()}
    out = nc.dram_tensor("out_rows", (NT + P, C), F32, kind="ExternalOutput").ap()
    build(nc, out=out, **aps)
    got = run_bass_kernel_spmd(nc, [{f"in_{n}": a for n, a in arrays.items()}], core_ids=[0])
    return got.results[0]["out_rows"][:NT].reshape(B, S, C)
```

```python
from contextlib import ExitStack

import numpy as np

import concourse.bass as bass
from concourse import mybir

F32 = mybir.dt.float32
F32R = mybir.dt.float32r
BF16 = mybir.dt.bfloat16
I32 = mybir.dt.int32
U32 = mybir.dt.uint32
ALU = mybir.AluOpType
ACT = mybir.ActivationFunctionType
AX = mybir.AxisListType

P = 128
B, S, C = 2, 4096, 512
E, H = 8, 512
HEAD = 32
NT = B * S
FC = C // P
GT = 512
TPG = GT // P
NG = NT // GT
GPB = NG // B
HG = C // P
HEADS = C // HEAD
LN_EPS = 1e-5
DEN_EPS = 1e-15
RMS_EPS = 1e-6
EW = FC * 2 * H + (H // P) * C
DOWN = FC * 2 * H
QW = 1536
QPE = EW // QW
KQW = 2 * FC * C // 4
CAP = NT + P
ROW = 528
W_AT, TOK_AT = C, C + E
META = 12
ITEMS = (2 * NT + E * (P - 1)) // P
RING = 4
EARLY = 3
SCAT = 16 * 2

PASSES = ((0, 0), (0, 1), (1, 0))


def at_least(eng, sem, value):
    if isinstance(value, int) and value <= 0:
        return
    eng.wait_ge(sem, value)


class Steps:

    def __init__(self, eng, sem, each):
        self.eng, self.sem, self.each = eng, sem, each

    def begin(self, turn, missing=0):
        self.base, self.n, self.at = turn * self.each - missing, 0, {}

    def did(self, ins, name=None):
        self.n += 1
        self.at[name] = self.n
        ins.then_inc(self.sem, 1)

    def after(self, name, wait=at_least):
        wait(self.eng, self.sem, self.base + self.at[name])

    def settle(self, wait=at_least):
        wait(self.eng, self.sem, self.base + self.n)

    def end(self, missing=0):
        assert self.n == self.each - missing, (self.n, self.each)


def build(nc, x, c_t, wmod, wqkv, wproj, b_proj, r_w, r_scale, pes, moe_w, out):
    qd = nc.dram_tensor("q_rows", (NG * P, FC * GT), F32, kind="Internal").ap()
    wd = nc.dram_tensor("expert_split", (E * QPE * P, 2 * QW), F32, kind="Internal").ap()
    mod_d = nc.dram_tensor("mod_rows", (B, 4 * C), F32, kind="Internal").ap()
    xs = nc.dram_tensor("expert_rows", (E * CAP + P, ROW), F32, kind="Internal").ap()

    keep, ph1, ph2, ph3 = ExitStack(), ExitStack(), ExitStack(), ExitStack()

    def sb(stack, name, shape, dt, side=None):
        return stack.enter_context(nc.sbuf_tensor(name, shape, dt, side=side) if side else nc.sbuf_tensor(name, shape, dt))

    def sem(name):
        return keep.enter_context(nc.semaphore(name))

    bank = [keep.enter_context(nc.psum_tensor(f"bank{i}", [P, 512], F32)) for i in range(8)]

    ident = sb(keep, "ident", [P, P], F32)
    before = sb(keep, "before", [P, P], BF16)
    ones = sb(keep, "ones", [P, P], BF16)
    headmask = sb(keep, "headmask", [P, P], F32)
    inhead = sb(keep, "inhead", [P, FC, HEADS], F32)
    iota_e = sb(keep, "iota_e", [P, E], F32)
    list_at = sb(keep, "list_at", [P, E], F32)
    lane = sb(keep, "lane", [P, 1], F32)
    item_no = sb(keep, "item_no", [P, ITEMS], F32)
    modcol = sb(keep, "modcol", [P, 2 * FC * B], F32)
    modbc = sb(keep, "modbc", [P, B, 4, C], F32)
    gab = sb(keep, "gab", [P, B, C], F32)
    wproj_f = sb(keep, "wproj_f", [P, FC, C], F32)
    ones_f = sb(keep, "ones_f", [P, P], F32)
    k_sum = sb(keep, "k_sum", [P, C], F32)
    kv = sb(keep, "kv", [P, B, C], F32)
    ksums = sb(keep, "ksums", [P, B, FC, HEADS], F32)
    rw = sb(keep, "rw", [P, FC, E], F32)
    rscale = sb(keep, "rscale", [P, FC], F32)
    pes_bc = sb(keep, "pes_bc", [P, E], F32)
    next_row = sb(keep, "next_row", [P, E], F32)
    tok_no = sb(keep, "tok_no", [P, TPG], F32)
    tables = sb(keep, "tables", [P, 3, ITEMS], I32)

    padrow = sb(keep, "padrow", [P, ROW], F32)
    pad_to = sb(keep, "pad_to", [P, E], U32)

    z_hi = sb(ph1, "z_hi", [P, TPG, C], F32R)
    wv_f = sb(ph1, "wv_f", [P, FC, C], F32)
    z_lo = sb(ph1, "z_lo", [P, TPG, C], F32R)
    zk = sb(ph1, "zk", [P, FC, C], F32)
    z_hl = [z_hi, z_lo]
    assert TPG == FC
    wq = [sb(ph1, f"wq_{k}", [P, 2 * FC * C], F32R) for k in ("hi", "lo")]
    raw = sb(ph1, "raw", [P, 2, QW], F32)
    sp_hl = [sb(ph1, f"split_{k}", [P, QW], F32R) for k in ("hi", "lo")]
    xg = sb(ph1, "xg", [P, TPG, C], F32)
    hf = [sb(ph1, f"hf{i}", [P, FC, P], F32) for i in range(2)]
    h_t = [[sb(ph1, f"h_t{i}_{k}", [P, FC, GT], F32R) for k in ("hi", "lo")] for i in range(2)]
    k_f = [sb(ph1, f"k_f{i}", [P, C], F32) for i in range(2)]
    k_hl = [[sb(ph1, f"k{i}_{k}", [P, C], F32R) for k in ("hi", "lo")] for i in range(2)]
    qf = [sb(ph1, f"qf{i}", [P, FC, GT], F32) for i in range(2)]
    sa_ks = qf[0]
    mod_stage = [wv_f, wproj_f, wv_f, wproj_f, qf[1], wv_f]
    modbc_flat = modbc[:, :, :, :].rearrange("p b m n -> p (b m n)")
    mod_row = modbc_flat[0:B, 0:6 * C].rearrange("b (m n) -> b m n", m=6)
    mod_tmp = modbc_flat[0:B, 6 * C:7 * C]
    c_sb = sb(ph1, "c_sb", [P, FC * B], F32)
    c_exp = sb(ph1, "c_exp", [P, FC * B], F32)
    silu_c = sb(ph1, "silu_c", [P, FC * B], F32)
    st = sb(ph1, "st", [P, TPG, 6], F32)
    mv = sb(ph1, "mv", [P, TPG, 2], F32)
    ve = sb(ph1, "ve", [P, TPG], F32)
    lnv = sb(ph1, "lnv", [P, TPG], F32)
    y0 = sb(ph1, "y0", [P, TPG], F32)
    nt1 = sb(ph1, "nt1", [P, TPG], F32)
    nt2 = sb(ph1, "nt2", [P, TPG], F32)
    ph1.close()

    kvp = [sb(ph2, f"kvp_{k}", [P, B, FC, C], F32R) for k in ("hi", "lo")]
    def tile2(name, dt=F32R):
        return sb(ph2, name, [P, FC, GT], dt)

    on = [[tile2("on0_hi"), tile2("on0_lo")]]
    qb = [tile2(f"qb{i}", F32) for i in range(2)]
    xb = [sb(ph2, "xb0", [P, TPG, C], F32)]
    on.append([tile2("on1_hi"), tile2("on1_lo")])
    xb.append(sb(ph2, "xb1", [P, TPG, C], F32))
    ksum_now = sb(ph2, "ksum_now", [P, FC, HEADS], F32)
    sel_f = sb(ph2, "sel_f", [HEADS, C], F32)
    sel = sb(ph2, "sel", [HEADS, C], F32R)
    den = sb(ph2, "den", [HEADS, GT], F32)
    rec0 = sb(ph2, "rec0", [HEADS, GT], F32)
    rec = sb(ph2, "rec", [HEADS, GT], F32)
    rec_hl = [sb(ph2, f"rec_{k}", [HEADS, GT], F32R) for k in ("hi", "lo")]
    onf = [sb(ph2, f"onf{i}", [P, GT], F32) for i in range(2)]
    x1 = sb(ph2, "x1", [P, TPG, C], F32)
    lnt = [sb(ph2, f"lnt{i}", [P, C], F32) for i in range(2)]
    rows = [sb(ph2, f"rows{i}", [P, TPG, ROW], F32) for i in range(2)]
    kvp_f = [[rows[b][:, t, 0:C] for t in range(TPG)] for b in range(B)]
    h2t = sb(ph2, "h2t", [P, TPG, C], F32)
    sq_out = sb(ph2, "sq_out", [P, C], F32)
    lg_t = sb(ph2, "lg_t", [E, GT], F32)
    ss = sb(ph2, "ss", [P, TPG], F32)
    st2 = sb(ph2, "st2", [P, TPG, 6], F32)
    mv2 = sb(ph2, "mv2", [P, TPG, 2], F32)
    ve2, ln2, y2, na2, nb2, rstd2 = (sb(ph2, f"ln2_{i}", [P, TPG], F32) for i in range(6))
    ve3, ln3, y3, na3, nb3, rs3 = (sb(ph2, f"rms_{i}", [P, TPG], F32) for i in range(6))
    lg, mx, dl, ex, em, ip, wts, pos = (sb(ph2, f"route_{i}", [P, TPG, E], F32) for i in range(8))
    oh = sb(ph2, "oh", [P, 2, TPG, E], F32)
    chosen = sb(ph2, "chosen", [P, 2, TPG, E], F32)
    destf = sb(ph2, "destf", [P, 2, TPG], F32)
    ix = sb(ph2, "ix", [P, TPG, E], U32)
    ixf = sb(ph2, "ixf", [P, 2, TPG], F32)
    mkb = sb(ph2, "mkb", [P, TPG, E], BF16)
    se, rse, rn, rng, rrn = (sb(ph2, f"sum_{i}", [P, TPG], F32) for i in range(5))
    dest = [sb(ph2, f"dest{i}", [P, 2, TPG], U32) for i in range(2)]
    cnt, ntl, cend = (sb(ph2, f"cnt_{i}", [P, E], F32) for i in range(3))
    cnti = sb(ph2, "cnti", [P, E], I32)
    ntli = sb(ph2, "ntli", [P, E], I32)
    it_e, it_r, it_t, it_k = (sb(ph2, f"it_{i}", [P, ITEMS], F32) for i in range(4))
    ph2.close()

    xrow = [sb(ph3, f"xrow{i}", [P, ROW], F32) for i in range(RING)]
    x_t = [sb(ph3, f"x_t_{k}", [P, C], F32R) for k in ("hi", "lo")]
    act_t = [sb(ph3, f"act_t_{k}", [P, H], F32R) for k in ("hi", "lo")]
    gact = sb(ph3, "gact", [P, H], F32)
    hact = sb(ph3, "hact", [P, H], F32)
    meta = [sb(ph3, f"meta{i}", [P, META], F32) for i in range(RING)]
    cur_w = sb(ph3, "cur_w", [P, 1], F32)
    cur_tok = [sb(ph3, f"cur_tok{i}", [P, 1], U32) for i in range(2)]
    in_b1 = sb(ph3, "in_b1", [P, 1], F32)
    in_b0 = sb(ph3, "in_b0", [P, 1], F32)
    gb0 = sb(ph3, "gb0", [P, C], F32)
    gbr = sb(ph3, "gbr", [P, C], F32)
    orow = [sb(ph3, f"orow{i}", [P, C], F32) for i in range(2)]
    sb(ph3, "spare", [P, 2 * C], F32)
    wbuf = sb(ph3, "wbuf", [P, 2 * 2 * EW], F32R)

    def f32(ap):
        return ap.bitcast(F32)

    T_B, QK_B, ZK_B = bank[0:2], bank[2:4], bank[4:8]
    MOD_B = [*QK_B, *ZK_B[0:2], *ZK_B[0:2]]
    Y_B, H2_B, RB_B, D_B, R_B = bank[0:2], bank[2:4], bank[4:6], bank[6], bank[7]
    M_B = [bank[0:4], [*bank[2:4], bank[7], bank[2]]]
    XT_B, HT_B, G_B, U_B, O_B = bank[0], bank[1], bank[2], bank[3], bank[4]

    s_c, s_x, s_const = sem("c_loaded"), sem("x_loaded"), sem("const_loaded")
    s_raw, s_mod = [sem("raw_even"), sem("raw_odd")], [sem(f"wmod{m}_loaded") for m in range(6)]
    s_modst, s_modbc = sem("mod_stored"), sem("modbc_loaded")
    s_qst, s_wst, s_zst = sem("q_stored"), sem("split_stored"), sem("zero_stored")
    s_passed = sem("waits_passed")
    s_id, s_vset, s_cexp, s_silu, s_modpe, s_modrow, s_colpe, s_col = (
        sem("ident_ready"), sem("vector_setup"), sem("c_exp_ready"), sem("silu_ready"), sem("mod_product"),
        sem("mod_row_ready"), sem("mod_col_turned"), sem("mod_col_ready"))
    s_gab = sem("gab_ready")
    s_hi, s_lo, s_elo = sem("split_hi"), sem("qkv_split_lo"), sem("expert_split_lo")
    s_var, s_seed, s_z, s_ln = sem("var_ready"), sem("rstd_seed"), sem("z_ready"), sem("ln1_step")
    s_T, s_hf, s_hhi, s_hlo = sem("z_turned"), sem("h_ready"), sem("h_hi_ready"), sem("h_lo_ready")
    s_q, s_qe = sem("q_done"), sem("q_taken")
    s_k, s_ke, s_klo, s_ksum1 = sem("k_done"), sem("k_taken"), sem("k_lo_ready"), sem("k_added")
    s_zhi, s_zlo, s_zk, s_zka = sem("z_hi_ready"), sem("z_lo_ready"), sem("zk_done"), sem("zk_added")
    s_vp, s_ksb, s_saks, s_hk = sem("v_proj_weights_loaded"), sem("key_sums_spread"), sem("sa_sums_ready"), sem("hk_ready")
    s_aln = sem("scalar_ln_step")
    s_prep, s_kvm, s_kvt, s_mp, s_mf, s_mhi, s_mlo, s_sel = (
        sem("prep_step"), sem("kv_ready"), sem("kv_done"), sem("kvp_done"),
        sem("kvp_ready"), sem("kvp_hi_ready"), sem("kvp_lo_ready"), sem("sel_ready"))
    s_q2, s_x2, s_x1st, s_ksum = sem("q_back"), sem("x_back"), sem("x1_stored"), sem("ksum_ready")
    s_den, s_dene, s_aden, s_rec0, s_recstep, s_rec, s_rechi, s_reclo, s_rb, s_on = (
        sem("den_done"), sem("den_taken"), sem("scalar_den_step"), sem("recip_seed"), sem("recip_step"), sem("recip_ready"),
        sem("recip_hi_ready"), sem("recip_lo_ready"), sem("recip_spread"), sem("on_ready"))
    s_onhi, s_onlo, s_y, s_xb, s_x1 = sem("on_hi_ready"), sem("on_lo_ready"), sem("proj_done"), sem("xb_ready"), sem("x1_ready")
    s_step2, s_var2, s_seed2, s_aln2 = sem("vector_step2"), sem("var2_ready"), sem("rstd2_seed"), sem("scalar_ln2_step")
    s_h2, s_sq, s_h2t, s_h2te = sem("h2_ready"), sem("sq_ready"), sem("h2_turned"), sem("h2t_ready")
    s_lgp, s_lgt, s_lg = sem("logits_done"), sem("logits_taken"), sem("logits_turned")
    s_var3, s_seed3, s_aln3, s_ex, s_dl = sem("rms_ready"), sem("rms_seed"), sem("scalar_rms_step"), sem("exp_ready"), sem("logits_less_max")
    s_mk, s_rank, s_ranku = sem("mask_ready"), sem("rank_done"), sem("rank_taken")
    s_rowm, s_free, s_dest = sem("row_numbers"), sem("rows_cleared"), sem("dest_ready")
    s_scat = [sem(f"tile{t}_scattered") for t in range(TPG)]
    s_it, s_pad0, s_pad, s_padi = sem("item_step"), sem("first_pads_scattered"), sem("pads_scattered"), sem("pad_rows_ready")
    s_w, s_xt, s_xthi, s_xtlo, s_meta = sem("weights_loaded"), sem("x_turned"), sem("x_hi_ready"), sem("x_lo_ready"), sem("meta_kept")
    s_xr = [sem(f"rows{i}_loaded") for i in range(RING)]
    s_g, s_u, s_ga, s_h, s_ht, s_hthi, s_htlo = sem("gate_done"), sem("up_done"), sem("gelu_ready"), sem("act_ready"), sem("act_turned"), sem("act_hi_ready"), sem("act_lo_ready")
    s_o, s_cur, s_gb0, s_gbr, s_or, s_add = sem("down_done"), sem("cur_ready"), sem("gb0_ready"), sem("gb_rows_step"), sem("out_rows_ready"), sem("rows_added")

    def wait_apart(eng, sem, value):
        at_least(eng, sem, value)
        if not isinstance(value, int):
            eng.sem_inc(s_passed, 1)

    def group_rows(t, g):
        return t[bass.ds(g * GT, GT), :].rearrange("(t p) c -> p t c", p=P)

    def has(g, ahead):
        return not isinstance(g, int) or g + ahead < NG

    def run_groups1(eng, group1, between=None):
        for g in range(3):
            group1(g, g % 2, 0)
            if between:
                between(g)
        with eng.Fori(1, GPB // 2 - 1) as j:
            group1(2 * j + 1, 1, 0)
            group1(2 * j + 2, 0, 0)
        group1(GPB - 1, 1, 0)
        group1(GPB, 0, 1)
        with eng.Fori(GPB // 2, NG // 2 - 2) as j:
            group1(2 * j + 1, 1, 1)
            group1(2 * j + 2, 0, 1)
        for g in range(NG - 3, NG):
            group1(g, g % 2, 1)

    def batch_after(g, b):
        return (g + 1) // GPB if isinstance(g, int) else b

    def ends_batch(g):
        return isinstance(g, int) and g == GPB

    def run_groups2(eng, group2, before_last=None):
        for g in range(3):
            group2(g, g % 2)
        with eng.Fori(1, (NG - 4) // 2) as j:
            group2(2 * j + 1, 1)
            group2(2 * j + 2, 0)
        for g in range(NG - 3, NG):
            if before_last and g == NG - 1:
                before_last()
            group2(g, g % 2)

    def run_items(eng, item):
        for i in range(1, RING + 2):
            item(i, i % RING)
        with eng.Fori(1, (ITEMS - 3) // RING) as j:
            for u in range(RING):
                item(RING * j + 2 + u, (2 + u) % RING)
        item(ITEMS - 1, (ITEMS - 1) % RING)

    assert (ITEMS - 3) % RING == 0

    def batch_of(g):
        return g // GPB if isinstance(g, int) else (g >> 3) & 1

    assert GPB == 8

    def phase1_over(eng):
        eng.wait_ge(s_zk, TPG * NG)
        eng.wait_ge(s_ksum1, TPG * NG)
        eng.wait_ge(s_qst, 16 * NG)
        eng.wait_ge(s_wst, 32 * E * QPE)
        eng.wait_ge(s_gab, B)

    def phase2_over(eng):
        for t in range(TPG):
            eng.wait_ge(s_scat[t], SCAT * NG)
        eng.wait_ge(s_pad0, 16)
        eng.wait_ge(s_x1st, 16 * NG)
        eng.wait_ge(s_zst, 32)
        eng.wait_ge(s_it, ITEM_STEPS)

    ITEM_STEPS = 5 + E - 1 + 11

    block = keep.enter_context(nc.Block())

    @block.sync
    def _(sp):
        sp.dma_start(c_sb[:, :], c_t).then_inc(s_c, 16)
        def load_wmod(m):
            if m in (2, 3, 5):
                sp.wait_ge(s_modpe, 3 if m == 5 else m - 1)
            sp.dma_start(mod_stage[m][:, :, :], wmod[:, m * C:(m + 1) * C].rearrange("(f p) n -> p f n", p=P)).then_inc(s_mod[m], 16)

        load_wmod(0)
        sp.dma_start(xg[:, :, :], group_rows(x, 0)).then_inc(s_x, 16)
        load_wmod(1)
        for f in range(FC):
            at_least(sp, s_lo, f - 1)
            sp.dma_start(raw[:, f % 2, 0:KQW], wqkv[:, f * KQW:(f + 1) * KQW]).then_inc(s_raw[f % 2], 16)

        def load_x1(g):
            sp.wait_ge(s_T, TPG * g)
            sp.wait_ge(s_zlo, TPG * g)
            sp.dma_start(xg[:, :, :], group_rows(x, g)).then_inc(s_x, 16)

        load_x1(1)
        def load_expert_raw(g, s):
            if isinstance(g, int) and g == 0:
                sp.wait_ge(s_lo, FC)
            else:
                sp.wait_ge(s_elo, 2 * (g - 1) + s + 1)
            sp.dma_start(raw[:, s, :], moe_w[bass.ds((2 * g + s) * P, P), :]).then_inc(s_raw[s], 16)

        def store_expert(g, s):
            sp.wait_ge(s_elo, 2 * g + s + 1)
            for k in range(2):
                sp.dma_start(wd[bass.ds((2 * g + s) * P, P), k * QW:(k + 1) * QW], f32(sp_hl[k][:, :])).then_inc(s_wst, 16)

        for s in range(2):
            load_expert_raw(0, s)
        for m in range(2, 5):
            load_wmod(m)
        for b in range(B):
            sp.dma_start(gab[:, b, :], b_proj.partition_broadcast(P)).then_inc(s_const, 16)
        sp.dma_start(rw[:, :, :], r_w.rearrange("p (f e) -> p f e", f=FC)).then_inc(s_const, 16)
        sp.dma_start(rscale[:, :], r_scale).then_inc(s_const, 16)
        sp.dma_start(pes_bc[:, :], pes.partition_broadcast(P)).then_inc(s_const, 16)

        def group1(g, par, b):
            last = not has(g, 1)
            store_expert(g, 0)
            if not last:
                load_expert_raw(g + 1, 0)
            if has(g, 2):
                load_x1(g + 2)
            if not last:
                store_expert(g, 1)
                load_expert_raw(g + 1, 1)
            wait_apart(sp, s_qst, 16 * g)
            if last:
                store_expert(g, 1)
            sp.wait_ge(s_qe, FC * (g + 1))
            sp.dma_start(qd[bass.ds(g * P, P), :], qf[par][:, :, :].rearrange("p f t -> p (f t)")).then_inc(s_qst, 16)

        def other_weights(g):
            if g == 0:
                load_wmod(5)
                sp.wait_ge(s_modpe, 6)
                sp.dma_start(wv_f[:, :, :], wqkv[:, 2 * FC * C:].rearrange("p (f n) -> p f n", f=FC)).then_inc(s_vp, 16)
                sp.dma_start(wproj_f[:, :, :], wproj.rearrange("p (f n) -> p f n", f=FC)).then_inc(s_vp, 16)

        run_groups1(sp, group1, between=other_weights)

        phase1_over(sp)

        def load_q(g, par):
            wait_apart(sp, s_q2, 16 * g)
            wait_apart(sp, s_on, HG * (g - 1))
            sp.dma_start(qb[par][:, :, :].rearrange("p f t -> p (f t)"), qd[bass.ds(g * P, P), :]).then_inc(s_q2, 16)

        def load_x(g, par):
            wait_apart(sp, s_x2, 16 * g)
            sp.dma_start(xb[par][:, :, :], group_rows(x, g)).then_inc(s_x2, 16)

        load_q(0, 0)
        load_x(0, 0)
        load_q(1, 1)
        load_x(1, 1)
        sp.wait_ge(s_padi, 1)
        sp.dma_start(out[NT:NT + P, :], padrow[:, 0:C]).then_inc(s_zst, 16)
        sp.wait_ge(s_padi, 2)
        sp.dma_start(xs[E * CAP:E * CAP + P, :], padrow[:, :]).then_inc(s_zst, 16)

        def group2(g, par):
            more = has(g, 2)
            if more:
                load_q(g + 2, par)
            sp.wait_ge(s_x1, TPG * (g + 1))
            sp.dma_start(group_rows(out, g), x1[:, :, :]).then_inc(s_x1st, 16)
            if more:
                load_x(g + 2, par)

        def load_piece(e, half, q):
            sp.dma_start(f32(wbuf[:, bass.ds(half * 2 * EW + q * 2 * QW, 2 * QW)]),
                         wd[bass.ds((e * QPE + q) * P, P), :]).then_inc(s_w, 16)

        def early_weights():
            sp.wait_ge(s_on, HG * NG)
            for q in range(EARLY):
                sp.wait_ge(s_x1, TPG * (NG - 1) + q)
                load_piece(0, 0, q)

        run_groups2(sp, group2, before_last=early_weights)

        for q in range(EARLY, QPE):
            load_piece(0, 0, q)
        phase2_over(sp)

        def load_rows(i, at):
            if not isinstance(i, int) or i >= RING:
                sp.wait_ge(s_xt, i - RING + 1)
                wait_apart(sp, s_meta, i - RING + 1)
            r = sp.value_load(tables[0:1, 0, bass.ds(i, 1)], min_val=0, max_val=E * CAP)
            sp.dma_start(xrow[at][:, :], xs[bass.ds(r, P), :]).then_inc(s_xr[at], 16)

        def next_weights(i):
            e = sp.value_load(tables[0:1, 1, bass.ds(i, 1)], min_val=0, max_val=E - 1)
            e_after = sp.value_load(tables[0:1, 1, bass.ds(i + 1, 1)], min_val=0, max_val=E - 1)
            of_e = sp.value_load(tables[0:1, 2, bass.ds(i, 1)], min_val=0, max_val=ITEMS)

            def piece(q):
                wait_apart(sp, s_w, 16 * QPE * (e + 1))
                wait_apart(sp, s_o, i)
                nxt = sp.value_load(tables[0:1, 1, bass.ds(i, 1)], min_val=0, max_val=E - 2) + 1
                load_piece(nxt, nxt & 1, q)

            with sp.If(e > 0):
                with sp.If(e < E - 1):
                    with sp.If(of_e < 1):
                        for q in range(QPE // 2):
                            piece(q)
                        with sp.If(e_after > e):
                            for q in range(QPE // 2, QPE):
                                piece(q)
                    with sp.If(of_e > 0):
                        with sp.If(of_e < 2):
                            for q in range(QPE // 2, QPE):
                                piece(q)

        load_rows(0, 0)
        sp.wait_ge(s_pad, 16 * (E - 1))
        for i in range(1, RING):
            load_rows(i, i)
        sp.wait_ge(s_w, 16 * QPE)
        for q in range(QPE):
            load_piece(1, 1, q)
        load_rows(RING, 0)

        def step(i, at):
            load_rows(i, at)
            next_weights(i - RING)

        first = RING + 1
        with sp.Fori(0, (ITEMS - first) // RING) as j:
            for u in range(RING):
                step(first + RING * j + u, (first + u) % RING)
        for i in range(ITEMS - (ITEMS - first) % RING, ITEMS):
            step(i, i % RING)
        for i in range(ITEMS - RING, ITEMS - 1):
            next_weights(i)
        sp.wait_ge(s_add, 16 * ITEMS)

    @block.gpsimd
    def _(pool):
        pool.memset(ident[:, :], 0.0).then_inc(s_id, 1)
        pool.memset(before[:, :], 1.0).then_inc(s_id, 1)
        pool.memset(ones[:, :], 1.0).then_inc(s_id, 1)
        pool.memset(headmask[:, :], 1.0).then_inc(s_id, 1)
        pool.memset(inhead[:, :, :], 1.0).then_inc(s_id, 1)
        pool.wait_ge(s_id, 5)
        pool.affine_select(out=ident[:, :], in_=ident[:, :], compare_op=ALU.not_equal, fill=1.0, base=0,
                           pattern=[[-1, P]], channel_multiplier=1).then_inc(s_id, 1)
        pool.affine_select(out=before[:, :], in_=before[:, :], compare_op=ALU.is_gt, fill=0.0, base=0,
                           pattern=[[1, P]], channel_multiplier=-1).then_inc(s_id, 1)
        blocks = headmask[:, :].rearrange("p (a n) -> p a n", n=HEAD)
        pool.affine_select(out=blocks, in_=blocks, compare_op=ALU.is_ge, fill=0.0, base=0,
                           pattern=[[-HEAD, P // HEAD], [0, HEAD]], channel_multiplier=1).then_inc(s_id, 1)
        pool.wait_ge(s_id, 8)
        pool.affine_select(out=blocks, in_=blocks, compare_op=ALU.is_ge, fill=0.0, base=HEAD - 1,
                           pattern=[[HEAD, P // HEAD], [0, HEAD]], channel_multiplier=-1).then_inc(s_id, 1)
        pool.affine_select(out=inhead[:, :, :], in_=inhead[:, :, :], compare_op=ALU.is_ge, fill=0.0, base=0,
                           pattern=[[P, FC], [-HEAD, HEADS]], channel_multiplier=1).then_inc(s_id, 1)
        pool.wait_ge(s_id, 10)
        pool.affine_select(out=inhead[:, :, :], in_=inhead[:, :, :], compare_op=ALU.is_ge, fill=0.0, base=HEAD - 1,
                           pattern=[[-P, FC], [HEAD, HEADS]], channel_multiplier=-1).then_inc(s_id, 1)
        pool.iota(iota_e[:, :], [[1, E]], base=0, channel_multiplier=0, allow_small_or_imprecise_dtypes=True).then_inc(s_id, 1)
        pool.iota(lane[:, :], [[1, 1]], base=0, channel_multiplier=1, allow_small_or_imprecise_dtypes=True).then_inc(s_id, 1)
        pool.iota(list_at[:, :], [[CAP, E]], base=0, channel_multiplier=0, allow_small_or_imprecise_dtypes=True).then_inc(s_id, 1)
        pool.iota(next_row[:, :], [[CAP, E]], base=0, channel_multiplier=0, allow_small_or_imprecise_dtypes=True).then_inc(s_id, 1)
        pool.iota(item_no[:, :], [[1, ITEMS]], base=0, channel_multiplier=0, allow_small_or_imprecise_dtypes=True).then_inc(s_id, 1)
        pool.iota(tok_no[:, :], [[P, TPG]], base=0, channel_multiplier=1, allow_small_or_imprecise_dtypes=True).then_inc(s_id, 1)

        pool.memset(ones_f[:, :], 1.0).then_inc(s_id, 1)

        def low_expert(g, s):
            pool.wait_ge(s_hi, FC + 2 * g + s + 1)
            pool.tensor_tensor(sp_hl[1][:, :], raw[:, s, :], f32(sp_hl[0][:, :]), ALU.subtract).then_inc(s_elo, 1)

        def low_z(g, t):
            pool.wait_ge(s_zhi, TPG * g + t + 1)
            pool.tensor_tensor(z_hl[1][:, t, :], xg[:, t, :], f32(z_hl[0][:, t, :]), ALU.subtract).then_inc(s_zlo, 1)

        def low_k(g, t):
            pool.wait_ge(s_ke, TPG * g + t + 1)
            pool.tensor_tensor(k_hl[t % 2][1][:, :], k_f[t % 2][:, :], f32(k_hl[t % 2][0][:, :]), ALU.subtract).then_inc(s_klo, 1)

        def add_k(g, t):
            if isinstance(g, int) and g % GPB == 0 and t == 0:
                if g:
                    pool.wait_ge(s_ksb, g // GPB)
                pool.tensor_copy(k_sum[:, :], k_f[t % 2][:, :]).then_inc(s_ksum1, 1)
            else:
                pool.wait_ge(s_ksum1, TPG * g + t)
                pool.tensor_tensor(k_sum[:, :], k_sum[:, :], k_f[t % 2][:, :], ALU.add).then_inc(s_ksum1, 1)

        def group1(g, par, b):
            more = has(g, 1)
            low_k(g, 0)
            add_k(g, 0)
            low_k(g, 1)
            add_k(g, 1)
            if more:
                low_z(g + 1, 0)
                low_expert(g, 0)
            low_k(g, 2)
            add_k(g, 2)
            if more:
                low_z(g + 1, 1)
            low_k(g, 3)
            add_k(g, 3)
            if more:
                low_z(g + 1, 2)
                low_z(g + 1, 3)
                low_expert(g, 1)

        def mod_rows(g):
            if g == 0:
                pool.wait_ge(s_modrow, 6)
                pool.dma_start(mod_d.rearrange("b (m n) -> b m n", m=4), mod_row[:, 2:6, :]).then_inc(s_modst, 16)
            elif g == 1:
                pool.wait_ge(s_modst, 16)
                for b in range(B):
                    pool.dma_start(modbc[:, b, :, :].rearrange("p m n -> p (m n)"), mod_d[b, :].partition_broadcast(P)).then_inc(s_modbc, 16)
            else:
                pool.wait_ge(s_modbc, 16 * B)
                pool.wait_ge(s_const, 16 * 5)
                for b in range(B):
                    pool.tensor_tensor(gab[:, b, :], modbc[:, b, 0, :], gab[:, b, :], ALU.mult).then_inc(s_gab, 1)

        for t in range(TPG):
            low_z(0, t)
        run_groups1(pool, group1, between=mod_rows)

        phase1_over(pool)
        for i in range(2):
            pool.memset(rows[i][:, :, C:], 0.0).then_inc(s_free, 1)
        pool.memset(padrow[:, :], 0.0).then_inc(s_padi, 1)
        pool.wait_ge(s_padi, 1)
        pool.tensor_scalar(padrow[:, TOK_AT:TOK_AT + 1].bitcast(I32), lane[:, :], float(NT), None, ALU.add).then_inc(s_padi, 1)

        def add_bias(g, par):
            pool.wait_ge(s_x2, 16 * (g + 1))
            for t in range(TPG):
                b = batch_of(g)
                row = gab[:, b, :] if isinstance(b, int) else gab[:, bass.ds(b, 1), :].rearrange("p a n -> p (a n)")
                pool.tensor_tensor(xb[par][:, t, :], xb[par][:, t, :], row, ALU.add).then_inc(s_xb, 1)

        def low_on(g, par, j):
            pool.wait_ge(s_onhi, HG * g + j + 1)
            pool.tensor_tensor(on[par][1][:, j, :], onf[j % 2][:, :], f32(on[par][0][:, j, :]), ALU.subtract).then_inc(s_onlo, 1)

        pool.memset(sel_f[:, :], 1.0).then_inc(s_sel, 1)
        pool.wait_ge(s_sel, 1)
        pool.affine_select(out=sel_f[:, :], in_=sel_f[:, :], compare_op=ALU.is_ge, fill=0.0, base=0,
                           pattern=[[1, C]], channel_multiplier=-HEAD).then_inc(s_sel, 1)
        pool.wait_ge(s_sel, 2)
        pool.affine_select(out=sel_f[:, :], in_=sel_f[:, :], compare_op=ALU.is_ge, fill=0.0, base=HEAD - 1,
                           pattern=[[-1, C]], channel_multiplier=HEAD).then_inc(s_sel, 1)
        pool.wait_ge(s_sel, 3)
        pool.tensor_copy(sel[:, :], sel_f[:, :]).then_inc(s_sel, 1)

        def number_rows(g, par):
            if not isinstance(g, int) or g:
                wait_apart(pool, s_rowm, 2 * g)
            pool.tensor_copy(rows[par][:, :, TOK_AT].bitcast(I32), tok_no[:, :]).then_inc(s_rowm, 1)
            wait_apart(pool, s_rowm, 2 * g + 1)
            pool.tensor_scalar(tok_no[:, :], tok_no[:, :], float(GT), None, ALU.add).then_inc(s_rowm, 1)

        def scatter(g, par):
            pool.wait_ge(s_dest, g + 1)
            wait_apart(pool, s_rowm, 2 * g + 1)
            for t in range(TPG):
                wait_apart(pool, s_scat[t], SCAT * g)
                for k in range(2):
                    pool.indirect_dma_start(out=xs, out_offset=bass.IndirectOffsetOnAxis(dest[par][:, k, t:t + 1], 0),
                                            in_=rows[par][:, t, :], in_offset=None).then_inc(s_scat[t], 16)

        def group2(g, par):
            if has(g, 1):
                low_on(g + 1, 1 - par, 0)
                low_on(g + 1, 1 - par, 1)
                if not isinstance(g, int) or g:
                    add_bias(g + 1, 1 - par)
                low_on(g + 1, 1 - par, 2)
                low_on(g + 1, 1 - par, 3)
                if isinstance(g, int) and g == 0:
                    add_bias(g + 1, 1 - par)
            if not isinstance(g, int) or g:
                scatter(g - 1, 1 - par)
            number_rows(g, par)

        add_bias(0, 0)
        run_groups2(pool, group2)
        pool.wait_ge(s_padi, 3)

        def pad(e):
            return pool.indirect_dma_start(out=xs, out_offset=bass.IndirectOffsetOnAxis(pad_to[:, e:e + 1], 0),
                                           in_=padrow[:, :], in_offset=None)

        pad(0).then_inc(s_pad0, 16)
        scatter(NG - 1, 1)
        for e in range(1, E):
            pad(e).then_inc(s_pad, 16)

        phase2_over(pool)

        def item(i, at):
            pool.wait_ge(s_or, i + 1)
            wait_apart(pool, s_add, 16 * i)
            pool.indirect_dma_start(out=out, out_offset=bass.IndirectOffsetOnAxis(cur_tok[at % 2][:, 0:1], 0), in_=orow[at % 2][:, :],
                                    in_offset=None, compute_op=ALU.add).then_inc(s_add, 16)

        item(0, 0)
        run_items(pool, item)
        pool.wait_ge(s_add, 16 * ITEMS)

    @block.scalar
    def _(act):
        act.preload_act_table_set("natural_log_exp_and_others")
        act.wait_ge(s_c, 16)
        act.activation(c_exp[:, :], c_sb[:, :], ACT.Exp, scale=-1.0).then_inc(s_cexp, 1)

        def split_hi(turn, half, dst, width=QW):
            act.wait_ge(s_raw[half], 16 * (turn + 1))
            act.activation(dst, raw[:, half, 0:width], ACT.Copy).then_inc(s_hi, 1)

        def expert_hi(g, s):
            at_least(act, s_wst, 32 * (2 * g + s))
            split_hi(FC // 2 + g, s, sp_hl[0][:, :])

        aln = Steps(act, s_aln, 1)

        def seed1(g):
            aln.begin(g)
            act.wait_ge(s_var, g + 1)
            aln.did(act.activation(lnv[:, :], ve[:, :], ACT.Ln))
            aln.settle()
            act.activation(y0[:, :], lnv[:, :], ACT.Exp, scale=-0.5).then_inc(s_seed, 1)
            aln.end()

        def hi1(g, t, par):
            act.wait_ge(s_hf, TPG * g + t + 1)
            act.activation(h_t[par][0][:, :, t * P:(t + 1) * P], hf[t % 2][:, :, :], ACT.Copy).then_inc(s_hhi, 1)

        def high_z(g, t):
            act.wait_ge(s_z, TPG * g + t + 1)
            at_least(act, s_zk, TPG * (g - 1) + t + 1)
            act.activation(z_hl[0][:, t, :], xg[:, t, :], ACT.Copy).then_inc(s_zhi, 1)

        def kq_hi(f):
            split_hi(f // 2, f % 2, wq[0][:, f * KQW:(f + 1) * KQW], KQW)

        def k_out(g, t):
            act.wait_ge(s_k, TPG * g + t + 1)
            at_least(act, s_ksum1, TPG * g + t - 1)
            at_least(act, s_zk, TPG * g + t - 1)
            act.activation(k_f[t % 2][:, :], QK_B[t % 2][:, :], ACT.Relu)
            act.activation(k_hl[t % 2][0][:, :], QK_B[t % 2][:, :], ACT.Relu).then_inc(s_ke, 1)

        def q_out(g, par, j):
            act.wait_ge(s_q, FC * g + j + 1)
            if j == 0:
                at_least(act, s_qst, 16 * (g - 1))
            src = QK_B if has(g, 1) else T_B
            act.activation(qf[par][:, j, :], src[j % 2][:, :], ACT.Relu).then_inc(s_qe, 1)

        def sa_sums(b, bc, tile):
            act.wait_ge(s_ksb, b + 1)
            for f in range(FC):
                at = f * B + b
                act.activation(tile[:, f, :], bc[:, :], ACT.Copy, scale=modcol[:, at:at + 1]).then_inc(s_saks, 1)

        seed1(0)
        for t in range(TPG):
            high_z(0, t)
        kq_hi(0)
        kq_hi(1)
        for t in range(TPG):
            hi1(0, t, 0)
        kq_hi(2)
        kq_hi(3)

        def group1(g, par, b):
            if not has(g, 1):
                for t in range(TPG):
                    k_out(g, t)
                    q_out(g, par, t)
                    if t % 2 == 0:
                        expert_hi(g, t // 2)
                return
            if ends_batch(g):
                act.wait_ge(s_qst, 16 * (g - 1))
                sa_sums(0, ZK_B[0], sa_ks)
            k_out(g, 0)
            k_out(g, 1)
            seed1(g + 1)
            high_z(g + 1, 0)
            expert_hi(g, 0)
            k_out(g, 2)
            high_z(g + 1, 1)
            k_out(g, 3)
            hi1(g + 1, 0, 1 - par)
            high_z(g + 1, 2)
            hi1(g + 1, 1, 1 - par)
            q_out(g, par, 0)
            hi1(g + 1, 2, 1 - par)
            high_z(g + 1, 3)
            expert_hi(g, 1)
            q_out(g, par, 1)
            hi1(g + 1, 3, 1 - par)
            q_out(g, par, 2)
            q_out(g, par, 3)

        assert TPG == FC
        run_groups1(act, group1)

        phase1_over(act)
        aln2, aln3, aden = Steps(act, s_aln2, 1), Steps(act, s_aln3, 1), Steps(act, s_aden, 1)

        def kvp_hi(b, parts):
            for a in parts:
                act.wait_ge(s_mf, HG * b + a + 1)
                act.activation(kvp[0][:, b, a, :], kvp_f[b][a], ACT.Copy).then_inc(s_mhi, 1)

        def den_out(g):
            aden.begin(g)
            act.wait_ge(s_den, g + 1)
            at_least(act, s_rec, g)
            act.activation(den[:, :], D_B[0:HEADS, :], ACT.Copy, bias=DEN_EPS).then_inc(s_dene, 1)
            act.wait_ge(s_dene, g + 1)
            aden.did(act.activation(rec0[:, :], den[:, :], ACT.Ln))
            aden.settle()
            act.activation(rec0[:, :], rec0[:, :], ACT.Exp, scale=-1.0).then_inc(s_rec0, 1)
            aden.end()

        def rec_hi(g):
            act.wait_ge(s_rec, g + 1)
            at_least(act, s_rb, HG * g)
            act.activation(rec_hl[0][:, :], rec[:, :], ACT.Copy).then_inc(s_rechi, 1)

        def on_hi(g, par, j):
            act.wait_ge(s_on, HG * g + j + 1)
            at_least(act, s_y, TPG * (g - 1))
            act.activation(on[par][0][:, j, :], onf[j % 2][:, :], ACT.Copy).then_inc(s_onhi, 1)

        def seed2(g, half):
            h = slice(2 * half, 2 * half + 2)
            aln2.begin(2 * g + half)
            act.wait_ge(s_var2, 2 * g + half + 1)
            aln2.did(act.activation(ln2[:, h], ve2[:, h], ACT.Ln))
            aln2.settle()
            act.activation(y2[:, h], ln2[:, h], ACT.Exp, scale=-0.5).then_inc(s_seed2, 1)
            aln2.end()

        def square(g, t, par):
            act.wait_ge(s_h2, TPG * g + t + 1)
            at_least(act, s_sq, TPG * g + t)
            if t == 0:
                at_least(act, s_var3, g)
            act.activation(sq_out[:, :], rows[par][:, t, 0:C], ACT.Square, accum_out=ss[:, t:t + 1]).then_inc(s_sq, 1)

        def h2t_copy(g, t):
            act.wait_ge(s_h2t, TPG * g + t + 1)
            act.activation(h2t[:, t, :], H2_B[t % 2][:, :], ACT.Copy).then_inc(s_h2te, 1)

        def logits_out(g):
            act.wait_ge(s_lgp, g + 1)
            at_least(act, s_lg, g)
            act.activation(lg_t[:, :], D_B[0:E, :], ACT.Copy).then_inc(s_lgt, 1)

        def rms_seed(g):
            aln3.begin(g)
            act.wait_ge(s_var3, g + 1)
            aln3.did(act.activation(ln3[:, :], ve3[:, :], ACT.Ln))
            aln3.settle()
            act.activation(y3[:, :], ln3[:, :], ACT.Exp, scale=-0.5).then_inc(s_seed3, 1)
            aln3.end()

        def exps(g):
            act.wait_ge(s_dl, g + 1)
            act.activation(ex[:, :, :], dl[:, :, :], ACT.Exp).then_inc(s_ex, 1)

        def group2(g, par):
            before_it = not isinstance(g, int) or g > 0
            if before_it:
                rms_seed(g - 1)
            if has(g, 1):
                rec_hi(g + 1)
            if before_it:
                for t in range(TPG):
                    h2t_copy(g - 1, t)
            if has(g, 1):
                on_hi(g + 1, 1 - par, 0)
            seed2(g, 0)
            if has(g, 1):
                on_hi(g + 1, 1 - par, 1)
            if before_it:
                logits_out(g - 1)
            square(g, 0, par)
            square(g, 1, par)
            if has(g, 1):
                on_hi(g + 1, 1 - par, 2)
                on_hi(g + 1, 1 - par, 3)
            if before_it:
                exps(g - 1)
            seed2(g, 1)
            if has(g, 2):
                den_out(g + 2)
            if not has(g, 1):
                h2t_copy(g, 0)
                h2t_copy(g, 1)
            square(g, 2, par)
            square(g, 3, par)
            if not before_it:
                kvp_hi(1, range(HG))

        kvp_hi(0, range(HG))
        den_out(0)
        rec_hi(0)
        on_hi(0, 0, 0)
        on_hi(0, 0, 1)
        den_out(1)
        on_hi(0, 0, 2)
        on_hi(0, 0, 3)
        sa_sums(1, H2_B[0], h2t)
        run_groups2(act, group2)
        for t in range(2, TPG):
            h2t_copy(NG - 1, t)
        rms_seed(NG - 1)
        logits_out(NG - 1)
        exps(NG - 1)

        phase2_over(act)
        act.preload_act_table(ACT.Gelu_apprx_tanh)

        def x_hi(i):
            act.wait_ge(s_xt, i + 1)
            at_least(act, s_u, i)
            act.activation(x_t[0][:, :], XT_B[:, :], ACT.Copy).then_inc(s_xthi, 1)

        def gelu(i):
            act.wait_ge(s_g, i + 1)
            at_least(act, s_h, i)
            act.activation(gact[:, :], G_B[:, :], ACT.Gelu_apprx_tanh).then_inc(s_ga, 1)

        def act_hi(i):
            act.wait_ge(s_ht, i + 1)
            at_least(act, s_o, i)
            act.activation(act_t[0][:, :], HT_B[:, :], ACT.Copy).then_inc(s_hthi, 1)

        def gb_rows(i):
            act.wait_ge(s_cur, 2 * (i + 1))
            act.activation(gb0[:, :], modbc[:, 0, 3, :], ACT.Copy, scale=in_b0[:, 0:1]).then_inc(s_gb0, 1)

        x_hi(0)
        gelu(0)
        x_hi(1)

        def item(i, at):
            gelu(i)
            act_hi(i - 1)
            if not isinstance(i, int) or i < ITEMS - 1:
                x_hi(i + 1)
            gb_rows(i - 1)

        run_items(act, item)
        act_hi(ITEMS - 1)
        gb_rows(ITEMS - 1)

    @block.vector
    def _(dve):
        tt, ts, stt = dve.tensor_tensor, dve.tensor_scalar, dve.scalar_tensor_tensor

        setup = Steps(dve, s_vset, 0)
        setup.begin(0)
        dve.wait_ge(s_c, 16)
        dve.wait_ge(s_cexp, 1)
        setup.did(ts(c_exp[:, :], c_exp[:, :], 1.0, None, ALU.add))
        setup.settle()
        setup.did(dve.reciprocal(c_exp[:, :], c_exp[:, :]))
        setup.settle()
        tt(silu_c[:, :], c_sb[:, :], c_exp[:, :], ALU.mult).then_inc(s_silu, 1)

        lns = Steps(dve, s_ln, 2 * TPG + 3)

        def stats1(g):
            lns.begin(g)
            dve.wait_ge(s_x, 16 * (g + 1))
            for t in range(TPG):
                lns.did(dve.bn_stats(st[:, t, :], xg[:, t, :]))
            lns.settle(wait_apart)
            for t in range(TPG):
                lns.did(dve.bn_aggr(mv[:, t, :], st[:, t, :]))
            lns.settle()
            ts(ve[:, :], mv[:, :, 1], LN_EPS, None, ALU.add).then_inc(s_var, 1)
            dve.wait_ge(s_seed, g + 1)
            newton(lns, y0[:, :], ve[:, :], nt1[:, :], nt2[:, :])
            for t in range(TPG):
                ts(xg[:, t, :], xg[:, t, :], mv[:, t, 0:1], nt2[:, t:t + 1], ALU.subtract, ALU.mult).then_inc(s_z, 1)
            lns.end()

        def newton(steps, y, v, a, res):
            steps.did(tt(a, y, y, ALU.mult))
            steps.settle()
            steps.did(stt(a, a, -0.5, v, ALU.mult, ALU.mult))
            steps.settle()
            steps.did(stt(res, a, 1.5, y, ALU.add, ALU.mult))
            steps.settle()

        def h_of(g, t, b):
            dve.wait_ge(s_T, TPG * g + t + 1)
            at_least(dve, s_hlo, TPG * g + t - 1)
            for f in range(FC):
                at = f * B + b
                last = ts(hf[t % 2][:, f, :], T_B[t % 2][:, f * P:(f + 1) * P], modcol[:, FC * B + at:FC * B + at + 1],
                          modcol[:, at:at + 1], ALU.mult, ALU.add)
            last.then_inc(s_hf, 1)

        def low_h(g, t, par):
            dve.wait_ge(s_hhi, TPG * g + t + 1)
            dve.wait_ge(s_hf, TPG * g + t + 1)
            tt(h_t[par][1][:, :, t * P:(t + 1) * P], hf[t % 2][:, :, :], f32(h_t[par][0][:, :, t * P:(t + 1) * P]), ALU.subtract).then_inc(s_hlo, 1)

        def mod_part(m):
            dve.wait_ge(s_modpe, m + 1)
            src = MOD_B[m][0:B, :]
            if m in (0, 3):
                dve.tensor_copy(mod_row[:, m, :], src).then_inc(s_modrow, 1)
            elif m in (1, 4):
                ts(mod_row[:, m, :], src, 1.0, None, ALU.add).then_inc(s_modrow, 1)
            else:
                setup.did(ts(mod_tmp[:, :], src, 0.0, 2.0, ALU.is_ge, ALU.mult))
                setup.settle()
                setup.did(ts(mod_tmp[:, :], mod_tmp[:, :], -1.0, None, ALU.add))
                setup.settle()
                setup.did(tt(mod_row[:, m, :], src, mod_tmp[:, :], ALU.mult))
                setup.settle()
                stt(mod_row[:, m, :], mod_row[:, m, :], 0.25, mod_tmp[:, :], ALU.max, ALU.mult).then_inc(s_modrow, 1)

        def kq_lo(f):
            dve.wait_ge(s_hi, f + 1)
            dve.wait_ge(s_raw[f % 2], 16 * (f // 2 + 1))
            cols = slice(f * KQW, (f + 1) * KQW)
            tt(wq[1][:, cols], raw[:, f % 2, 0:KQW], f32(wq[0][:, cols]), ALU.subtract).then_inc(s_lo, 1)

        stats1(0)
        mod_part(0)
        mod_part(1)
        dve.wait_ge(s_colpe, 1)
        dve.tensor_copy(modcol[:, :], ZK_B[0][:, 0:2 * FC * B]).then_inc(s_col, 1)
        dve.wait_ge(s_col, 1)
        h_of(0, 0, 0)
        kq_lo(0)
        low_h(0, 0, 0)
        kq_lo(1)
        h_of(0, 1, 0)
        h_of(0, 2, 0)
        low_h(0, 1, 0)
        h_of(0, 3, 0)
        low_h(0, 2, 0)
        low_h(0, 3, 0)
        kq_lo(2)
        kq_lo(3)

        def add_zk(g):
            dve.wait_ge(s_zk, TPG * (g + 1))
            first = isinstance(g, int) and g % GPB == 0
            if not first:
                dve.wait_ge(s_zka, g)
            for f in range(FC):
                if first:
                    last = dve.tensor_copy(zk[:, f, :], ZK_B[f][:, :])
                else:
                    last = tt(zk[:, f, :], zk[:, f, :], ZK_B[f][:, :], ALU.add)
            last.then_inc(s_zka, 1)

        def keep_ksums(b, cols):
            dve.wait_ge(s_ksb, b + 1)
            tt(ksums[:, b, :, :], inhead[:, :, :], cols[:, 0:FC].unsqueeze(2).to_broadcast([P, FC, HEADS]), ALU.mult).then_inc(s_prep, 1)

        def hk_of(b, tile):
            dve.wait_ge(s_zka, GPB * (b + 1))
            for f in range(FC):
                at = FC * B + f * B + b
                dve.wait_ge(s_saks, FC * b + f + 1)
                stt(zk[:, f, :], zk[:, f, :], modcol[:, at:at + 1], tile[:, f, :], ALU.mult, ALU.add).then_inc(s_hk, 1)

        def keep_kv(b, src):
            dve.wait_ge(s_kvt, b + 1)
            tt(kv[:, b, :].rearrange("p (a n) -> p a n", a=HG), src[:, :].rearrange("p (a n) -> p a n", a=HG),
               headmask[:, :].unsqueeze(1).to_broadcast([P, HG, P]), ALU.mult).then_inc(s_kvm, 1)

        def group1(g, par, b):
            more, b_after = has(g, 1), batch_after(g, b)
            if ends_batch(g):
                dve.wait_ge(s_id, 18)
                keep_ksums(0, ZK_B[1])
                hk_of(0, sa_ks)
            if more:
                stats1(g + 1)
            if ends_batch(g):
                keep_kv(0, ZK_B[2])
            if not more:
                for s in range(2):
                    dve.wait_ge(s_hi, FC + 2 * g + s + 1)
                    tt(sp_hl[1][:, :], raw[:, s, :], f32(sp_hl[0][:, :]), ALU.subtract).then_inc(s_elo, 1)
            for t in range(TPG):
                if t == TPG - 1:
                    add_zk(g)
                if more:
                    h_of(g + 1, t, b_after)
                    low_h(g + 1, t, 1 - par)

        def mod_parts(g):
            if g == 0:
                for m in range(2, 6):
                    mod_part(m)

        run_groups1(dve, group1, between=mod_parts)

        phase1_over(dve)
        dve.wait_ge(s_const, 16 * 5)
        def ksum_of(g):
            at_least(dve, s_den, g)
            if isinstance(g, int) and g == 2:
                dve.wait_ge(s_prep, 3)
            b = batch_of(g)
            dve.tensor_copy(ksum_now[:, :, :], ksums[:, b, :, :] if isinstance(b, int) else
                            ksums[:, bass.ds(b, 1), :, :].rearrange("p a f h -> p (a f) h")).then_inc(s_ksum, 1)

        rst = Steps(dve, s_recstep, 1)

        def recip(g):
            rst.begin(g)
            dve.wait_ge(s_rec0, g + 1)
            at_least(dve, s_reclo, g)
            rst.did(stt(den[:, :], den[:, :], -1.0, rec0[:, :], ALU.mult, ALU.mult))
            rst.settle()
            stt(rec[:, :], den[:, :], 2.0, rec0[:, :], ALU.add, ALU.mult).then_inc(s_rec, 1)
            rst.end()

        def rec_lo(g):
            dve.wait_ge(s_rechi, g + 1)
            tt(rec_hl[1][:, :], rec[:, :], f32(rec_hl[0][:, :]), ALU.subtract).then_inc(s_reclo, 1)

        def divide(g, par, j):
            dve.wait_ge(s_rb, HG * g + j + 1)
            at_least(dve, s_onlo, HG * g + j - 1)
            tt(onf[j % 2][:, :], RB_B[j % 2][:, :], qb[par][:, j, :], ALU.mult).then_inc(s_on, 1)

        def kvp_of(b, a):
            dve.wait_ge(s_mp, HG * b + a + 1)
            tt(kvp_f[b][a], M_B[b][a][:, :], modbc[:, b, 0, :], ALU.mult).then_inc(s_mf, 1)

        def kvp_lo(b):
            for a in range(HG):
                dve.wait_ge(s_mhi, HG * b + a + 1)
                tt(kvp[1][:, b, a, :], kvp_f[b][a], f32(kvp[0][:, b, a, :]), ALU.subtract).then_inc(s_mlo, 1)

        NORM_STEPS, ROUTE_STEPS = 3 * TPG + 2 * 3, 20
        turn = Steps(dve, s_step2, NORM_STEPS + ROUTE_STEPS)

        def per_row(ap):
            return ap.unsqueeze(2).to_broadcast([P, TPG, E])

        def per_expert(ap):
            return ap.unsqueeze(1).to_broadcast([P, TPG, E])

        def residual(g, t, par):
            dve.wait_ge(s_y, TPG * g + t + 1)
            dve.wait_ge(s_xb, TPG * g + t + 1)
            if t == 0:
                at_least(dve, s_x1st, 16 * g)
            tt(x1[:, t, :], Y_B[t % 2][:, :], xb[par][:, t, :], ALU.add).then_inc(s_x1, 1)

        def sums(g, t):
            dve.wait_ge(s_x1, TPG * g + t + 1)
            turn.did(dve.bn_stats(st2[:, t, :], x1[:, t, :]), f"sums{t}")

        def moments(t):
            turn.after(f"sums{t}", wait_apart)
            turn.did(dve.bn_aggr(mv2[:, t, :], st2[:, t, :]), f"moments{t}")

        def halves(half):
            return slice(2 * half, 2 * half + 2)

        def var2(half):
            h = halves(half)
            turn.after(f"moments{2 * half + 1}")
            ts(ve2[:, h], mv2[:, h, 1], LN_EPS, None, ALU.add).then_inc(s_var2, 1)

        def seed_squared(g, half):
            h = halves(half)
            dve.wait_ge(s_seed2, 2 * g + half + 1)
            turn.did(tt(na2[:, h], y2[:, h], y2[:, h], ALU.mult), f"yy{half}")

        def seed_error(half):
            h = halves(half)
            turn.after(f"yy{half}")
            turn.did(stt(na2[:, h], na2[:, h], -0.5, ve2[:, h], ALU.mult, ALU.mult), f"vyy{half}")

        def rstd2_of(half):
            h = halves(half)
            turn.after(f"vyy{half}")
            turn.did(stt(rstd2[:, h], na2[:, h], 1.5, y2[:, h], ALU.add, ALU.mult), f"rstd{half}")

        def mod_row_of(g, k):
            b = batch_of(g)
            return modbc[:, b, k, :] if isinstance(b, int) else modbc[:, bass.ds(b, 1), k, :].rearrange("p a n -> p (a n)")

        def centred(g, t):
            at_least(dve, s_h2, TPG * g + t - 1)
            if t % 2 == 0:
                turn.after(f"moments{t + 1}")
            turn.did(stt(lnt[t % 2][:, :], x1[:, t, :], mv2[:, t, 0:1], mod_row_of(g, 2), ALU.subtract, ALU.mult), f"centred{t}")

        def normed(g, t, par):
            at_least(dve, s_scat[t], SCAT * (g - 1))
            turn.after(f"centred{t}")
            if t % 2 == 0:
                turn.after(f"rstd{t // 2}")
            stt(rows[par][:, t, 0:C], lnt[t % 2][:, :], rstd2[:, t:t + 1], mod_row_of(g, 1), ALU.mult, ALU.add).then_inc(s_h2, 1)

        def rms_var(g):
            dve.wait_ge(s_sq, TPG * (g + 1))
            ts(ve3[:, :], ss[:, :], 1.0 / C, RMS_EPS, ALU.mult, ALU.add).then_inc(s_var3, 1)

        def rms_seed_squared(g):
            dve.wait_ge(s_seed3, g + 1)
            turn.did(tt(na3[:, :], y3[:, :], y3[:, :], ALU.mult), "yy_rms")

        def rms_seed_error():
            turn.after("yy_rms")
            turn.did(stt(na3[:, :], na3[:, :], -0.5, ve3[:, :], ALU.mult, ALU.mult), "vyy_rms")

        def rms():
            turn.after("vyy_rms")
            turn.did(stt(rs3[:, :], na3[:, :], 1.5, y3[:, :], ALU.add, ALU.mult), "rms")

        def logits(g):
            dve.wait_ge(s_lg, g + 1)
            turn.after("rms")
            turn.did(stt(lg[:, :, :], R_B[:, 0:TPG * E].rearrange("p (t e) -> p t e", e=E), float(np.float32(C) ** np.float32(-0.5)),
                       per_row(rs3[:, :]), ALU.mult, ALU.mult), "logits")

        def largest():
            turn.after("logits", wait_apart)
            for t in range(TPG):
                last = dve.max(mx[:, t, :], lg[:, t, :])
            turn.did(last, "largest")

        def less_max():
            turn.after("largest")
            tt(dl[:, :, :], lg[:, :, :], mx[:, :, 0:1].to_broadcast([P, TPG, E]), ALU.subtract).then_inc(s_dl, 1)

        def where_largest():
            for t in range(TPG):
                last = dve.max_index(ix[:, t, :], mx[:, t, :], lg[:, t, :])
            turn.did(last, "where")

        def chosen_two():
            turn.after("where")
            turn.did(dve.tensor_copy(ixf[:, :, :], ix[:, :, 0:2].rearrange("p t k -> p k t")), "two")

        def one_hot():
            turn.after("two")
            turn.did(tt(oh[:, :, :, :], iota_e[:, :].unsqueeze(1).unsqueeze(1).to_broadcast([P, 2, TPG, E]),
                      ixf[:, :, :].unsqueeze(3).to_broadcast([P, 2, TPG, E]), ALU.is_equal), "one_hot")

        def mask():
            turn.after("one_hot")
            tt(mkb[:, :, :], oh[:, 0, :, :], oh[:, 1, :, :], ALU.add).then_inc(s_mk, 1)

        def exp_sum(g):
            dve.wait_ge(s_ex, g + 1)
            turn.did(dve.tensor_reduce(se[:, :], ex[:, :, :], AX.X, ALU.add), "exp_sum")

        def exp_chosen(g):
            dve.wait_ge(s_mk, g + 1)
            turn.did(tt(em[:, :, :], ex[:, :, :], mkb[:, :, :], ALU.mult), "exp_chosen")

        def exp_sum_recip():
            turn.after("exp_sum")
            turn.did(dve.reciprocal(rse[:, :], se[:, :]), "exp_sum_recip")

        def probs():
            turn.after("exp_sum_recip")
            turn.did(tt(ip[:, :, :], em[:, :, :], per_row(rse[:, :]), ALU.mult), "probs")

        def renorm():
            turn.after("probs")
            turn.did(dve.tensor_reduce(rn[:, :], ip[:, :, :], AX.X, ALU.add), "renorm")

        def scaled():
            turn.did(tt(wts[:, :, :], ip[:, :, :], per_expert(pes_bc[:, :]), ALU.mult), "scaled")

        def renorm_guard():
            turn.after("renorm")
            turn.did(stt(rng[:, :], rn[:, :], 0.0, rn[:, :], ALU.is_le, ALU.add), "guarded")

        def renorm_recip():
            turn.after("guarded")
            turn.did(dve.reciprocal(rrn[:, :], rng[:, :]), "renorm_recip")

        def weights(par):
            turn.after("renorm_recip")
            turn.did(tt(rows[par][:, :, W_AT:W_AT + E], wts[:, :, :], per_row(rrn[:, :]), ALU.mult), "weights")

        def places(g):
            dve.wait_ge(s_rank, g + 1)
            turn.did(tt(pos[:, :, :], R_B[:, TPG * E:2 * TPG * E].rearrange("p (t e) -> p t e", e=E), per_expert(next_row[:, :]), ALU.add), "places")

        def next_places():
            turn.after("places")
            tt(next_row[:, :], next_row[:, :], R_B[:, 2 * TPG * E:2 * TPG * E + E], ALU.add).then_inc(s_ranku, 1)

        def places_chosen():
            turn.after("places")
            turn.did(tt(chosen[:, :, :, :], pos[:, :, :].unsqueeze(1).to_broadcast([P, 2, TPG, E]), oh[:, :, :, :], ALU.mult), "chosen")

        def two_places():
            turn.after("chosen")
            turn.did(dve.tensor_reduce(destf[:, :, :], chosen[:, :, :, :], AX.X, ALU.add), "two_places")

        def destinations(par):
            turn.after("two_places")
            dve.tensor_copy(dest[par][:, :, :], destf[:, :, :]).then_inc(s_dest, 1)

        def group2(g, par):
            router = not isinstance(g, int) or g > 0
            last = not has(g, 1)
            turn.begin(g, ROUTE_STEPS if router else 0)
            if router:
                rms_var(g - 1)
            if not last:
                rec_lo(g + 1)
            if has(g, 2):
                ksum_of(g + 2)
            residual(g, 0, par)
            if router:
                rms_seed_squared(g - 1)
            sums(g, 0)
            if router:
                rms_seed_error()
            residual(g, 1, par)
            moments(0)
            sums(g, 1)
            if isinstance(g, int) and g == 1:
                kvp_lo(1)
            if router:
                rms()
            if not last:
                divide(g + 1, 1 - par, 0)
            moments(1)
            if not last:
                divide(g + 1, 1 - par, 1)
            var2(0)
            centred(g, 0)
            seed_squared(g, 0)
            centred(g, 1)
            seed_error(0)
            residual(g, 2, par)
            if not router:
                keep_kv(1, H2_B[1])
            rstd2_of(0)
            sums(g, 2)
            normed(g, 0, par)
            moments(2)
            normed(g, 1, par)
            if router:
                logits(g - 1)
            if not last:
                divide(g + 1, 1 - par, 2)
            if router:
                largest()
            if not last:
                divide(g + 1, 1 - par, 3)
            if router:
                less_max()
                where_largest()
                chosen_two()
                one_hot()
                mask()
            residual(g, 3, par)
            if not router:
                kvp_of(1, 0)
            if router and not last:
                exp_sum(g - 1)
            sums(g, 3)
            if router and not last:
                exp_chosen(g - 1)
                exp_sum_recip()
            moments(3)
            if router and not last:
                probs()
            var2(1)
            centred(g, 2)
            if router:
                places(g - 1)
            seed_squared(g, 1)
            if router and not last:
                renorm()
            centred(g, 3)
            seed_error(1)
            if router:
                places_chosen()
            if router and not last:
                renorm_guard()
                scaled()
            rstd2_of(1)
            if router:
                two_places()
            if router and not last:
                renorm_recip()
            if router:
                next_places()
            if router and not last:
                weights(1 - par)
                destinations(1 - par)
            normed(g, 2, par)
            normed(g, 3, par)
            if not router:
                for a in range(1, HG):
                    kvp_of(1, a)
            if router and last:
                exp_sum(g - 1)
                exp_chosen(g - 1)
                finish_weights()
                weights(1 - par)
                destinations(1 - par)
            if has(g, 2):
                recip(g + 2)
            turn.end(0 if router else ROUTE_STEPS)

        def finish_weights():
            exp_sum_recip()
            probs()
            renorm()
            scaled()
            renorm_guard()
            renorm_recip()

        dve.wait_ge(s_free, 2)
        ksum_of(0)
        tt(rw[:, :, :], rw[:, :, :], rscale[:, :].unsqueeze(2).to_broadcast([P, FC, E]), ALU.mult).then_inc(s_prep, 1)
        for a in range(HG):
            kvp_of(0, a)
        kvp_lo(0)
        ksum_of(1)
        recip(0)
        rec_lo(0)
        def low_on(j):
            dve.wait_ge(s_onhi, j + 1)
            tt(on[0][1][:, j, :], onf[j % 2][:, :], f32(on[0][0][:, j, :]), ALU.subtract).then_inc(s_onlo, 1)

        divide(0, 0, 0)
        divide(0, 0, 1)
        low_on(0)
        divide(0, 0, 2)
        low_on(1)
        divide(0, 0, 3)
        low_on(2)
        low_on(3)
        recip(1)
        keep_ksums(1, H2_B[1])
        hk_of(1, h2t)
        run_groups2(dve, group2)
        turn.begin(NG, ROUTE_STEPS)
        rms_var(NG - 1)
        rms_seed_squared(NG - 1)
        rms_seed_error()
        rms()
        logits(NG - 1)
        largest()
        less_max()
        where_largest()
        chosen_two()
        one_hot()
        mask()
        exp_sum(NG - 1)
        exp_chosen(NG - 1)
        finish_weights()
        weights(1)
        places(NG - 1)
        next_places()
        places_chosen()
        two_places()
        destinations(1)
        turn.end(NORM_STEPS)

        its = Steps(dve, s_it, ITEM_STEPS)
        its.begin(0)

        def step(ins):
            its.did(ins)
            its.settle()

        dve.wait_ge(s_ranku, NG)
        dve.wait_ge(s_padi, 2)
        ts(pad_to[:, :], next_row[:, :], lane[:, 0:1], None, ALU.add).then_inc(s_padi, 1)
        step(tt(cnt[:, :], next_row[:, :], list_at[:, :], ALU.subtract))
        step(ts(cnti[:, :], cnt[:, :], 1.0, float(P - 1), ALU.max, ALU.add))
        step(ts(ntli[:, :], cnti[:, :], P.bit_length() - 1, None, ALU.arith_shift_right))
        step(dve.tensor_copy(ntl[:, :], ntli[:, :]))
        step(dve.tensor_copy(cend[:, :], ntl[:, :]))
        for e in range(1, E):
            step(tt(cend[:, e:e + 1], cend[:, e - 1:e], ntl[:, e:e + 1], ALU.add))
        lies = [h2t[:, 0:2, :].rearrange("p a n -> p (a n)")[:, 0:ITEMS * (E - 1)].rearrange("p (i e) -> p i e", e=E - 1),
                h2t[:, 2:4, :].rearrange("p a n -> p (a n)")[:, 0:ITEMS * (E - 1)].rearrange("p (i e) -> p i e", e=E - 1)]

        def all_experts(ap):
            return ap[:, 0:E - 1].unsqueeze(1).to_broadcast([P, ITEMS, E - 1])

        step(tt(lies[0], item_no[:, :].unsqueeze(2).to_broadcast([P, ITEMS, E - 1]), all_experts(cend[:, :]), ALU.is_ge))
        its.did(dve.tensor_reduce(it_e[:, :], lies[0], AX.X, ALU.add))
        step(tt(lies[1], lies[0], all_experts(ntl[:, :]), ALU.mult))
        step(dve.tensor_reduce(it_t[:, :], lies[1], AX.X, ALU.add))
        step(tt(it_k[:, :], item_no[:, :], it_t[:, :], ALU.subtract))
        step(ts(it_r[:, :], it_e[:, :], float(CAP), -float(E * CAP), ALU.mult, ALU.add))
        step(stt(it_r[:, :], it_k[:, :], float(P), it_r[:, :], ALU.mult, ALU.add))
        step(stt(it_r[:, :], item_no[:, :], cend[:, E - 1:E], it_r[:, :], ALU.is_lt, ALU.mult))
        step(ts(tables[:, 0, :], it_r[:, :], float(E * CAP), None, ALU.add))
        its.did(dve.tensor_copy(tables[:, 1, :], it_e[:, :]))
        its.did(dve.tensor_copy(tables[:, 2, :], it_k[:, :]))
        its.end()

        phase2_over(dve)

        def x_lo(i):
            dve.wait_ge(s_xthi, i + 1)
            at_least(dve, s_u, i)
            tt(x_t[1][:, :], XT_B[:, :], f32(x_t[0][:, :]), ALU.subtract).then_inc(s_xtlo, 1)

        def keep_meta(i, at):
            dve.wait_ge(s_xr[at], 16 * ((i // RING if isinstance(i, int) else i >> 2) + 1))
            dve.tensor_copy(meta[at][:, :], xrow[at][:, W_AT:W_AT + META]).then_inc(s_meta, 1)

        def glu(i):
            dve.wait_ge(s_u, i + 1)
            dve.wait_ge(s_ga, i + 1)
            at_least(dve, s_ht, i)
            tt(hact[:, :], U_B[:, :], gact[:, :], ALU.mult).then_inc(s_h, 1)

        def act_lo(i):
            dve.wait_ge(s_hthi, i + 1)
            tt(act_t[1][:, :], HT_B[:, :], f32(act_t[0][:, :]), ALU.subtract).then_inc(s_htlo, 1)

        gbs = Steps(dve, s_gbr, 3)

        def out_rows(i, at):
            gbs.begin(i)
            e = dve.value_load(tables[0:1, 1, bass.ds(i, 1)], min_val=0, max_val=E - 1)
            at_least(dve, s_or, i)
            at_least(dve, s_add, 16 * (i - 1))
            dve.wait_ge(s_meta, i + 1)
            gbs.did(dve.tensor_copy(cur_w[:, :], meta[at][:, bass.ds(e, 1)]))
            gbs.did(dve.tensor_copy(cur_tok[at % 2][:, :], meta[at][:, E:E + 1].bitcast(U32)))
            gbs.settle()
            ts(in_b0[:, :], cur_tok[at % 2][:, :], float(S), None, ALU.is_lt).then_inc(s_cur, 1)
            ts(in_b1[:, :], cur_tok[at % 2][:, :], float(S), None, ALU.is_ge).then_inc(s_cur, 1)
            dve.wait_ge(s_cur, 2 * (i + 1))
            dve.wait_ge(s_gb0, i + 1)
            gbs.did(stt(gbr[:, :], modbc[:, 1, 3, :], in_b1[:, 0:1], gb0[:, :], ALU.mult, ALU.add))
            dve.wait_ge(s_o, i + 1)
            gbs.settle()
            stt(orow[at % 2][:, :], O_B[:, :], cur_w[:, 0:1], gbr[:, :], ALU.mult, ALU.mult).then_inc(s_or, 1)
            gbs.end()

        keep_meta(0, 0)
        x_lo(0)
        glu(0)
        keep_meta(1, 1)
        x_lo(1)

        def item(i, at):
            act_lo(i - 1)
            glu(i)
            if not isinstance(i, int) or i < ITEMS - 1:
                keep_meta(i + 1, (at + 1) % RING)
                x_lo(i + 1)
            out_rows(i - 1, (at - 1) % RING)

        run_items(dve, item)
        act_lo(ITEMS - 1)
        out_rows(ITEMS - 1, (ITEMS - 1) % RING)

    @block.tensor
    def _(pe):
        mm = pe.matmul

        pe.wait_ge(s_silu, 1)
        def mod_part(m):
            pe.wait_ge(s_mod[m], 16)
            if m >= 4:
                pe.wait_ge(s_modrow, m - 1)
            for f in range(FC):
                last = mm(MOD_B[m][0:B, :], silu_c[:, f * B:(f + 1) * B], mod_stage[m][:, f, :], start=(f == 0), stop=(f == FC - 1))
            last.then_inc(s_modpe, 1)

        def turn(g, t):
            pe.wait_ge(s_z, TPG * g + t + 1)
            at_least(pe, s_hf, TPG * g + t - 1)
            for f in range(FC):
                last = pe.transpose(T_B[t % 2][:, f * P:(f + 1) * P], xg[:, t, f * P:(f + 1) * P], ident[:, :])
            last.then_inc(s_T, 1)

        mod_part(0)
        mod_part(1)
        pe.wait_ge(s_id, 6)
        turn(0, 0)
        turn(0, 1)
        pe.wait_ge(s_modrow, 2)
        for r in range(2 * FC):
            last = pe.transpose(ZK_B[0][:, r * B:(r + 1) * B], mod_row[:, r // FC, r % FC * P:(r % FC + 1) * P], ident[0:B, 0:B])
        last.then_inc(s_colpe, 1)
        turn(0, 2)
        turn(0, 3)

        def product(dst, parts, n, stationary, moving):
            k = 0
            for f in range(n):
                for a, b in PASSES[:parts]:
                    last = mm(dst, stationary(a, f), moving(b, f), start=(k == 0), stop=(k == parts * n - 1))
                    k += 1
            return last

        def k_product(g, t, par):
            pe.wait_ge(s_hlo, TPG * g + t + 1)
            if t < 2:
                at_least(pe, s_qe, FC * g - 1 + t)
            else:
                at_least(pe, s_ke, TPG * g + t - 1)
            product(QK_B[t % 2][:, :], 3, FC, lambda a, f: h_t[par][a][:, f, t * P:(t + 1) * P],
                    lambda b, f: wq[b][:, f * C:(f + 1) * C]).then_inc(s_k, 1)

        def q_product(g, j, par):
            dst = QK_B if has(g, 1) else T_B
            pe.wait_ge(s_hlo, TPG * (g + 1))
            if j >= 2:
                at_least(pe, s_qe, FC * g + j - 1)
            elif has(g, 1):
                at_least(pe, s_ke, TPG * g + 3 + j)
            product(dst[j % 2][:, :], 3, FC, lambda a, f: wq[a][:, (FC + f) * C + j * P:(FC + f) * C + (j + 1) * P],
                    lambda b, f: h_t[par][b][:, f, :]).then_inc(s_q, 1)

        def zk_product(g, t):
            pe.wait_ge(s_zlo, TPG * g + t + 1)
            if t == 0:
                at_least(pe, s_zka, g)
                if isinstance(g, int) and g == 1:
                    pe.wait_ge(s_modrow, 6)
            pe.wait_ge(s_klo, TPG * g + t + 1)
            for f in range(FC):
                for a, b in PASSES:
                    last = mm(ZK_B[f][:, :], z_hl[a][:, t, f * P:(f + 1) * P], k_hl[t % 2][b][:, :],
                              start=(t == 0 and (a, b) == PASSES[0]), stop=(t == TPG - 1 and (a, b) == PASSES[-1]), skip_group_check=True)
            last.then_inc(s_zk, 1)

        def key_sums(b, bc, cols):
            pe.wait_ge(s_ksum1, TPG * GPB * (b + 1))
            mm(bc[:, :], ones_f[:, :], k_sum[:, :], start=True, stop=True)
            for a in range(FC):
                last = mm(cols[:, a:a + 1], k_sum[:, a * P:(a + 1) * P], ones_f[:, 0:1], start=True, stop=True)
            last.then_inc(s_ksb, 1)

        def values_keys(b, dst):
            pe.wait_ge(s_hk, FC * (b + 1))
            pe.wait_ge(s_vp, 32)
            for a in range(HG):
                cols = slice(a * P, (a + 1) * P)
                for f in range(FC):
                    last = mm(dst[:, cols], wv_f[:, f, cols], zk[:, f, cols], start=(f == 0), stop=(f == FC - 1))
            last.then_inc(s_kvt, 1)

        def group1(g, par, b):
            if not has(g, 1):
                for t in range(2):
                    k_product(g, t, par)
                    q_product(g, t, par)
                for t in range(2):
                    zk_product(g, t)
                    k_product(g, t + 2, par)
                    q_product(g, t + 2, par)
                zk_product(g, 2)
                zk_product(g, 3)
                return
            if ends_batch(g):
                pe.wait_ge(s_id, 18)
                pe.wait_ge(s_zka, GPB)
                key_sums(0, ZK_B[0], ZK_B[1])
            k_product(g, 0, par)
            k_product(g, 1, par)
            if ends_batch(g):
                values_keys(0, ZK_B[2])
                pe.wait_ge(s_kvm, 1)
            zk_product(g, 0)
            k_product(g, 2, par)
            zk_product(g, 1)
            k_product(g, 3, par)
            turn(g + 1, 0)
            zk_product(g, 2)
            turn(g + 1, 1)
            if isinstance(g, int) and g == 0:
                pe.wait_ge(s_lo, 4)
            q_product(g, 0, par)
            turn(g + 1, 2)
            zk_product(g, 3)
            q_product(g, 1, par)
            turn(g + 1, 3)
            q_product(g, 2, par)
            q_product(g, 3, par)

        def mod_parts(g):
            if g == 0:
                pe.wait_ge(s_zka, 1)
                for m in range(2, 6):
                    mod_part(m)

        pe.wait_ge(s_lo, 2)
        run_groups1(pe, group1, between=mod_parts)

        phase1_over(pe)

        def denominators(g, par, meanwhile=None):
            pe.wait_ge(s_q2, 16 * (g + 1))
            pe.wait_ge(s_ksum, g + 1)
            at_least(pe, s_dene, g)
            at_least(pe, s_lgt, g - 2)
            for f in range(FC):
                if meanwhile and f == FC // 2:
                    meanwhile()
                last = mm(D_B[0:HEADS, :], ksum_now[:, f, :], qb[par][:, f, :], start=(f == 0), stop=(f == FC - 1))
            last.then_inc(s_den, 1)

        def spread(g, j):
            pe.wait_ge(s_reclo, g + 1)
            if isinstance(g, int) and g == 0:
                pe.wait_ge(s_sel, 4)
            at_least(pe, s_on, HG * g + j - 1)
            for k in range(2):
                last = mm(RB_B[j % 2][:, :], sel[:, j * P:(j + 1) * P], rec_hl[k][:, :], start=(k == 0), stop=(k == 1))
            last.then_inc(s_rb, 1)

        def project_sums(b, a):
            pe.wait_ge(s_kvm, b + 1)
            if b:
                pe.wait_ge(s_mf, HG * b + a // 3)
            mm(M_B[b][a][:, :], kv[:, b, a * P:(a + 1) * P], wproj_f[:, a, :], start=True, stop=True).then_inc(s_mp, 1)

        for a in range(HG):
            project_sums(0, a)
        pe.wait_ge(s_zka, NG)
        denominators(0, 0)
        pe.wait_ge(s_mf, HG)
        key_sums(1, H2_B[0], H2_B[1])
        denominators(1, 1)
        for j in range(HG):
            spread(0, j)

        def rank(g):
            pe.wait_ge(s_mk, g + 1)
            for t in range(TPG):
                dst = R_B[:, (TPG + t) * E:(TPG + t + 1) * E]
                for s in range(t):
                    mm(dst, ones[:, :], mkb[:, s, :], start=(s == 0), stop=False)
                mm(dst, before[:, :], mkb[:, t, :], start=(t == 0), stop=True)
            for t in range(TPG):
                last = mm(R_B[:, 2 * TPG * E:2 * TPG * E + E], ones[:, :], mkb[:, t, :], start=(t == 0), stop=(t == TPG - 1))
            last.then_inc(s_rank, 1)

        def project(g, par, t):
            b = batch_of(g)
            if t == 0:
                pe.wait_ge(s_onlo, HG * (g + 1))
            at_least(pe, s_x1, TPG * g + t - 1)
            product(Y_B[t % 2][:, :], 3, FC, lambda a, f: on[par][a][:, f, t * P:(t + 1) * P],
                    lambda k, f: kvp[k][:, b, f, :] if isinstance(b, int) else
                    kvp[k][:, bass.ds(b, 1), f, :].rearrange("p a n -> p (a n)")).then_inc(s_y, 1)

        def turn_h2(g, par, t):
            pe.wait_ge(s_h2, TPG * g + t + 1)
            at_least(pe, s_h2te, TPG * g + t - 1)
            for f in range(FC):
                last = pe.transpose(H2_B[t % 2][:, f * P:(f + 1) * P], rows[par][:, t, f * P:(f + 1) * P], ident[:, :])
            last.then_inc(s_h2t, 1)

        def logits_of(g, a, b):
            pe.wait_ge(s_h2te, TPG * g + b)
            if a == 0:
                pe.wait_ge(s_dene, min(g + 3, NG) if isinstance(g, int) else g + 3)
            for f in range(FC):
                last = mm(D_B[0:E, a * P:b * P], rw[:, f, :], h2t[:, a:b, f * P:(f + 1) * P], start=(f == 0), stop=(f == FC - 1))
            return last

        def logits(g):
            logits_of(g, 0, TPG).then_inc(s_lgp, 1)

        def turn_logits(g):
            pe.wait_ge(s_lgt, g + 1)
            wait_apart(pe, s_ranku, g)
            for t in range(TPG):
                last = pe.transpose(R_B[:, t * E:(t + 1) * E], lg_t[:, t * P:(t + 1) * P], ident[0:E, 0:E])
            last.then_inc(s_lg, 1)

        def group2(g, par):
            before_it = not isinstance(g, int) or g > 0
            project(g, par, 0)
            if isinstance(g, int) and g == 1:
                pe.wait_ge(s_mf, B * HG)
            if before_it:
                turn_h2(g - 1, 1 - par, 0)
                turn_h2(g - 1, 1 - par, 1)
            project(g, par, 1)
            if not before_it:
                values_keys(1, H2_B[1])
            if has(g, 1):
                spread(g + 1, 0)
                spread(g + 1, 1)
            if before_it:
                turn_h2(g - 1, 1 - par, 2)
                turn_h2(g - 1, 1 - par, 3)
            project(g, par, 2)
            if before_it:
                logits(g - 1)
            if has(g, 1):
                spread(g + 1, 2)
                spread(g + 1, 3)
            if not before_it:
                for a in range(3):
                    project_sums(1, a)
            if before_it:
                turn_logits(g - 1)
            project(g, par, 3)
            if has(g, 2):
                denominators(g + 2, par, meanwhile=(lambda: rank(g - 1)) if before_it else None)
            elif before_it:
                rank(g - 1)
            if not before_it:
                project_sums(1, 3)

        run_groups2(pe, group2)
        half = TPG // 2
        for t in range(half):
            turn_h2(NG - 1, 1, t)
        logits_of(NG - 1, 0, half)
        for t in range(half, TPG):
            turn_h2(NG - 1, 1, t)
        logits_of(NG - 1, half, TPG).then_inc(s_lgp, 1)
        turn_logits(NG - 1)
        rank(NG - 1)

        phase2_over(pe)

        def expert_of(i):
            return pe.value_load(tables[0:1, 1, bass.ds(i, 1)], min_val=0, max_val=E - 1)

        def weights(e, at):
            base = pe.snap((e & 1) * (2 * EW), min_val=0, max_val=2 * EW)
            return lambda k, f: wbuf[:, bass.ds(base + (at(f) // QW * 2 * QW + k * QW + at(f) % QW), 512)]

        def turn_rows(i, at):
            pe.wait_ge(s_xr[at], 16 * ((i // RING if isinstance(i, int) else i >> 2) + 1))
            at_least(pe, s_xtlo, i)
            for f in range(FC):
                last = pe.transpose(XT_B[:, f * P:(f + 1) * P], xrow[at][:, f * P:(f + 1) * P], ident[:, :])
            last.then_inc(s_xt, 1)

        def gate(i, e):
            pe.wait_ge(s_xtlo, i + 1)
            pe.wait_ge(s_w, 16 * QPE * (e + 1))
            at_least(pe, s_ga, i)
            product(G_B[:, :], 3, FC, lambda a, f: x_t[a][:, f * P:(f + 1) * P], weights(e, lambda f: f * 2 * H)).then_inc(s_g, 1)

        def up(i, e):
            at_least(pe, s_h, i)
            product(U_B[:, :], 3, FC, lambda a, f: x_t[a][:, f * P:(f + 1) * P], weights(e, lambda f: f * 2 * H + H)).then_inc(s_u, 1)

        def turn_act(i):
            pe.wait_ge(s_h, i + 1)
            at_least(pe, s_htlo, i)
            for f in range(H // P):
                last = pe.transpose(HT_B[:, f * P:(f + 1) * P], hact[:, f * P:(f + 1) * P], ident[:, :])
            last.then_inc(s_ht, 1)

        def down(i, e):
            pe.wait_ge(s_htlo, i + 1)
            at_least(pe, s_or, i)
            product(O_B[:, :], 3, H // P, lambda a, f: act_t[a][:, f * P:(f + 1) * P], weights(e, lambda f: DOWN + f * C)).then_inc(s_o, 1)

        turn_rows(0, 0)
        e = expert_of(0)
        gate(0, e)
        up(0, e)
        turn_rows(1, 1)

        def item(i, at):
            e, e_before = expert_of(i), expert_of(i - 1)
            gate(i, e)
            turn_act(i - 1)
            up(i, e)
            if not isinstance(i, int) or i < ITEMS - 1:
                turn_rows(i + 1, (at + 1) % RING)
            down(i - 1, e_before)

        run_items(pe, item)
        turn_act(ITEMS - 1)
        down(ITEMS - 1, expert_of(ITEMS - 1))

    ph3.close()
    keep.close()




def laid_out(i):
    def chunks(a):
        return np.ascontiguousarray(a.reshape(-1, P, a.shape[1]).transpose(1, 0, 2).reshape(P, -1))

    gate = i["L0_ffn_gating_einsum"].transpose(0, 3, 1, 2).reshape(E, C, 2 * H)
    experts = np.stack([np.concatenate([chunks(gate[e]), chunks(i["L0_ffn_linear"][e])], axis=1) for e in range(E)])
    experts = np.ascontiguousarray(experts.reshape(E, P, QPE, QW).transpose(0, 2, 1, 3).reshape(E * QPE * P, QW))
    return {
        "x": np.ascontiguousarray(i["L0_attn_x"].reshape(NT, C)),
        "c_t": chunks(i["L0_c"].T),
        "wmod": np.ascontiguousarray(i["L0_wmod"]),
        "wqkv": np.concatenate([chunks(i["L0_attn_w_qkv"][k * C:(k + 1) * C].T) for k in (1, 0, 2)], axis=1),
        "wproj": chunks(i["L0_attn_w_proj"].T),
        "b_proj": np.ascontiguousarray(i["L0_attn_b_proj"]),
        "r_w": chunks(i["L0_ffn_router_logits"]),
        "r_scale": chunks(i["L0_ffn_router_scale"].reshape(C, 1)),
        "pes": np.ascontiguousarray(i["L0_ffn_per_expert_scale"]),
        "moe_w": experts,
    }


def kernel(**inputs):
    from concourse import bacc
    from concourse.bass_utils import run_bass_kernel_spmd

    nc = bacc.Bacc("TRN2", target_bir_lowering=False, num_devices=1)
    arrays = laid_out({k: np.asarray(v) for k, v in inputs.items()})
    aps = {n: nc.dram_tensor(f"in_{n}", a.shape, F32, kind="ExternalInput").ap() for n, a in arrays.items()}
    out = nc.dram_tensor("out_rows", (NT + P, C), F32, kind="ExternalOutput").ap()
    build(nc, out=out, **aps)
    got = run_bass_kernel_spmd(nc, [{f"in_{n}": a for n, a in arrays.items()}], core_ids=[0])
    return got.results[0]["out_rows"][:NT].reshape(B, S, C)
```
